# Optimizing a Trainium2 kernel written in Bass

```python
import numpy as np
import jax
import jax.numpy as jnp

def _softmax(x, axis=-1):
    return jax.nn.softmax(x, axis=axis)

def _gelu(x):
    return jax.nn.gelu(x, approximate=True)

def _silu(x):
    return jax.nn.silu(x)

def _sigmoid(x):
    return jax.nn.sigmoid(x)

def _layernorm(x, axis=-1, eps=1e-05):
    m = jnp.mean(x, axis=axis, keepdims=True)
    v = jnp.var(x, axis=axis, keepdims=True)
    return (x - m) / jnp.sqrt(v + eps)

def _scatter_add(tgt, idx, src, axis=0):
    return tgt.at[idx].add(src)

def _segment_sum(src, seg, n):
    return jax.ops.segment_sum(src, seg, n)
kernel_name = 'mk_conv_attn_hybrid_d2_conv_nchw256_r4_a270c8'

def setup_inputs(seed: int=0):
    np.random.seed(seed)
    _w = jnp.asarray

    def _rec_inputs():
        import jax
        import jax.numpy as jnp
        _gk = jax.random.key(seed)
        x = -0.0002928 + 1 * jax.random.normal(jax.random.fold_in(_gk, 1), (4, 64, 16, 16), jnp.float32)
        return x
    x = _rec_inputs()

    def _L0_conv_setup():
        import jax, jax.numpy as jnp
        import numpy as np
        from jax import lax
        EPS = 1e-06
        CLAMP = 10000.0

        def _ln_last(x, w, b):
            mu = jnp.mean(x, axis=-1, keepdims=True)
            var = jnp.mean(jnp.square(x - mu), axis=-1, keepdims=True)
            return (x - mu) * lax.rsqrt(var + EPS) * w + b

        def _nan_clean(x):
            return jnp.nan_to_num(x, nan=0.0, posinf=CLAMP, neginf=-CLAMP)
        key = jax.random.key(seed)
        B, C, H, W = (4, 64, 16, 16)
        hid = 2 * C
        k = 3
        ks = jax.random.split(key, 12)
        s = 0.02
        return {'x': jax.random.normal(ks[0], (B, C, H, W), jnp.float32), 'ln2d_w': jnp.ones((C,), jnp.float32), 'ln2d_b': jnp.zeros((C,), jnp.float32), 'inproj_w': jax.random.normal(ks[1], (C, C), jnp.float32) * s, 'inproj_b': jnp.zeros((C,), jnp.float32), 'dw2d_w': jax.random.normal(ks[2], (C, 3, 3), jnp.float32) * s, 'dw2d_b': jnp.zeros((C,), jnp.float32), 'ssm_ln_w': jnp.ones((C,), jnp.float32), 'ssm_ln_b': jnp.zeros((C,), jnp.float32), 'ssm_in_w': jax.random.normal(ks[3], (2 * hid, C), jnp.float32) * s, 'ssm_in_b': jnp.zeros((2 * hid,), jnp.float32), 'ssm_dw_w': jax.random.normal(ks[4], (hid, k), jnp.float32) * s, 'ssm_dw_b': jnp.zeros((hid,), jnp.float32), 'ssm_out_w': jax.random.normal(ks[5], (C, hid), jnp.float32) * s, 'ssm_out_b': jnp.zeros((C,), jnp.float32), 'outproj_w': jax.random.normal(ks[6], (C, C), jnp.float32) * s, 'outproj_b': jnp.zeros((C,), jnp.float32)}
    _L0_conv_all = _L0_conv_setup()
    _L0_conv_in = {k: v for k, v in _L0_conv_all.items() if k in ('ln2d_w', 'ln2d_b', 'inproj_w', 'inproj_b', 'dw2d_w', 'dw2d_b', 'ssm_ln_w', 'ssm_ln_b', 'ssm_in_w', 'ssm_in_b', 'ssm_dw_w', 'ssm_dw_b', 'ssm_out_w', 'ssm_out_b', 'outproj_w', 'outproj_b')}
    del _L0_conv_all

    def _L1_attn_setup():
        import jax, jax.numpy as jnp
        import numpy as np
        MIDC = 64
        HEADS = 16
        HEADC = MIDC // HEADS
        EPS = 1e-05

        def _layernorm(x, w, b):
            mean = jnp.mean(x, axis=-1, keepdims=True)
            std = jnp.std(x, axis=-1, keepdims=True, ddof=1)
            return w * (x - mean) / (std + EPS) + b
        key = jax.random.key(seed)
        ks = jax.random.split(key, 3)
        B, HW = (8, 4096)
        x = jax.random.normal(ks[0], (B, HW, MIDC), dtype=jnp.float32)
        W_qkv = jax.random.normal(ks[1], (3 * MIDC, MIDC), dtype=jnp.float32) * 0.02
        b_qkv = jnp.zeros((3 * MIDC,), dtype=jnp.float32)
        kln_w = jnp.ones((HEADS, 1, HEADC), dtype=jnp.float32)
        kln_b = jnp.zeros((HEADS, 1, HEADC), dtype=jnp.float32)
        vln_w = jnp.ones((HEADS, 1, HEADC), dtype=jnp.float32)
        vln_b = jnp.zeros((HEADS, 1, HEADC), dtype=jnp.float32)
        W_proj = jax.random.normal(ks[2], (MIDC, MIDC), dtype=jnp.float32) * 0.02
        b_proj = jnp.zeros((MIDC,), dtype=jnp.float32)
        return {'x': x, 'W_qkv': W_qkv, 'b_qkv': b_qkv, 'kln_w': kln_w, 'kln_b': kln_b, 'vln_w': vln_w, 'vln_b': vln_b, 'W_proj': W_proj, 'b_proj': b_proj}
    _L1_attn_all = _L1_attn_setup()
    _L1_attn_in = {k: v for k, v in _L1_attn_all.items() if k in ('W_qkv', 'b_qkv', 'kln_w', 'kln_b', 'vln_w', 'vln_b', 'W_proj', 'b_proj')}
    del _L1_attn_all

    def _L1_ffn_setup():
        import jax, jax.numpy as jnp
        import numpy as np
        TOP_K = 2
        key = jax.random.key(seed)
        ks = jax.random.split(key, 4)
        B, L, D, H, E = (8, 1024, 64, 256, 8)
        s = 0.02
        return {'x': jax.random.normal(ks[0], (B, L, D), jnp.float32), 'Wg': jax.random.normal(ks[1], (D, E), jnp.float32) * s, 'bg': jnp.zeros((E,), jnp.float32), 'W1': jax.random.normal(ks[2], (E, D, H), jnp.float32) * s, 'b1': jnp.zeros((E, H), jnp.float32), 'W2': jax.random.normal(ks[3], (E, H, D), jnp.float32) * s, 'b2': jnp.zeros((E, D), jnp.float32)}
    _L1_ffn_all = _L1_ffn_setup()
    _L1_ffn_in = {k: v for k, v in _L1_ffn_all.items() if k in ('Wg', 'bg', 'W1', 'b1', 'W2', 'b2')}
    del _L1_ffn_all
    return {'x': x, 'L0_conv_ln2d_w': _L0_conv_in['ln2d_w'], 'L0_conv_ln2d_b': _L0_conv_in['ln2d_b'], 'L0_conv_inproj_w': _L0_conv_in['inproj_w'], 'L0_conv_inproj_b': _L0_conv_in['inproj_b'], 'L0_conv_dw2d_w': _L0_conv_in['dw2d_w'], 'L0_conv_dw2d_b': _L0_conv_in['dw2d_b'], 'L0_conv_ssm_ln_w': _L0_conv_in['ssm_ln_w'], 'L0_conv_ssm_ln_b': _L0_conv_in['ssm_ln_b'], 'L0_conv_ssm_in_w': _L0_conv_in['ssm_in_w'], 'L0_conv_ssm_in_b': _L0_conv_in['ssm_in_b'], 'L0_conv_ssm_dw_w': _L0_conv_in['ssm_dw_w'], 'L0_conv_ssm_dw_b': _L0_conv_in['ssm_dw_b'], 'L0_conv_ssm_out_w': _L0_conv_in['ssm_out_w'], 'L0_conv_ssm_out_b': _L0_conv_in['ssm_out_b'], 'L0_conv_outproj_w': _L0_conv_in['outproj_w'], 'L0_conv_outproj_b': _L0_conv_in['outproj_b'], 'L1_attn_W_qkv': _L1_attn_in['W_qkv'], 'L1_attn_b_qkv': _L1_attn_in['b_qkv'], 'L1_attn_kln_w': _L1_attn_in['kln_w'], 'L1_attn_kln_b': _L1_attn_in['kln_b'], 'L1_attn_vln_w': _L1_attn_in['vln_w'], 'L1_attn_vln_b': _L1_attn_in['vln_b'], 'L1_attn_W_proj': _L1_attn_in['W_proj'], 'L1_attn_b_proj': _L1_attn_in['b_proj'], 'L1_ffn_Wg': _L1_ffn_in['Wg'], 'L1_ffn_bg': _L1_ffn_in['bg'], 'L1_ffn_W1': _L1_ffn_in['W1'], 'L1_ffn_b1': _L1_ffn_in['b1'], 'L1_ffn_W2': _L1_ffn_in['W2'], 'L1_ffn_b2': _L1_ffn_in['b2']}

def reference(x, L0_conv_ln2d_w, L0_conv_ln2d_b, L0_conv_inproj_w, L0_conv_inproj_b, L0_conv_dw2d_w, L0_conv_dw2d_b, L0_conv_ssm_ln_w, L0_conv_ssm_ln_b, L0_conv_ssm_in_w, L0_conv_ssm_in_b, L0_conv_ssm_dw_w, L0_conv_ssm_dw_b, L0_conv_ssm_out_w, L0_conv_ssm_out_b, L0_conv_outproj_w, L0_conv_outproj_b, L1_attn_W_qkv, L1_attn_b_qkv, L1_attn_kln_w, L1_attn_kln_b, L1_attn_vln_w, L1_attn_vln_b, L1_attn_W_proj, L1_attn_b_proj, L1_ffn_Wg, L1_ffn_bg, L1_ffn_W1, L1_ffn_b1, L1_ffn_W2, L1_ffn_b2):
    import jax
    import jax.numpy as jnp

    def _L0_conv_ref(x, ln2d_w, ln2d_b, inproj_w, inproj_b, dw2d_w, dw2d_b, ssm_ln_w, ssm_ln_b, ssm_in_w, ssm_in_b, ssm_dw_w, ssm_dw_b, ssm_out_w, ssm_out_b, outproj_w, outproj_b):
        import jax, jax.numpy as jnp
        import numpy as np
        from jax import lax
        EPS = 1e-06
        CLAMP = 10000.0

        def _ln_last(x, w, b):
            mu = jnp.mean(x, axis=-1, keepdims=True)
            var = jnp.mean(jnp.square(x - mu), axis=-1, keepdims=True)
            return (x - mu) * lax.rsqrt(var + EPS) * w + b

        def _nan_clean(x):
            return jnp.nan_to_num(x, nan=0.0, posinf=CLAMP, neginf=-CLAMP)
        B, C, H, W = x.shape
        L = H * W
        y = _ln_last(x.transpose(0, 2, 3, 1), ln2d_w, ln2d_b).transpose(0, 3, 1, 2)
        y = jnp.einsum('bchw,oc->bohw', y, inproj_w) + inproj_b[None, :, None, None]
        y = lax.conv_general_dilated(y, dw2d_w[:, None, :, :], (1, 1), ((1, 1), (1, 1)), dimension_numbers=('NCHW', 'OIHW', 'NCHW'), feature_group_count=C) + dw2d_b[None, :, None, None]
        s0 = y.reshape(B, C, L).transpose(0, 2, 1)
        s1 = s0[:, ::-1]
        s2 = y.transpose(0, 1, 3, 2).reshape(B, C, L).transpose(0, 2, 1)
        s3 = s2[:, ::-1]
        s = jnp.concatenate([s0, s1, s2, s3], axis=0)
        r = _ln_last(s, ssm_ln_w, ssm_ln_b)
        r = r @ ssm_in_w.T + ssm_in_b
        a, g = jnp.split(r, 2, axis=-1)
        r = a * jax.nn.sigmoid(g)
        r = r.transpose(0, 2, 1)
        hid = r.shape[1]
        k = ssm_dw_w.shape[-1]
        pad = ((k - 1) // 2, k // 2)
        r = lax.conv_general_dilated(r, ssm_dw_w[:, None, :], (1,), (pad,), dimension_numbers=('NCH', 'OIH', 'NCH'), feature_group_count=hid) + ssm_dw_b[None, :, None]
        r = r.transpose(0, 2, 1) @ ssm_out_w.T + ssm_out_b
        ys = _nan_clean(r) + s
        y0, y1, y2, y3 = jnp.split(ys, 4, axis=0)
        m0 = y0.transpose(0, 2, 1).reshape(B, C, H, W)
        m1 = y1[:, ::-1].transpose(0, 2, 1).reshape(B, C, H, W)
        m2 = y2.transpose(0, 2, 1).reshape(B, C, W, H).transpose(0, 1, 3, 2)
        m3 = y3[:, ::-1].transpose(0, 2, 1).reshape(B, C, W, H).transpose(0, 1, 3, 2)
        m = (m0 + m1 + m2 + m3) * 0.25
        out = jnp.einsum('bchw,oc->bohw', m, outproj_w) + outproj_b[None, :, None, None]
        out = _nan_clean(out)
        return out + x

    def _L1_attn_ref(x, W_qkv, b_qkv, kln_w, kln_b, vln_w, vln_b, W_proj, b_proj):
        import jax, jax.numpy as jnp
        import numpy as np
        MIDC = 64
        HEADS = 16
        HEADC = MIDC // HEADS
        EPS = 1e-05

        def _layernorm(x, w, b):
            mean = jnp.mean(x, axis=-1, keepdims=True)
            std = jnp.std(x, axis=-1, keepdims=True, ddof=1)
            return w * (x - mean) / (std + EPS) + b
        B, HW, C = x.shape
        bias = x
        qkv = jnp.einsum('bnc,oc->bno', x, W_qkv) + b_qkv
        qkv = qkv.reshape(B, HW, HEADS, 3 * HEADC).transpose(0, 2, 1, 3)
        q, k, v = jnp.split(qkv, 3, axis=-1)
        k = _layernorm(k, kln_w, kln_b)
        v = _layernorm(v, vln_w, vln_b)
        kv = jnp.einsum('bhnd,bhne->bhde', k, v) / HW
        out = jnp.einsum('bhnd,bhde->bhne', q, kv)
        out = out.transpose(0, 2, 1, 3).reshape(B, HW, C)
        ret = out + bias
        proj = jnp.einsum('bnc,oc->bno', ret, W_proj) + b_proj
        return jax.nn.gelu(proj, approximate=False) + bias

    def _L1_ffn_ref(x, Wg, bg, W1, b1, W2, b2):
        import jax, jax.numpy as jnp
        import numpy as np
        TOP_K = 2
        B, L, D = x.shape
        E = W1.shape[0]
        xf = x.reshape(-1, D)
        gate_logits = xf @ Wg + bg
        top_w, top_i = jax.lax.top_k(gate_logits, TOP_K)
        top_w = jax.nn.softmax(top_w, axis=-1)
        w_dense = jnp.sum(jax.nn.one_hot(top_i, E, dtype=xf.dtype) * top_w[..., None], axis=1)
        out = jnp.zeros_like(xf)
        for e in range(E):
            h = jax.nn.gelu(xf @ W1[e] + b1[e], approximate=False)
            out = out + w_dense[:, e:e + 1] * (h @ W2[e] + b2[e])
        return out.reshape(B, L, D)

    def _gn(v, G=32, eps=1e-05):
        B_, C_, H_, W_ = v.shape
        g = v.reshape(B_, G, C_ // G, H_, W_)
        m = jnp.mean(g, axis=(2, 3, 4), keepdims=True)
        s = jnp.var(g, axis=(2, 3, 4), keepdims=True)
        return ((g - m) / jnp.sqrt(s + eps)).reshape(v.shape)

    def _ln_c(v, eps=1e-06):
        m = jnp.mean(v, axis=1, keepdims=True)
        s = jnp.var(v, axis=1, keepdims=True)
        return (v - m) / jnp.sqrt(s + eps)

    def _ln_t(v, eps=1e-05):
        m = jnp.mean(v, axis=-1, keepdims=True)
        s = jnp.var(v, axis=-1, keepdims=True)
        return (v - m) / jnp.sqrt(s + eps)

    def _to_tokens(v):
        B_, C_, H_, W_ = v.shape
        return v.reshape(B_, C_, H_ * W_).transpose(0, 2, 1)

    def _from_tokens(t, like):
        B_, C_, H_, W_ = like.shape
        return t.transpose(0, 2, 1).reshape(B_, C_, H_, W_)
    x = _L0_conv_ref(x, L0_conv_ln2d_w, L0_conv_ln2d_b, L0_conv_inproj_w, L0_conv_inproj_b, L0_conv_dw2d_w, L0_conv_dw2d_b, L0_conv_ssm_ln_w, L0_conv_ssm_ln_b, L0_conv_ssm_in_w, L0_conv_ssm_in_b, L0_conv_ssm_dw_w, L0_conv_ssm_dw_b, L0_conv_ssm_out_w, L0_conv_ssm_out_b, L0_conv_outproj_w, L0_conv_outproj_b)
    t = _to_tokens(x)
    t = t + _L1_attn_ref(_ln_t(t), L1_attn_W_qkv, L1_attn_b_qkv, L1_attn_kln_w, L1_attn_kln_b, L1_attn_vln_w, L1_attn_vln_b, L1_attn_W_proj, L1_attn_b_proj)
    t = t + _L1_ffn_ref(_ln_t(t), L1_ffn_Wg, L1_ffn_bg, L1_ffn_W1, L1_ffn_b1, L1_ffn_W2, L1_ffn_b2)
    x = _from_tokens(t, x)
    return x

_drawn_inputs = setup_inputs


def setup_inputs(seed=0):
    import zlib

    import numpy as np

    out = dict(_drawn_inputs(seed))
    spreads = {'L0_conv_ln2d_w': (1.0, 0.6),
     'L0_conv_ln2d_b': (0.0, 0.8),
     'L0_conv_inproj_b': (0.0, 0.8),
     'L0_conv_dw2d_b': (0.0, 0.504),
     'L0_conv_ssm_ln_w': (1.0, 0.6),
     'L0_conv_ssm_ln_b': (0.0, 0.8),
     'L0_conv_ssm_in_b': (0.0, 0.8),
     'L0_conv_ssm_dw_b': (0.0, 0.8),
     'L0_conv_ssm_out_b': (0.0, 0.456),
     'L0_conv_outproj_b': (0.0, 0.1),
     'L1_attn_b_qkv': (0.0, 0.8),
     'L1_attn_kln_w': (1.0, 0.6),
     'L1_attn_kln_b': (0.0, 0.8),
     'L1_attn_vln_w': (1.0, 0.6),
     'L1_attn_vln_b': (0.0, 0.8),
     'L1_attn_b_proj': (0.0, 0.334),
     'L1_ffn_bg': (0.0, 0.1),
     'L1_ffn_b1': (0.0, 0.8),
     'L1_ffn_b2': (0.0, 0.302)}
    factors = {'L0_conv_inproj_w': 8.0,
     'L0_conv_dw2d_w': 8.0,
     'L0_conv_ssm_in_w': 8.0,
     'L0_conv_ssm_dw_w': 8.0,
     'L0_conv_ssm_out_w': 8.0,
     'L0_conv_outproj_w': 2.835,
     'L1_attn_W_qkv': 8.0,
     'L1_ffn_W1': 6.097,
     'L1_ffn_W2': 5.119}
    for name, (base, spread) in spreads.items():
        noise = np.random.default_rng([zlib.crc32(name.encode()), seed]).standard_normal(out[name].shape)
        drawn = base * np.exp(spread * noise) if base else spread * noise
        out[name] = jnp.asarray(drawn.astype(out[name].dtype))
    for name, factor in factors.items():
        out[name] = (out[name] * factor).astype(out[name].dtype)
    return out
```

```python
from contextlib import ExitStack

import concourse.bass as bass
from concourse import mybir

F32 = mybir.dt.float32
F32R = mybir.dt.float32r
BF16 = mybir.dt.bfloat16
I32 = mybir.dt.int32
ALU = mybir.AluOpType
ACT = mybir.ActivationFunctionType
AX = mybir.AxisListType

LN_EPS_CONV = 1e-6
LN_EPS_TOKEN = 1e-5
STD_EPS_HEAD = 1e-5
TINY_VARIANCE = 1e-19
CLAMP = 1e4
RSQRT_MAGIC = 0x5F3759DF

(V_LN0_W, V_LN0_B, V_IN_B, V_CONV_B, V_LN1_W, V_LN1_B, V_SSM_A_B, V_SSM_G_B, V_SSM_DW_B, V_SSM_OUT_B,
 V_OUT_B, V_Q_B, V_PROJ_B, V_B1) = range(14)


def conv_attention_moe(nc: bass.Bass, a: dict, out: bass.AP):
    B, C, H, W = a["x"].shape
    L = H * W
    P = 128
    PAIRS = B // 2
    T = L // P
    HID = a["L0_conv_ssm_in_w"].shape[0] // 2
    HEADS, _, HC = a["L1_attn_kln_w"].shape
    E, _, FH = a["L1_ffn_W1"].shape
    CK = FH // P
    V_B2 = V_B1 + E * CK
    NVEC = V_B2 + E
    PADW = W + 2
    PH = L + 2 * W
    assert 2 * C == P and HID == P and H == W and T == 2 and PAIRS == 2 and 2 * L == 512

    with ExitStack() as ctx:
        def sb(name, shape, dt=F32):
            return ctx.enter_context(nc.sbuf_tensor(name, shape, dt))

        def ps(name, shape, dt=F32):
            return ctx.enter_context(nc.psum_tensor(name, shape, dt))

        def sem(name):
            return ctx.enter_context(nc.semaphore(name))

        psT = ps("psT", [P, PAIRS, 512])
        psM = ps("psM", [P, PAIRS, 512])
        psA = ps("psA", [P, PAIRS, 512])
        psB = ps("psB", [P, PAIRS, 512])

        vec_rows = sb("vec_rows", [NVEC, P])
        nat_in = sb("nat_in", [P, P])
        nat_ssm = sb("nat_ssm", [P, 2, 2, P])
        nat_sout = sb("nat_sout", [P, HID])
        nat_bd = sb("nat_bd", [P, 5, P])
        OUTPROJ, WK, WV, WQ, WPROJ = range(5)
        kv_row = sb("kv_row", [1, 3, 2, 2, C])
        conv_w = sb("conv_w", [P, 9])
        sdw_w = sb("sdw_w", [P, 3])
        gate_w = sb("gate_w", [P, E])
        gate_b = sb("gate_b", [P, E])
        w1_nat = sb("w1_nat", [P, E, FH])
        w2_sb = sb("w2_sb", [P, E * CK, C])

        ident = sb("ident", [P, P])
        ident_aug = sb("ident_aug", [P, P + 1])
        ident_bf = sb("ident_bf", [P, P], BF16)
        pick3 = sb("pick3", [3 * 2 * E, 2 * E], BF16)
        pick_q = sb("pick_q", [3 * 2 * E, E, 2, C], BF16)
        ones_row = sb("ones_row", [1, P])
        head_mask = sb("head_mask", [P, P])
        minus_clamp = sb("minus_clamp", [P, 512])
        rev8 = sb("rev8", [P, E])
        vec = sb("vec", [P, NVEC])
        in_raw = sb("in_raw", [P, P])
        in_w = sb("in_w", [P, P])
        in_b = sb("in_b", [P, 1])
        ssm_raw = sb("ssm_raw", [P, 2, P])
        ssm_w = sb("ssm_w", [P, 2, 2, P])
        ssm_b = sb("ssm_b", [P, 2])
        half_g_b = sb("half_g_b", [P, 1])
        sout_raw = sb("sout_raw", [P, P])
        half_dw = sb("half_dw", [P, 3])
        sout_w = sb("sout_w", [P, 3, P])
        sout_b = sb("sout_b", [P, 1])
        outproj_w = sb("outproj_w", [P, P])
        outproj_q = sb("outproj_q", [P, C])
        kvT = sb("kvT", [P, 2, P])
        kv_gsum = sb("kv_gsum", [P, 4 * HEADS])
        kv_w = sb("kv_w", [P, 2 * P])
        kv_vecs = sb("kv_vecs", [P, 3, 2 * P])
        kv_bsum = sb("kv_bsum", [P, 4 * HEADS])
        kv_b = sb("kv_b", [P, 2 * P])
        proj_w = sb("proj_w", [P, P])
        w1_hl = sb("w1_hl", [P, E, FH], F32R)
        gate_hl = sb("gate_hl", [P, E], F32R)

        x_sb = sb("x_sb", [P, PAIRS, L])
        st = sb("st", [P, PAIRS, 4, 6])
        mv = sb("mv", [P, PAIRS, 4, 2])
        lnv = sb("lnv", [P, PAIRS, 4])
        rstd = sb("rstd", [P, PAIRS, 4])
        norm_t = sb("norm_t", [P, PAIRS, T, P])
        norm_d = sb("norm_d", [P, PAIRS, 2 * T, 2, C])
        norm_c = sb("norm_c", [P, PAIRS, L])
        zpad = sb("zpad", [P, PAIRS, H + 2, PADW])
        y_sb = sb("y_sb", [P, PAIRS, L])
        tanh_g = sb("tanh_g", [P, PAIRS, 2, L])
        a_sb = sb("a_sb", [P, PAIRS, 2, L])
        u_sb = sb("u_sb", [P, PAIRS, 2, PH])
        dirs = sb("dirs", [P, PAIRS, 2, 2 * L])
        dirs_fin = sb("dirs_fin", [P, PAIRS, 2, 2 * L], I32)
        dirs_pos = sb("dirs_pos", [P, PAIRS, 2, 2 * L])
        dirs_neg = sb("dirs_neg", [P, PAIRS, 2, 2 * L])
        dirs_sum = sb("dirs_sum", [P, PAIRS, 2 * L])
        o_sb = sb("o_sb", [P, PAIRS, L])
        o_fin = sb("o_fin", [P, PAIRS, L], I32)
        o_pos = sb("o_pos", [P, PAIRS, L])
        o_neg = sb("o_neg", [P, PAIRS, L])
        x1 = sb("x1", [P, PAIRS, L])
        xa_c = sb("xa_c", [P, PAIRS, L])
        x1_xa = sb("x1_xa", [P, PAIRS, L])
        kv = sb("kv", [P, PAIRS, T, 2 * P])
        kv_sq = sb("kv_sq", [P, PAIRS, T, 2 * P])
        ss = sb("ss", [P, PAIRS, T * 4 * HEADS])
        ss_ln = sb("ss_ln", [P, PAIRS, T * 4 * HEADS])
        std = sb("std", [P, PAIRS, T * 4 * HEADS])
        std_eps = sb("std_eps", [P, PAIRS, T * 4 * HEADS])
        rinv = sb("rinv", [P, PAIRS, T * 4 * HEADS])
        kv_n = sb("kv_n", [P, PAIRS, T, 2 * P])
        kv_nw = sb("kv_nw", [P, PAIRS, T, 2 * P])
        kv_nb = sb("kv_nb", [P, PAIRS, T, 2 * P])
        heads = sb("heads", [P, PAIRS, P])
        yq = sb("yq", [P, PAIRS, P + 1])
        zT = sb("zT", [P, PAIRS, P])
        zb = sb("zb", [P, PAIRS, 1])
        gelu_p = sb("gelu_p", [P, PAIRS, L])
        t2 = sb("t2", [P, PAIRS, L])
        ve = sb("ve", [P, PAIRS, 4])
        nhv = sb("nhv", [P, PAIRS, 4])
        guess = sb("guess", [P, PAIRS, 4, 4])
        sq = sb("sq", [P, PAIRS, 3, 4])
        xh = sb("xh", [P, PAIRS, 2 * L], F32R)
        xl = sb("xl", [P, PAIRS, 2 * L], F32R)
        lg = sb("lg", [P, PAIRS, 4, E])
        m1 = sb("m1", [P, PAIRS, 4])
        eq1 = sb("eq1", [P, PAIRS, 4, E])
        pr1 = sb("pr1", [P, PAIRS, 4, E])
        i1 = sb("i1", [P, PAIRS, 4])
        f1 = sb("f1", [P, PAIRS, 4, E])
        lg2 = sb("lg2", [P, PAIRS, 4, E])
        m2 = sb("m2", [P, PAIRS, 4])
        eq2 = sb("eq2", [P, PAIRS, 4, E])
        pr2 = sb("pr2", [P, PAIRS, 4, E])
        i2 = sb("i2", [P, PAIRS, 4])
        f2 = sb("f2", [P, PAIRS, 4, E])
        sel = sb("sel", [P, PAIRS, 4, E])
        m12 = sb("m12", [P, PAIRS, 4])
        ld = sb("ld", [P, PAIRS, 4, E])
        th = sb("th", [P, PAIRS, 4, E])
        wg2 = sb("wg2", [P, PAIRS, 4, E])
        wg = sb("wg", [P, PAIRS, 4, E])
        wr1 = sb("wr1", [P, PAIRS, 4, E])
        wr2 = sb("wr2", [P, PAIRS, 4, E])
        w3 = sb("w3", [P, PAIRS, T, 3, 2, E], BF16)
        w3T = sb("w3T", [3 * 2 * E, PAIRS, L], BF16)
        wbc = sb("wbc", [P, PAIRS, E, L])
        hs = sb("hs", [P, 4, 2 * L])
        prod = sb("prod", [P, 2, 2, L])
        acc = sb("acc", [P, PAIRS, 2, L])
        fin = sb("fin", [P, PAIRS, L])

        names = """x_in vec_in in_in conv_in ssm_in bd_in kvrow_in gate_in w1_in w2_in
            ident0 ident_ok aug_ok bf_ok zeros_ok nat_zero_ok pick0 pick_ok pickq_ok mask0 mask1 mask_ok ones_ok rev_ok clamp_ok
            vecT_ps vec_ok inT_ps in_raw_ok in_w_ok inb_ps in_b_ok
            ssmT_ps ssm_raw_ok ssm_w_ok ssmb_ps ssm_b_ok half_g_ok soutT_ps sout_raw_ok half_dw_ok sout_w_ok soutb_ps
            sout_b_ok bdT_ps outproj_ok outq_ok kvT_ok kvg_ok kvw_ok projT_ps proj_ok kvvec_ps kvvec_ok kvbg_ok kvb_ok
            w1h_ok w1l_ok gateh_ok gatel_ok
            tT_ps t_stats t_mv t_lnv t_rstd t_norm cT_ps c_norm
            z_ps z_ok taps y_ok ag_ps tanh_ok a_ok u_ok u_left u_right dirs_ps dirs_ok dirsfin_ok dpos_ok dneg_ok
            dsum_ok dclean_ok dall_ok out_ps o_ok ofin_ok opos_ok oneg_ok osum_ok oclean_ok x1_ok x1xa_ok
            kv_ps kv_ok kvsq_ok ss_ok ssln_ok std_ok stde_ok rinv_ok kvn_ok kvnw_ok kvnb_ok heads_ps heads_ok
            yq_ps yq_ok zT_ps zT_ok zb_ok p_ps gelu_ok t2_ok newton xdup_ps xh_ok xl_ok
            lg_ps gate_chain th_ok w3_ok w3T_ps w3T_ok wbc_ps wbc_ok
            h_ps h_ok e_ps prod_ok acc_ok acc_last fin_ok out_done""".split()
        S = {n: sem(n) for n in names}

        def per_q(ap):
            return ap.rearrange("p (q l) -> p q l", q=2)

        def cols(i, n=1):
            return vec[:, i:i + n]

        block = ctx.enter_context(nc.Block())

        def twice(v):
            return v.partition_broadcast(2).unsqueeze(0)

        qkv_rows = a["L1_attn_W_qkv"].rearrange("(h g d) c -> g h d c", g=3, d=HC)
        qkv_bias = a["L1_attn_b_qkv"].rearrange("(h g d) -> g h d", g=3, d=HC)
        x_pairs = a["x"].rearrange("(h q) c y x -> h (q c) (y x)", q=2)
        out_pairs = out.rearrange("(h q) c y x -> h (q c) (y x)", q=2)

        VEC_DMAS = 16 * 16
        vec2 = vec_rows[:, :].rearrange("r (q c) -> r q c", q=2)

        @block.sync
        def _(sp):
            for h in range(PAIRS):
                sp.dma_start(x_sb[:, h, :], x_pairs[h]).then_inc(S["x_in"], 16)
            for q in range(2):
                sp.dma_start(nat_in[q * C:(q + 1) * C, q * C:(q + 1) * C], a["L0_conv_inproj_w"]).then_inc(S["in_in"], 16)
            for q in range(2):
                sp.dma_start(conv_w[q * C:(q + 1) * C, :],
                             a["L0_conv_dw2d_w"].rearrange("c y x -> c (y x)")).then_inc(S["conv_in"], 16)
            for q in range(2):
                sp.dma_start(nat_ssm[:, :, q, q * C:(q + 1) * C],
                             a["L0_conv_ssm_in_w"].rearrange("(g o) c -> o g c", g=2)).then_inc(S["ssm_in"], 16)
            for q in range(2):
                sp.dma_start(nat_sout[q * C:(q + 1) * C, :], a["L0_conv_ssm_out_w"]).then_inc(S["ssm_in"], 16)
            sp.dma_start(sdw_w[:, :], a["L0_conv_ssm_dw_w"]).then_inc(S["ssm_in"], 16)
            for q in range(2):
                rows, c = slice(q * C, (q + 1) * C), slice(q * C, (q + 1) * C)
                sp.dma_start(nat_bd[rows, OUTPROJ, c], a["L0_conv_outproj_w"]).then_inc(S["bd_in"], 16)
                sp.dma_start(nat_bd[rows, WPROJ, c], a["L1_attn_W_proj"]).then_inc(S["bd_in"], 16)
            for j in range(CK):
                rows = slice(j * C, (j + 1) * C)
                sp.dma_start(w1_nat[rows, :, :], a["L1_ffn_W1"].rearrange("e d h -> d e h")).then_inc(S["w1_in"], 16)
            for h in range(PAIRS):
                sp.wait_ge(S["fin_ok"], h + 1)
                sp.dma_start(out_pairs[h], fin[:, h, :]).then_inc(S["out_done"], 16)
            sp.wait_ge(S["out_done"], 16 * PAIRS)

        @block.gpsimd
        def _(pool):
            nc.gpsimd.memset(ident[:, :], 0.0).then_inc(S["ident0"], 1)
            pool.wait_ge(S["ident0"], 1)
            nc.gpsimd.affine_select(out=ident[:, :], in_=ident[:, :], compare_op=ALU.not_equal, fill=1.0, base=0,
                                    pattern=[[-1, P]], channel_multiplier=1).then_inc(S["ident_ok"], 1)
            nc.gpsimd.memset(zpad[:, :, :, :], 0.0).then_inc(S["zeros_ok"], 1)
            nc.gpsimd.memset(u_sb[:, :, :, 0:1], 0.0).then_inc(S["zeros_ok"], 1)
            nc.gpsimd.memset(u_sb[:, :, :, PH - 1:PH], 0.0).then_inc(S["zeros_ok"], 1)
            nc.gpsimd.memset(ones_row[:, :], 1.0).then_inc(S["ones_ok"], 1)
            nc.gpsimd.memset(minus_clamp[:, :], -CLAMP).then_inc(S["clamp_ok"], 1)
            nc.gpsimd.iota(rev8[:, :], pattern=[[-1, E]], base=E, channel_multiplier=0,
                           allow_small_or_imprecise_dtypes=True).then_inc(S["rev_ok"], 1)
            hm = head_mask[:, :].rearrange("p (g d) -> p g d", d=HC)
            nc.gpsimd.memset(head_mask[:, :], 1.0 / L).then_inc(S["mask0"], 1)
            pool.wait_ge(S["mask0"], 1)
            nc.gpsimd.affine_select(out=hm, in_=hm, compare_op=ALU.is_ge, fill=0.0, base=0,
                                    pattern=[[-HC, P // HC], [0, HC]], channel_multiplier=1).then_inc(S["mask1"], 1)
            pool.wait_ge(S["mask1"], 1)
            nc.gpsimd.affine_select(out=hm, in_=hm, compare_op=ALU.is_ge, fill=0.0, base=HC - 1,
                                    pattern=[[HC, P // HC], [0, HC]], channel_multiplier=-1).then_inc(S["mask_ok"], 1)
            nc.gpsimd.memset(pick3[:, :], 0.0).then_inc(S["pick0"], 1)
            for j in range(3):
                pool.wait_ge(S["pick0"], j + 1)
                nc.gpsimd.affine_select(out=pick3[:, :], in_=pick3[:, :], compare_op=ALU.not_equal, fill=1.0,
                                        base=-2 * E * j, pattern=[[-1, 2 * E]],
                                        channel_multiplier=1).then_inc(S["pick0" if j < 2 else "pick_ok"], 1)
            pool.wait_ge(S["pick_ok"], 1)
            spread = pick3[:, :].rearrange("r (q e) -> r e q", q=2)
            for q in range(2):
                nc.gpsimd.tensor_copy(pick_q[:, :, q, :], spread[:, :, q:q + 1].to_broadcast([6 * E, E, C]))\
                    .then_inc(S["pickq_ok"], 1)
            pool.wait_ge(S["ident_ok"], 1)
            nc.gpsimd.tensor_copy(ident_bf[:, :], ident[:, :]).then_inc(S["bf_ok"], 1)
            nc.gpsimd.tensor_copy(ident_aug[:, 0:P], ident[:, :]).then_inc(S["aug_ok"], 1)
            nc.gpsimd.memset(ident_aug[:, P:P + 1], 0.0).then_inc(S["aug_ok"], 1)

            for h in range(PAIRS):
                pool.wait_ge(S["u_ok"], h + 1)
                pool.wait_ge(S["zeros_ok"], 3)
                nc.gpsimd.tensor_copy(u_sb[:, h, :, 1:W], u_sb[:, h, :, L:L + W - 1]).then_inc(S["u_left"], 1)
                nc.gpsimd.tensor_copy(u_sb[:, h, :, L + W:L + 2 * W - 1],
                                      u_sb[:, h, :, W + 1:2 * W]).then_inc(S["u_right"], 1)
            for h in range(PAIRS):
                for k in range(2):
                    pool.wait_ge(S["dirs_ok"], 2 * h + k + 1)
                    nc.gpsimd.tensor_scalar(dirs_pos[:, h, k, :], dirs[:, h, k, :], 0.0, CLAMP,
                                            ALU.max, ALU.min).then_inc(S["dpos_ok"], 1)
                    nc.gpsimd.tensor_scalar(dirs_neg[:, h, k, :], dirs[:, h, k, :], 0.0, -CLAMP,
                                            ALU.min, ALU.max).then_inc(S["dneg_ok"], 1)
            for h in range(PAIRS):
                pool.wait_ge(S["o_ok"], h + 1)
                nc.gpsimd.tensor_scalar(o_pos[:, h, :], o_sb[:, h, :], 0.0, CLAMP,
                                        ALU.max, ALU.min).then_inc(S["opos_ok"], 1)
                nc.gpsimd.tensor_scalar(o_neg[:, h, :], o_sb[:, h, :], 0.0, -CLAMP,
                                        ALU.min, ALU.max).then_inc(S["oneg_ok"], 1)
            for h in range(PAIRS):
                pool.wait_ge(S["kvn_ok"], h + 1)
                pool.wait_ge(S["kvvec_ok"], 1)
                wrep = kv_vecs[:, 1:2, :].to_broadcast([P, T, 2 * P])
                brep = kv_vecs[:, 2:3, :].to_broadcast([P, T, 2 * P])
                nc.gpsimd.tensor_tensor(kv_nw[:, h, :, :], kv_n[:, h, :, :], wrep, ALU.mult).then_inc(S["kvnw_ok"], 1)
                pool.wait_ge(S["kvnw_ok"], h + 1)
                nc.gpsimd.tensor_tensor(kv_nb[:, h, :, :], kv_nw[:, h, :, :], brep, ALU.add).then_inc(S["kvnb_ok"], 1)
                pool.wait_ge(S["x1_ok"], h + 1)
                pool.wait_ge(S["c_norm"], 2 * PAIRS + h + 1)
                nc.gpsimd.tensor_tensor(x1_xa[:, h, :], x1[:, h, :], xa_c[:, h, :], ALU.add).then_inc(S["x1xa_ok"], 1)
            n = 0
            for h in range(PAIRS):
                for e in range(0, E, 2):
                    pool.wait_ge(S["prod_ok"], 2 * n + 2)
                    if e:
                        pool.wait_ge(S["acc_ok"], n)
                        nc.gpsimd.tensor_tensor(acc[:, h, :, :], acc[:, h, :, :], prod[:, n % 2, :, :],
                                                ALU.add).then_inc(S["acc_ok"], 1)
                    else:
                        pool.wait_ge(S["t2_ok"], h + 1)
                        nc.gpsimd.tensor_tensor(acc[:, h, 0, :], t2[:, h, :], prod[:, n % 2, 0, :], ALU.add)
                        nc.gpsimd.tensor_copy(acc[:, h, 1, :], prod[:, n % 2, 1, :]).then_inc(S["acc_ok"], 1)
                    n += 1

        @block.scalar
        def _(act):
            for r, v in ((V_LN0_W, "L0_conv_ln2d_w"), (V_LN0_B, "L0_conv_ln2d_b"), (V_IN_B, "L0_conv_inproj_b"),
                         (V_CONV_B, "L0_conv_dw2d_b"), (V_LN1_W, "L0_conv_ssm_ln_w"), (V_LN1_B, "L0_conv_ssm_ln_b"),
                         (V_SSM_OUT_B, "L0_conv_ssm_out_b"), (V_OUT_B, "L0_conv_outproj_b"), (V_PROJ_B, "L1_attn_b_proj")):
                act.dma_start(vec2[r:r + 1], twice(a[v])).then_inc(S["vec_in"], 16)
            for g in range(2):
                act.dma_start(vec_rows[V_SSM_A_B + g:V_SSM_A_B + g + 1, :],
                              a["L0_conv_ssm_in_b"][g * P:(g + 1) * P].unsqueeze(0)).then_inc(S["vec_in"], 16)
            act.dma_start(vec_rows[V_SSM_DW_B:V_SSM_DW_B + 1, :], a["L0_conv_ssm_dw_b"].unsqueeze(0)).then_inc(S["vec_in"], 16)
            for q in range(2):
                act.dma_start(vec2[V_Q_B:V_Q_B + 1, q, :].rearrange("r (h d) -> r h d", d=HC),
                              qkv_bias[0:1]).then_inc(S["vec_in"], 16)
            act.dma_start(vec_rows[V_B1:V_B1 + E * CK, :],
                          a["L1_ffn_b1"].rearrange("e (k j) -> (e k) j", j=P)).then_inc(S["vec_in"], 16)
            act.dma_start(vec2[V_B2:V_B2 + E, :, :],
                          a["L1_ffn_b2"].unsqueeze(1).to_broadcast([E, 2, C])).then_inc(S["vec_in"], 16)
            for q in range(2):
                for i, g in ((WK, 1), (WV, 2), (WQ, 0)):
                    act.dma_start(nat_bd[q * C:(q + 1) * C, i, q * C:(q + 1) * C], qkv_rows[g]).then_inc(S["bd_in"], 16)
            for q in range(2):
                for g in range(2):
                    act.dma_start(kv_row[:, 0, g, q, :].rearrange("p (h d) -> p h d", d=HC),
                                  qkv_bias[g + 1:g + 2]).then_inc(S["kvrow_in"], 16)
                    for i, v in ((1, ("L1_attn_kln_w", "L1_attn_vln_w")), (2, ("L1_attn_kln_b", "L1_attn_vln_b"))):
                        act.dma_start(kv_row[:, i, g, q, :],
                                      a[v[g]].rearrange("h o d -> o (h d)")).then_inc(S["kvrow_in"], 16)
            for q in range(2):
                act.dma_start(gate_w[q * C:(q + 1) * C, :], a["L1_ffn_Wg"]).then_inc(S["gate_in"], 16)
            act.dma_start(gate_b[:, :], a["L1_ffn_bg"].partition_broadcast(P)).then_inc(S["gate_in"], 16)
            act.dma_start(w2_sb[:, :, :], a["L1_ffn_W2"].rearrange("e (k j) d -> j (e k) d", j=P)).then_inc(S["w2_in"], 16)

            nc.scalar.preload_act_table_set("natural_log_exp_and_others")

            def rsqrt(n, h, eps):
                act.wait_ge(S["t_mv"], PAIRS * n + h + 1)
                nc.scalar.activation(lnv[:, h, :], mv[:, h, :, 1], ACT.Ln, bias=eps).then_inc(S["t_lnv"], 1)
                act.wait_ge(S["t_lnv"], PAIRS * n + h + 1)
                nc.scalar.activation(rstd[:, h, :], lnv[:, h, :], ACT.Exp, scale=-0.5).then_inc(S["t_rstd"], 1)

            def norm_out(n, h, dst):
                act.wait_ge(S["cT_ps"], PAIRS * n + h + 1)
                nc.scalar.copy(dst[:, h, :], psT[:, h, L:2 * L]).then_inc(S["c_norm"], 1)

            act.wait_ge(S["vecT_ps"], 1)
            act.wait_ge(S["inT_ps"], 1)
            nc.scalar.copy(vec[:, :], psA[:, 0, P:P + NVEC]).then_inc(S["vec_ok"], 1)
            nc.scalar.copy(in_raw[:, :], psA[:, 0, 0:P]).then_inc(S["in_raw_ok"], 1)
            act.wait_ge(S["vec_ok"], 1)
            nc.scalar.activation(in_w[:, :], psA[:, 0, 0:P], ACT.Copy, scale=cols(V_LN0_W)).then_inc(S["in_w_ok"], 1)
            act.wait_ge(S["inb_ps"], 1)
            nc.scalar.activation(in_b[:, :], psA[:, 0, 256:257], ACT.Identity, bias=cols(V_IN_B)).then_inc(S["in_b_ok"], 1)
            for h in range(PAIRS):
                rsqrt(0, h, LN_EPS_CONV)
            for h in range(PAIRS):
                norm_out(0, h, norm_c)
            for h in range(PAIRS):
                act.wait_ge(S["z_ps"], h + 1)
                act.wait_ge(S["zeros_ok"], 1)
                act.wait_ge(S["in_b_ok"], 1)
                nc.scalar.activation(zpad[:, h, 1:H + 1, 1:W + 1], psM[:, h, 0:L].rearrange("p (y x) -> p y x", x=W),
                                     ACT.Identity, bias=in_b[:, 0:1]).then_inc(S["z_ok"], 1)

            act.wait_ge(S["ssmT_ps"], 1)
            nc.scalar.activation(ssm_w[:, :, :, :].rearrange("p g q o -> p (g q o)"), psA[:, 1, :], ACT.Copy,
                                 scale=cols(V_LN1_W)).then_inc(S["ssm_w_ok"], 1)
            nc.scalar.copy(ssm_raw[:, :, :], psA[:, 1, :].rearrange("p (g q o) -> p g q o", g=2, q=2)[:, :, 0, :])\
                .then_inc(S["ssm_raw_ok"], 1)
            act.wait_ge(S["soutT_ps"], 1)
            act.wait_ge(S["bdT_ps"], 1)
            nc.scalar.copy(sout_raw[:, :], psB[:, 0, 0:P]).then_inc(S["sout_raw_ok"], 1)
            act.wait_ge(S["ssm_in"], 16 * 5)
            nc.scalar.mul(half_dw[:, :], sdw_w[:, :], 0.5).then_inc(S["half_dw_ok"], 1)
            act.wait_ge(S["half_dw_ok"], 1)
            for tap, (fwd, bwd) in enumerate(((0, 2), (1, 1), (2, 0))):
                for d, k in enumerate((fwd, bwd)):
                    nc.scalar.activation(sout_w[:, tap, d * C:(d + 1) * C], psB[:, 0, d * C:(d + 1) * C], ACT.Copy,
                                         scale=half_dw[:, k:k + 1]).then_inc(S["sout_w_ok"], 1)
            nc.scalar.copy(outproj_w[:, :], psB[:, 0, P:2 * P]).then_inc(S["outproj_ok"], 1)
            nc.scalar.copy(kvT[:, :, :], psB[:, 0, 2 * P:4 * P].rearrange("p (g o) -> p g o", g=2)).then_inc(S["kvT_ok"], 1)
            act.wait_ge(S["projT_ps"], 1)
            act.wait_ge(S["ssmb_ps"], 1)
            act.wait_ge(S["soutb_ps"], 1)
            act.wait_ge(S["kvvec_ps"], 1)
            nc.scalar.copy(proj_w[:, :], psB[:, 1, 0:P]).then_inc(S["proj_ok"], 1)
            nc.scalar.activation(ssm_b[:, 0:1], psB[:, 1, P:P + 1], ACT.Identity, bias=cols(V_SSM_A_B)).then_inc(S["ssm_b_ok"], 1)
            nc.scalar.activation(ssm_b[:, 1:2], psB[:, 1, P + 1:P + 2], ACT.Identity, bias=cols(V_SSM_G_B)).then_inc(S["ssm_b_ok"], 1)
            act.wait_ge(S["ssm_b_ok"], 2)
            nc.scalar.mul(half_g_b[:, :], ssm_b[:, 1:2], 0.5).then_inc(S["half_g_ok"], 1)
            nc.scalar.activation(sout_b[:, :], psB[:, 1, P + 2:P + 3], ACT.Identity, bias=cols(V_SSM_OUT_B)).then_inc(S["sout_b_ok"], 1)
            nc.scalar.copy(kv_vecs[:, 0:2, :].rearrange("p i n -> p (i n)"), psA[:, 0, :])
            nc.scalar.copy(kv_vecs[:, 2, :], psB[:, 1, 256:512]).then_inc(S["kvvec_ok"], 1)
            act.wait_ge(S["w1_in"], 32)
            nc.scalar.copy(w1_hl[:, :, :], w1_nat[:, :, :]).then_inc(S["w1h_ok"], 1)
            act.wait_ge(S["gate_in"], 48)
            nc.scalar.copy(gate_hl[:, :], gate_w[:, :]).then_inc(S["gateh_ok"], 1)

            for h in range(PAIRS):
                rsqrt(1, h, LN_EPS_CONV)
            nc.scalar.preload_act_table_set("gelu_and_others")
            for h in range(PAIRS):
                norm_out(1, h, norm_c)
            for h in range(PAIRS):
                act.wait_ge(S["ag_ps"], 2 * h + 1)
                act.wait_ge(S["half_g_ok"], 1)
                nc.scalar.activation(tanh_g[:, h, :, :], per_q(psB[:, h, :]), ACT.Tanh, bias=half_g_b[:, 0:1],
                                     scale=0.5).then_inc(S["tanh_ok"], 1)
                act.wait_ge(S["ag_ps"], 2 * h + 2)
                nc.scalar.activation(a_sb[:, h, :, :], per_q(psA[:, h, :]), ACT.Identity,
                                     bias=ssm_b[:, 0:1]).then_inc(S["a_ok"], 1)
            nc.scalar.preload_act_table_set("natural_log_exp_and_others")
            for h in range(PAIRS):
                for k, bank in enumerate((psA, psB)):
                    act.wait_ge(S["dirs_ps"], 2 * h + k + 1)
                    act.wait_ge(S["sout_b_ok"], 1)
                    nc.scalar.activation(dirs[:, h, k, :], bank[:, h, :], ACT.Identity,
                                         bias=sout_b[:, 0:1]).then_inc(S["dirs_ok"], 1)
            for h in range(PAIRS):
                act.wait_ge(S["out_ps"], h + 1)
                nc.scalar.activation(o_sb[:, h, :], psM[:, h, 0:L], ACT.Identity, bias=cols(V_OUT_B)).then_inc(S["o_ok"], 1)
            for h in range(PAIRS):
                rsqrt(2, h, LN_EPS_TOKEN)
            for h in range(PAIRS):
                norm_out(2, h, xa_c)
            for h in range(PAIRS):
                act.wait_ge(S["kv_ok"], h + 1)
                nc.scalar.activation(kv_sq[:, h, :, :], kv[:, h, :, :], ACT.Square).then_inc(S["kvsq_ok"], 1)
            for h in range(PAIRS):
                act.wait_ge(S["ss_ok"], h + 1)
                nc.scalar.activation(ss_ln[:, h, :], ss[:, h, :], ACT.Ln, scale=1.0 / (HC - 1),
                                     bias=TINY_VARIANCE).then_inc(S["ssln_ok"], 1)
                act.wait_ge(S["ssln_ok"], h + 1)
                nc.scalar.activation(std[:, h, :], ss_ln[:, h, :], ACT.Exp, scale=0.5).then_inc(S["std_ok"], 1)
            nc.scalar.preload_act_table_set("gelu_and_others")
            for h in range(PAIRS):
                act.wait_ge(S["zT_ps"], 2 * h + 2)
                nc.scalar.copy(zT[:, h, :], psT[:, h, 0:P]).then_inc(S["zT_ok"], 1)
                nc.scalar.activation(zb[:, h, :], psT[:, h, P:P + 1], ACT.Identity, bias=cols(V_PROJ_B)).then_inc(S["zb_ok"], 1)
            for h in range(PAIRS):
                act.wait_ge(S["p_ps"], h + 1)
                act.wait_ge(S["zb_ok"], h + 1)
                nc.scalar.activation(gelu_p[:, h, :], psM[:, h, 0:L], ACT.Gelu, bias=zb[:, h, :]).then_inc(S["gelu_ok"], 1)
            for h in range(PAIRS):
                act.wait_ge(S["xdup_ps"], h + 1)
                nc.scalar.copy(xh[:, h, :], psT[:, h, :]).then_inc(S["xh_ok"], 1)

            n = 0
            for h in range(PAIRS):
                for j in range(E * CK):
                    act.wait_ge(S["h_ps"], n + 1)
                    if n >= 4:
                        act.wait_ge(S["e_ps"], (n - 4) // CK + 1)
                    nc.scalar.activation(hs[:, n % 4, :], (psA, psB)[n % 2][:, n // 2 % 2, :], ACT.Gelu,
                                         bias=cols(V_B1 + j)).then_inc(S["h_ok"], 1)
                    n += 1
                    if j == 5:
                        act.wait_ge(S["gate_chain"], 21 * h + 13)
                        nc.scalar.activation(th[:, h, :, :], ld[:, h, :, :], ACT.Tanh, scale=0.5).then_inc(S["th_ok"], 1)

        @block.tensor
        def _(pe):
            def to_tokens(n, h, src):
                for t in range(T):
                    m = nc.tensor.transpose(psT[:, h, t * P:(t + 1) * P], src[:, h, t * P:(t + 1) * P], ident[:, :])
                m.then_inc(S["tT_ps"], 1)

            def to_channels(n, h):
                pe.wait_ge(S["t_norm"], PAIRS * n + h + 1)
                for t in range(T):
                    m = nc.tensor.transpose(psT[:, h, L + t * P:L + (t + 1) * P], norm_t[:, h, t, :], ident[:, :])
                m.then_inc(S["cT_ps"], 1)

            pe.wait_ge(S["ident_ok"], 1)
            for h in range(PAIRS):
                pe.wait_ge(S["x_in"], 16 * PAIRS)
                to_tokens(0, h, x_sb)
            pe.wait_ge(S["vec_in"], VEC_DMAS)
            nc.tensor.transpose(psA[:, 0, P:P + NVEC], vec_rows[:, :], ident[0:NVEC, 0:NVEC]).then_inc(S["vecT_ps"], 1)
            pe.wait_ge(S["in_in"], 32)
            pe.wait_ge(S["nat_zero_ok"], 1)
            nc.tensor.transpose(psA[:, 0, 0:P], nat_in[:, :], ident[:, :]).then_inc(S["inT_ps"], 1)
            pe.wait_ge(S["in_raw_ok"], 1)
            pe.wait_ge(S["in_w_ok"], 1)
            nc.tensor.matmul(psA[:, 0, 256:257], in_raw[:, :], cols(V_LN0_B), start=True, stop=True).then_inc(S["inb_ps"], 1)
            for h in range(PAIRS):
                to_channels(0, h)
            for h in range(PAIRS):
                pe.wait_ge(S["c_norm"], h + 1)
                pe.wait_ge(S["in_w_ok"], 1)
                nc.tensor.matmul(psM[:, h, 0:L], in_w[:, :], norm_c[:, h, :], start=True, stop=True).then_inc(S["z_ps"], 1)

            pe.wait_ge(S["ssm_in"], 16 * 5)
            pe.wait_ge(S["nat_zero_ok"], 4)
            for g in range(2):
                for q in range(2):
                    m = nc.tensor.transpose(psA[:, 1, (2 * g + q) * P:(2 * g + q + 1) * P], nat_ssm[:, g, q, :], ident[:, :])
            m.then_inc(S["ssmT_ps"], 1)
            nc.tensor.transpose(psB[:, 0, 0:P], nat_sout[:, :], ident[:, :]).then_inc(S["soutT_ps"], 1)
            pe.wait_ge(S["bd_in"], 16 * 10)
            for j, i in enumerate((OUTPROJ, WK, WV)):
                m = nc.tensor.transpose(psB[:, 0, (j + 1) * P:(j + 2) * P], nat_bd[:, i, :], ident[:, :])
            m.then_inc(S["bdT_ps"], 1)
            nc.tensor.transpose(psB[:, 1, 0:P], nat_bd[:, WPROJ, :], ident[:, :]).then_inc(S["projT_ps"], 1)
            pe.wait_ge(S["ssm_raw_ok"], 1)
            for g in range(2):
                m = nc.tensor.matmul(psB[:, 1, P + g:P + g + 1], ssm_raw[:, g, :], cols(V_LN1_B), start=True, stop=True)
            m.then_inc(S["ssmb_ps"], 1)
            pe.wait_ge(S["sout_raw_ok"], 1)
            nc.tensor.matmul(psB[:, 1, P + 2:P + 3], sout_raw[:, :], cols(V_SSM_DW_B), start=True, stop=True)\
                .then_inc(S["soutb_ps"], 1)
            pe.wait_ge(S["kvrow_in"], 16 * 12)
            pe.wait_ge(S["ones_ok"], 1)
            pe.wait_ge(S["in_b_ok"], 1)
            pe.wait_ge(S["in_w_ok"], 1)
            flat = kv_row[:, :, :, :, :].rearrange("p i g q c -> p (i g q c)")
            nc.tensor.matmul(psA[:, 0, :], ones_row[:, :], flat[:, 0:512], start=True, stop=True)
            nc.tensor.matmul(psB[:, 1, 256:512], ones_row[:, :], flat[:, 512:768], start=True, stop=True)\
                .then_inc(S["kvvec_ps"], 1)

            for h in range(PAIRS):
                pe.wait_ge(S["y_ok"], h + 1)
                pe.wait_ge(S["t_norm"], h + 1)
                to_tokens(1, h, y_sb)
            for h in range(PAIRS):
                pe.wait_ge(S["c_norm"], h + 1)
                to_channels(1, h)
            for h in range(PAIRS):
                pe.wait_ge(S["c_norm"], PAIRS + h + 1)
                pe.wait_ge(S["ssm_w_ok"], 1)
                pe.wait_ge(S["kvvec_ok"], 1)
                pe.wait_ge(S["sout_w_ok"], 6)
                pe.wait_ge(S["kvT_ok"], 1)
                for g, bank in ((1, psB), (0, psA)):
                    for q in range(2):
                        m = nc.tensor.matmul(bank[:, h, q * L:(q + 1) * L], ssm_w[:, g, q, :], norm_c[:, h, :],
                                             start=True, stop=True)
                    m.then_inc(S["ag_ps"], 1)
            for h in range(PAIRS):
                pe.wait_ge(S["u_ok"], h + 1)
                mid = u_sb[:, h, :, W:W + L]
                bank = per_q(psA[:, h, :])
                nc.tensor.matmul(bank, sout_w[:, 1, :], mid, start=True, stop=False)
                nc.tensor.matmul(bank[:, :, 1:L], sout_w[:, 0, :], u_sb[:, h, :, W:W + L - 1], start=False, stop=False)
                nc.tensor.matmul(bank[:, :, 0:L - 1], sout_w[:, 2, :], u_sb[:, h, :, W + 1:W + L], start=False,
                                 stop=True).then_inc(S["dirs_ps"], 1)
                bank = per_q(psB[:, h, :])
                nc.tensor.matmul(bank, sout_w[:, 1, :], mid, start=True, stop=False)
                pe.wait_ge(S["u_left"], h + 1)
                nc.tensor.matmul(bank, sout_w[:, 0, :], u_sb[:, h, :, 0:L], start=False, stop=False)
                pe.wait_ge(S["u_right"], h + 1)
                nc.tensor.matmul(bank, sout_w[:, 2, :], u_sb[:, h, :, 2 * W:2 * W + L], start=False,
                                 stop=True).then_inc(S["dirs_ps"], 1)
            for h in range(PAIRS):
                pe.wait_ge(S["outproj_ok"], 1)
                pe.wait_ge(S["outq_ok"], 1)
                nc.tensor.matmul(psM[:, h, 0:L], outproj_w[:, :], y_sb[:, h, :], start=True, stop=False)
                pe.wait_ge(S["dall_ok"], h + 1)
                for q in range(2):
                    m = nc.tensor.matmul(psM[q * C:(q + 1) * C, h, 0:L], outproj_q[:, :], dirs_sum[:, h, q * L:(q + 1) * L],
                                         start=False, stop=True)
                m.then_inc(S["out_ps"], 1)
            for h in range(PAIRS):
                pe.wait_ge(S["x1_ok"], h + 1)
                to_tokens(2, h, x1)
            for h in range(PAIRS):
                to_channels(2, h)
            for h in range(PAIRS):
                pe.wait_ge(S["c_norm"], 2 * PAIRS + h + 1)
                pe.wait_ge(S["kvw_ok"], 1)
                pe.wait_ge(S["dirs_ok"], 2 * h + 1)
                for t in range(T):
                    m = nc.tensor.matmul(psA[:, h, t * 2 * P:(t + 1) * 2 * P], xa_c[:, h, t * P:(t + 1) * P], kv_w[:, :],
                                         start=True, stop=True)
                m.then_inc(S["kv_ps"], 1)
            for h in range(PAIRS):
                pe.wait_ge(S["kvnb_ok"], h + 1)
                pe.wait_ge(S["dirs_ok"], 2 * h + 2)
                for t in range(T):
                    m = nc.tensor.matmul(psB[:, h, 0:P], kv_nb[:, h, t, 0:P], kv_nb[:, h, t, P:2 * P],
                                         start=(t == 0), stop=(t == T - 1))
                m.then_inc(S["heads_ps"], 1)
            for h in range(PAIRS):
                pe.wait_ge(S["heads_ok"], h + 1)
                nc.tensor.matmul(psB[:, h, P:2 * P], heads[:, h, :], nat_bd[:, WQ, :], start=True, stop=True)
                nc.tensor.matmul(psB[:, h, 2 * P:2 * P + 1], heads[:, h, :], cols(V_Q_B), start=True,
                                 stop=True).then_inc(S["yq_ps"], 1)
            for h in range(PAIRS):
                pe.wait_ge(S["yq_ok"], h + 1)
                pe.wait_ge(S["proj_ok"], 1)
                nc.tensor.matmul(psT[:, h, 0:P], yq[:, h, 0:P], proj_w[:, :], start=True, stop=True).then_inc(S["zT_ps"], 1)
                nc.tensor.matmul(psT[:, h, P:P + 1], proj_w[:, :], yq[:, h, P:P + 1], start=True,
                                 stop=True).then_inc(S["zT_ps"], 1)
            for h in range(PAIRS):
                pe.wait_ge(S["zT_ok"], h + 1)
                pe.wait_ge(S["o_ok"], h + 1)
                nc.tensor.matmul(psM[:, h, 0:L], zT[:, h, :], xa_c[:, h, :], start=True, stop=True).then_inc(S["p_ps"], 1)
            for h in range(PAIRS):
                pe.wait_ge(S["t2_ok"], h + 1)
                pe.wait_ge(S["zb_ok"], h + 1)
                to_tokens(3, h, t2)
            for h in range(PAIRS):
                pe.wait_ge(S["t_norm"], 3 * PAIRS + h + 1)
                for q in range(2):
                    for t in range(T):
                        src = norm_d[:, h, q * T + t, :, :].rearrange("p a c -> p (a c)")
                        m = nc.tensor.transpose(psT[:, h, (q * T + t) * P:(q * T + t + 1) * P], src, ident[:, :])
                m.then_inc(S["xdup_ps"], 1)

            n = 0

            def hidden(h, j, n):
                if n >= 4:
                    pe.wait_ge(S["h_ok"], n - 3)
                e, k = divmod(j, CK)
                w = w1_hl[:, e, k * P:(k + 1) * P]
                bank = (psA, psB)[n % 2][:, n // 2 % 2, :]
                nc.tensor.matmul(bank, w, xh[:, h, :], start=True, stop=False)
                nc.tensor.matmul(bank, w, xl[:, h, :], start=False, stop=True).then_inc(S["h_ps"], 1)

            def expert(h, e, m0):
                n_e = m0
                bank = n_e // 2 % 2
                if n_e >= 4 and n_e % 2 == 0:
                    pe.wait_ge(S["prod_ok"], n_e - 2)
                if n_e % 2 == 1 and n_e >= 4:
                    pass
                c0 = (n_e % 2) * L
                for k in range(CK):
                    s = CK * n_e + k
                    pe.wait_ge(S["h_ok"], s + 1)
                    for q in range(2):
                        m = nc.tensor.matmul(psM[q * C:(q + 1) * C, bank, c0:c0 + L], w2_sb[:, e * CK + k, :],
                                             hs[:, s % 4, q * L:(q + 1) * L], start=(k == 0), stop=(k == CK - 1))
                m.then_inc(S["e_ps"], 1)

            for h in range(PAIRS):
                if h == 0:
                    pe.wait_ge(S["w1l_ok"], 1)
                    pe.wait_ge(S["gatel_ok"], 1)
                    pe.wait_ge(S["w2_in"], 16)
                    pe.wait_ge(S["yq_ok"], PAIRS)
                    pe.wait_ge(S["gelu_ok"], PAIRS)
                pe.wait_ge(S["xh_ok"], h + 1)
                pe.wait_ge(S["xl_ok"], h + 1)
                for g in range(4):
                    for x_part in (xh, xl):
                        m = nc.tensor.matmul(psT[:, h, E * g:E * (g + 1)], x_part[:, h, g * P:(g + 1) * P], gate_hl[:, :],
                                             start=(x_part is xh), stop=(x_part is xl))
                m.then_inc(S["lg_ps"], 1)
                for e in range(E):
                    for k in range(CK):
                        hidden(h, e * CK + k, CK * (E * h + e) + k)
                    if e >= 1:
                        expert(h, e - 1, E * h + e - 1)
                    if e == 3:
                        pe.wait_ge(S["w3_ok"], h + 1)
                        pe.wait_ge(S["bf_ok"], 1)
                        pT = psT[:, h, 256:512].bitcast(BF16)
                        for t in range(T):
                            m = nc.tensor.transpose(pT[0:6 * E, t * P:(t + 1) * P],
                                                    w3[:, h, t].rearrange("p i q e -> p (i q e)"), ident_bf[:, :])
                        m.then_inc(S["w3T_ps"], 1)
                    if e >= 4:
                        i = e - 4
                        pe.wait_ge(S["w3T_ok"], h + 1)
                        pe.wait_ge(S["pickq_ok"], 2)
                        if i:
                            pe.wait_ge(S["wbc_ok"], 4 * h + i)
                        for g in range(2):
                            pick = pick_q[:, 2 * i + g, :, :].rearrange("r q c -> r (q c)")
                            m = nc.tensor.matmul(psT[:, h, g * L:(g + 1) * L], pick, w3T[:, h, :], start=True, stop=True)
                        m.then_inc(S["wbc_ps"], 1)
                expert(h, E - 1, E * h + E - 1)

        @block.vector
        def _(dve):
            nc.vector.memset(nat_in[0:C, C:P], 0.0)
            nc.vector.memset(nat_in[C:P, 0:C], 0.0).then_inc(S["nat_zero_ok"], 1)
            for q in range(2):
                nc.vector.memset(nat_ssm[:, :, q, (1 - q) * C:(2 - q) * C], 0.0).then_inc(S["nat_zero_ok"], 1)
            nc.vector.memset(nat_bd[0:C, :, C:P], 0.0)
            nc.vector.memset(nat_bd[C:P, :, 0:C], 0.0).then_inc(S["nat_zero_ok"], 1)

            def stats(n, h):
                dve.wait_ge(S["tT_ps"], PAIRS * n + h + 1)
                if n:
                    dve.wait_ge(S["t_norm"], PAIRS * (n - 1) + h + 1)
                for g in range(4):
                    m = nc.vector.bn_stats(st[:, h, g, :], psT[:, h, g * C:(g + 1) * C])
                m.then_inc(S["t_stats"], 1)
                dve.wait_ge(S["t_stats"], PAIRS * n + h + 1)
                for g in range(4):
                    m = nc.vector.bn_aggr(mv[:, h, g, :], st[:, h, g, :])
                m.then_inc(S["t_mv"], 1)

            def normalise(n, h, r=None):
                r = rstd[:, h, :] if r is None else r
                if n < 3:
                    dve.wait_ge(S["t_rstd"], PAIRS * n + h + 1)
                if n:
                    dve.wait_ge(S["cT_ps"], PAIRS * (n - 1) + h + 1)
                for g in range(4):
                    if n == 3:
                        t, q = divmod(g, 2)
                        src = psT[:, h, g * C:(g + 1) * C].unsqueeze(1).to_broadcast([P, 2, C])
                        m = nc.vector.tensor_scalar(norm_d[:, h, q * T + t, :, :], src, mv[:, h, g, 0:1], r[:, g:g + 1],
                                                    ALU.subtract, ALU.mult)
                        continue
                    m = nc.vector.tensor_scalar(norm_t[:, h, g // 2, (g % 2) * C:(g % 2 + 1) * C],
                                                psT[:, h, g * C:(g + 1) * C], mv[:, h, g, 0:1], r[:, g:g + 1],
                                                ALU.subtract, ALU.mult)
                m.then_inc(S["t_norm"], 1)

            for h in range(PAIRS):
                stats(0, h)
            for h in range(PAIRS):
                normalise(0, h)
            dve.wait_ge(S["conv_in"], 32)
            dve.wait_ge(S["vec_ok"], 1)
            for tap in range(9):
                dy, dx = divmod(tap, 3)
                for h in range(PAIRS):
                    z = zpad[:, h, dy:dy + H, dx:dx + W]
                    y = y_sb[:, h, :].rearrange("p (y x) -> p y x", x=W)
                    if tap == 0:
                        dve.wait_ge(S["z_ok"], h + 1)
                        nc.vector.tensor_scalar(y, z, conv_w[:, 0:1], cols(V_CONV_B), ALU.mult, ALU.add)\
                            .then_inc(S["taps"], 1)
                    else:
                        dve.wait_ge(S["taps"], PAIRS * (tap - 1) + h + 1)
                        nc.vector.scalar_tensor_tensor(out=y, in0=z, scalar=conv_w[:, tap:tap + 1], in1=y,
                                                       op0=ALU.mult, op1=ALU.add)\
                            .then_inc(S["taps" if tap < 8 else "y_ok"], 1)
            for h in range(PAIRS):
                stats(1, h)
            for h in range(PAIRS):
                normalise(1, h)
            dve.wait_ge(S["outproj_ok"], 1)
            for q in range(2):
                m = nc.vector.tensor_scalar(outproj_q[q * C:(q + 1) * C, :], outproj_w[q * C:(q + 1) * C, q * C:(q + 1) * C],
                                            0.25, None, ALU.mult)
            m.then_inc(S["outq_ok"], 1)
            dve.wait_ge(S["kvT_ok"], 1)
            by_head = kvT[:, :, :].rearrange("p g (h d) -> p (g h) d", d=HC)
            nc.vector.tensor_reduce(kv_gsum[:, :], by_head, AX.X, ALU.add).then_inc(S["kvg_ok"], 1)
            dve.wait_ge(S["kvvec_ok"], 1)
            by_head_b = kv_vecs[:, 0, :].rearrange("p (h d) -> p h d", d=HC)
            nc.vector.tensor_reduce(kv_bsum[:, :], by_head_b, AX.X, ALU.add).then_inc(S["kvbg_ok"], 1)
            dve.wait_ge(S["kvg_ok"], 1)
            nc.vector.scalar_tensor_tensor(out=kv_w[:, :].rearrange("p (h d) -> p h d", d=HC),
                                           in0=kv_gsum[:, :].unsqueeze(2).to_broadcast([P, 4 * HEADS, HC]),
                                           scalar=-1.0 / HC, in1=by_head, op0=ALU.mult, op1=ALU.add).then_inc(S["kvw_ok"], 1)
            dve.wait_ge(S["kvbg_ok"], 1)
            nc.vector.scalar_tensor_tensor(out=kv_b[:, :].rearrange("p (h d) -> p h d", d=HC),
                                           in0=kv_bsum[:, :].unsqueeze(2).to_broadcast([P, 4 * HEADS, HC]),
                                           scalar=-1.0 / HC, in1=by_head_b, op0=ALU.mult, op1=ALU.add).then_inc(S["kvb_ok"], 1)
            dve.wait_ge(S["w1h_ok"], 1)
            nc.vector.tensor_tensor(w1_hl[C:P, :, :], w1_nat[C:P, :, :], w1_hl[C:P, :, :].bitcast(F32),
                                    ALU.subtract).then_inc(S["w1l_ok"], 1)
            dve.wait_ge(S["gateh_ok"], 1)
            nc.vector.tensor_tensor(gate_hl[C:P, :], gate_w[C:P, :], gate_hl[C:P, :].bitcast(F32),
                                    ALU.subtract).then_inc(S["gatel_ok"], 1)
            for h in range(PAIRS):
                dve.wait_ge(S["tanh_ok"], h + 1)
                dve.wait_ge(S["a_ok"], h + 1)
                nc.vector.scalar_tensor_tensor(out=u_sb[:, h, :, W:W + L], in0=tanh_g[:, h, :, :], scalar=1.0,
                                               in1=a_sb[:, h, :, :], op0=ALU.add, op1=ALU.mult).then_inc(S["u_ok"], 1)
            for h in range(PAIRS):
                for k in range(2):
                    i = 2 * h + k + 1
                    dve.wait_ge(S["dirs_ok"], i)
                    nc.vector.tensor_scalar(dirs_fin[:, h, k, :], dirs[:, h, k, :], 0.0, 0.0, ALU.mult,
                                            ALU.is_equal).then_inc(S["dirsfin_ok"], 1)
                    dve.wait_ge(S["dpos_ok"], i)
                    dve.wait_ge(S["dneg_ok"], i)
                    nc.vector.tensor_tensor(dirs_pos[:, h, k, :], dirs_pos[:, h, k, :], dirs_neg[:, h, k, :],
                                            ALU.add).then_inc(S["dsum_ok"], 1)
                    dve.wait_ge(S["dsum_ok"], i)
                    dve.wait_ge(S["dirsfin_ok"], i)
                    nc.vector.copy_predicated(dirs_pos[:, h, k, :], dirs_fin[:, h, k, :],
                                              dirs[:, h, k, :]).then_inc(S["dclean_ok"], 1)
                dve.wait_ge(S["dclean_ok"], 2 * h + 2)
                nc.vector.tensor_tensor(dirs_sum[:, h, :], dirs_pos[:, h, 0, :], dirs_pos[:, h, 1, :],
                                        ALU.add).then_inc(S["dall_ok"], 1)
            for h in range(PAIRS):
                dve.wait_ge(S["o_ok"], h + 1)
                nc.vector.tensor_scalar(o_fin[:, h, :], o_sb[:, h, :], 0.0, 0.0, ALU.mult,
                                        ALU.is_equal).then_inc(S["ofin_ok"], 1)
                dve.wait_ge(S["opos_ok"], h + 1)
                dve.wait_ge(S["oneg_ok"], h + 1)
                nc.vector.tensor_tensor(o_pos[:, h, :], o_pos[:, h, :], o_neg[:, h, :], ALU.add).then_inc(S["osum_ok"], 1)
                dve.wait_ge(S["osum_ok"], h + 1)
                dve.wait_ge(S["ofin_ok"], h + 1)
                nc.vector.copy_predicated(o_pos[:, h, :], o_fin[:, h, :], o_sb[:, h, :])\
                    .then_inc(S["oclean_ok"], 1)
                dve.wait_ge(S["oclean_ok"], h + 1)
                nc.vector.tensor_tensor(x1[:, h, :], o_pos[:, h, :], x_sb[:, h, :], ALU.add).then_inc(S["x1_ok"], 1)
            for h in range(PAIRS):
                stats(2, h)
            for h in range(PAIRS):
                normalise(2, h)
            for h in range(PAIRS):
                dve.wait_ge(S["kv_ps"], h + 1)
                dve.wait_ge(S["kvb_ok"], 1)
                nc.vector.tensor_tensor(kv[:, h, :, :], psA[:, h, :].rearrange("p (t n) -> p t n", t=T),
                                        kv_b[:, :].unsqueeze(1).to_broadcast([P, T, 2 * P]), ALU.add).then_inc(S["kv_ok"], 1)
            for h in range(PAIRS):
                dve.wait_ge(S["kvsq_ok"], h + 1)
                nc.vector.tensor_reduce(ss[:, h, :], kv_sq[:, h, :, :].rearrange("p t (h d) -> p (t h) d", d=HC),
                                        AX.X, ALU.add).then_inc(S["ss_ok"], 1)
            for h in range(PAIRS):
                dve.wait_ge(S["std_ok"], h + 1)
                nc.vector.tensor_scalar(std_eps[:, h, :], std[:, h, :], STD_EPS_HEAD, None, ALU.add).then_inc(S["stde_ok"], 1)
                dve.wait_ge(S["stde_ok"], h + 1)
                nc.vector.reciprocal(rinv[:, h, :], std_eps[:, h, :]).then_inc(S["rinv_ok"], 1)
                dve.wait_ge(S["rinv_ok"], h + 1)
                nc.vector.tensor_tensor(kv_n[:, h, :, :].rearrange("p t (h d) -> p (t h) d", d=HC),
                                        kv[:, h, :, :].rearrange("p t (h d) -> p (t h) d", d=HC),
                                        rinv[:, h, :].unsqueeze(2).to_broadcast([P, T * 4 * HEADS, HC]),
                                        ALU.mult).then_inc(S["kvn_ok"], 1)
            for h in range(PAIRS):
                dve.wait_ge(S["heads_ps"], h + 1)
                dve.wait_ge(S["mask_ok"], 1)
                nc.vector.tensor_tensor(heads[:, h, :], psB[:, h, 0:P], head_mask[:, :], ALU.mult).then_inc(S["heads_ok"], 1)
            for h in range(PAIRS):
                dve.wait_ge(S["yq_ps"], h + 1)
                dve.wait_ge(S["aug_ok"], 2)
                nc.vector.tensor_tensor(yq[:, h, :], psB[:, h, P:2 * P + 1], ident_aug[:, :], ALU.add).then_inc(S["yq_ok"], 1)
            for h in range(PAIRS):
                dve.wait_ge(S["gelu_ok"], h + 1)
                dve.wait_ge(S["x1xa_ok"], h + 1)
                nc.vector.tensor_tensor(t2[:, h, :], gelu_p[:, h, :], x1_xa[:, h, :], ALU.add).then_inc(S["t2_ok"], 1)
            for h in range(PAIRS):
                stats(3, h)
            step = [0]

            def after(k):
                dve.wait_ge(S["newton"], k)

            def done(ins):
                ins.then_inc(S["newton"], 1)
                step[0] += 1

            for h in range(PAIRS):
                dve.wait_ge(S["t_mv"], 3 * PAIRS + h + 1)
                done(nc.vector.tensor_scalar(ve[:, h, :], mv[:, h, :, 1], LN_EPS_TOKEN, None, ALU.add))
            for h in range(PAIRS):
                after(h + 1)
                done(nc.vector.tensor_scalar(guess[:, h, 0, :].bitcast(I32), ve[:, h, :].bitcast(I32), 1, None,
                                             ALU.arith_shift_right))
                nc.vector.tensor_scalar(nhv[:, h, :], ve[:, h, :], -0.5, None, ALU.mult)
            for h in range(PAIRS):
                after(PAIRS + h + 1)
                done(nc.vector.tensor_scalar(guess[:, h, 0, :].bitcast(I32), guess[:, h, 0, :].bitcast(I32), -1.0,
                                             float(RSQRT_MAGIC), ALU.mult, ALU.add))
            for i in range(3):
                for k in range(3):
                    for h in range(PAIRS):
                        after(PAIRS * (2 + 3 * i + k) + h + 1)
                        y0, y1 = guess[:, h, i, :], guess[:, h, i + 1, :]
                        if k == 0:
                            done(nc.vector.tensor_tensor(sq[:, h, 0, :], y0, y0, ALU.mult))
                        elif k == 1:
                            done(nc.vector.tensor_tensor(sq[:, h, 1, :], sq[:, h, 0, :], nhv[:, h, :], ALU.mult))
                        else:
                            done(nc.vector.scalar_tensor_tensor(out=y1, in0=sq[:, h, 1, :], scalar=1.5, in1=y0,
                                                                op0=ALU.add, op1=ALU.mult))
            for h in range(PAIRS):
                after(PAIRS * 11 + h + 1)
                normalise(3, h, guess[:, h, 3, :])
            for h in range(PAIRS):
                dve.wait_ge(S["xh_ok"], h + 1)
                nc.vector.tensor_tensor(xl[:, h, :], psT[:, h, :], xh[:, h, :].bitcast(F32), ALU.subtract)\
                    .then_inc(S["xl_ok"], 1)

            gate = [0]

            def chain(ins):
                ins.then_inc(S["gate_chain"], 1)
                gate[0] += 1
                dve.wait_ge(S["gate_chain"], gate[0])

            def over_e(ap):
                return ap.unsqueeze(2).to_broadcast([P, 4, E])

            def gates(h):
                dve.wait_ge(S["lg_ps"], h + 1)
                dve.wait_ge(S["gate_in"], 48)
                dve.wait_ge(S["rev_ok"], 1)
                rev = rev8[:, :].unsqueeze(1).to_broadcast([P, 4, E])
                chain(nc.vector.tensor_tensor(lg[:, h], psT[:, h, 0:4 * E].rearrange("p (g e) -> p g e", e=E),
                                              gate_b[:, :].unsqueeze(1).to_broadcast([P, 4, E]), ALU.add))
                chain(nc.vector.tensor_reduce(m1[:, h], lg[:, h], AX.X, ALU.max))
                chain(nc.vector.tensor_tensor(eq1[:, h], lg[:, h], over_e(m1[:, h]), ALU.is_equal))
                chain(nc.vector.tensor_tensor(pr1[:, h], eq1[:, h], rev, ALU.mult))
                chain(nc.vector.tensor_reduce(i1[:, h], pr1[:, h], AX.X, ALU.max))
                chain(nc.vector.tensor_tensor(f1[:, h], rev, over_e(i1[:, h]), ALU.is_equal))
                chain(nc.vector.scalar_tensor_tensor(out=lg2[:, h], in0=f1[:, h], scalar=-3.0e38, in1=lg[:, h],
                                                     op0=ALU.mult, op1=ALU.add))
                chain(nc.vector.tensor_reduce(m2[:, h], lg2[:, h], AX.X, ALU.max))
                chain(nc.vector.tensor_tensor(eq2[:, h], lg2[:, h], over_e(m2[:, h]), ALU.is_equal))
                chain(nc.vector.tensor_tensor(pr2[:, h], eq2[:, h], rev, ALU.mult))
                chain(nc.vector.tensor_reduce(i2[:, h], pr2[:, h], AX.X, ALU.max))
                chain(nc.vector.tensor_tensor(m12[:, h], m1[:, h], m2[:, h], ALU.add))
                chain(nc.vector.scalar_tensor_tensor(out=ld[:, h], in0=lg[:, h], scalar=2.0, in1=over_e(m12[:, h]),
                                                     op0=ALU.mult, op1=ALU.subtract))
                chain(nc.vector.tensor_tensor(f2[:, h], rev, over_e(i2[:, h]), ALU.is_equal))
                chain(nc.vector.tensor_tensor(sel[:, h], f1[:, h], f2[:, h], ALU.add))
                dve.wait_ge(S["th_ok"], h + 1)
                chain(nc.vector.scalar_tensor_tensor(out=wg2[:, h], in0=th[:, h], scalar=1.0, in1=sel[:, h],
                                                     op0=ALU.add, op1=ALU.mult))
                chain(nc.vector.tensor_scalar(wg[:, h], wg2[:, h], 0.5, None, ALU.mult))

                def part(i):
                    return w3[:, h, :, i, :, :].rearrange("p t q e -> p q t e")

                def qt(ap):
                    return ap.rearrange("p (q t) e -> p q t e", q=2)
                chain(nc.vector.tensor_copy(part(0), qt(wg[:, h])))
                chain(nc.vector.tensor_tensor(qt(wr1[:, h]), qt(wg[:, h]), part(0), ALU.subtract))
                chain(nc.vector.tensor_copy(part(1), qt(wr1[:, h])))
                chain(nc.vector.tensor_tensor(qt(wr2[:, h]), qt(wr1[:, h]), part(1), ALU.subtract))
                nc.vector.tensor_copy(part(2), qt(wr2[:, h])).then_inc(S["w3_ok"], 1)

            for h in range(PAIRS):
                gates(h)
                dve.wait_ge(S["w3T_ps"], h + 1)
                nc.vector.tensor_copy(w3T[:, h, :], psT[0:6 * E, h, 256:384].bitcast(BF16)).then_inc(S["w3T_ok"], 1)
                for i in range(E // 2):
                    dve.wait_ge(S["wbc_ps"], 4 * h + i + 1)
                    nc.vector.tensor_copy(wbc[:, h, 2 * i:2 * i + 2, :], per_q(psT[:, h, :])).then_inc(S["wbc_ok"], 1)
                    for g in range(2):
                        e = 2 * i + g
                        n = E * h + e
                        dve.wait_ge(S["e_ps"], E * h + 2 * i + 2)
                        dve.wait_ge(S["wbc_ok"], 4 * h + i + 1)
                        if n >= 4:
                            dve.wait_ge(S["acc_ok"], n // 2 - 1)
                        nc.vector.scalar_tensor_tensor(out=prod[:, n // 2 % 2, g, :], in0=psM[:, n // 2 % 2, g * L:(g + 1) * L],
                                                       scalar=cols(V_B2 + e), in1=wbc[:, h, e, :],
                                                       op0=ALU.add, op1=ALU.mult).then_inc(S["prod_ok"], 1)
                dve.wait_ge(S["acc_ok"], E // 2 * (h + 1))
                nc.vector.tensor_tensor(fin[:, h, :], acc[:, h, 0, :], acc[:, h, 1, :], ALU.add).then_inc(S["fin_ok"], 1)


_INS = ['x', 'L0_conv_ln2d_w', 'L0_conv_ln2d_b', 'L0_conv_inproj_w', 'L0_conv_inproj_b', 'L0_conv_dw2d_w',
        'L0_conv_dw2d_b', 'L0_conv_ssm_ln_w', 'L0_conv_ssm_ln_b', 'L0_conv_ssm_in_w', 'L0_conv_ssm_in_b',
        'L0_conv_ssm_dw_w', 'L0_conv_ssm_dw_b', 'L0_conv_ssm_out_w', 'L0_conv_ssm_out_b', 'L0_conv_outproj_w',
        'L0_conv_outproj_b', 'L1_attn_W_qkv', 'L1_attn_b_qkv', 'L1_attn_kln_w', 'L1_attn_kln_b', 'L1_attn_vln_w',
        'L1_attn_vln_b', 'L1_attn_W_proj', 'L1_attn_b_proj', 'L1_ffn_Wg', 'L1_ffn_bg', 'L1_ffn_W1', 'L1_ffn_b1',
        'L1_ffn_W2', 'L1_ffn_b2']


def kernel(**inputs):
    import numpy as _np
    import concourse.bacc as _bacc
    from concourse import mybir as _mybir
    from concourse.bass_utils import run_bass_kernel_spmd as _run

    nc = _bacc.Bacc("TRN2", target_bir_lowering=False, num_devices=1)
    arrays, aps = {}, {}
    for name in _INS:
        v = _np.ascontiguousarray(inputs[name])
        arrays[f"in_{name}_dram"] = v
        aps[name] = nc.dram_tensor(f"in_{name}_dram", v.shape, _mybir.dt.from_np(v.dtype), kind="ExternalInput").ap()
    x = arrays["in_x_dram"]
    out = nc.dram_tensor("out_0_dram", x.shape, _mybir.dt.from_np(x.dtype), kind="ExternalOutput").ap()
    conv_attention_moe(nc, aps, out)
    r = _run(nc, [arrays], core_ids=[0])
    return r.results[0]["out_0_dram"]
```

```python
from contextlib import ExitStack

import concourse.bass as bass
from concourse import mybir

F32 = mybir.dt.float32
F32R = mybir.dt.float32r
BF16 = mybir.dt.bfloat16
I32 = mybir.dt.int32
ALU = mybir.AluOpType
ACT = mybir.ActivationFunctionType
AX = mybir.AxisListType

LN_EPS_CONV = 1e-6
LN_EPS_TOKEN = 1e-5
STD_EPS_HEAD = 1e-5
TINY_VARIANCE = 1e-19
CLAMP = 1e4
RSQRT_MAGIC = 0x5F3759DF

OUTPUTS_AFTER = {1: (0,), 2: (1,), 3: (2,), 4: (3,), 8: (4,), 9: (5, 6), 10: (7,), 11: (8,), 12: (9,), 13: (10,),
                 14: (11,), 15: (12, 13, 14, 15)}
ROWS_AFTER_HIDDEN = 5
SPREADS_AFTER_HIDDEN = {6: (0, 1)}
SPREADS_AFTER_OUTPUT = {4: (2,), 5: (3,), 7: (4,), 9: (5,), 11: (6,), 12: (7,)}
RING = 12
TANH_AFTER = 7


def output_slot(n):
    return (n // 2 % 2, n % 2 * 256) if n < 14 else (15 - n, 0)


(V_LN0_W, V_LN0_B, V_IN_B, V_CONV_B, V_LN1_W, V_LN1_B, V_SSM_A_B, V_SSM_G_B, V_SSM_DW_B, V_SSM_OUT_B,
 V_OUT_B, V_Q_B, V_PROJ_B, V_KLN_W, V_KLN_B, V_SSM_DW) = range(16)
V_CONV = V_SSM_DW + 3
V_B1 = V_CONV + 9
PE_TAPS = (0, 1, 2, 3, 4)


def conv_attention_moe(nc: bass.Bass, a: dict, shapes: dict, out: bass.AP):
    B, C, H, W = shapes["x"]
    L = H * W
    P = 128
    PAIRS = B // 2
    T = L // P
    HID = shapes["L0_conv_ssm_in_w"][0] // 2
    HEADS, _, HC = shapes["L1_attn_kln_w"]
    E, _, FH = shapes["L1_ffn_W1"]
    CK = FH // P
    V_B2 = V_B1 + E * CK
    NVEC = V_B2 + E
    PADW = W + 2
    PH = L + 2 * W
    assert 2 * C == P and HID == P and H == W and T == 2 and PAIRS == 2 and 2 * L == 512

    with ExitStack() as ctx:
        def sb(name, shape, dt=F32):
            return ctx.enter_context(nc.sbuf_tensor(name, shape, dt))

        def ps(name, shape, dt=F32):
            return ctx.enter_context(nc.psum_tensor(name, shape, dt))

        def sem(name):
            return ctx.enter_context(nc.semaphore(name))

        psT = ps("psT", [P, PAIRS, 512])
        psM = ps("psM", [P, PAIRS, 512])
        psA = ps("psA", [P, PAIRS, 512])
        psB = ps("psB", [P, PAIRS, 512])

        x_tok = sb("x_tok", [P, PAIRS, T, P])
        early = sb("early", [P, P + NVEC])
        ssm_in = sb("ssm_in", [P, 5, P])
        DW = 9 * P + C + 2 * E
        late = sb("late", [P, DW])
        x_sb = sb("x_sb", [P, PAIRS, L])
        w1_nat = sb("w1_nat", [P, E, FH])
        w2_sb = sb("w2_sb", [P, E * CK, C])
        in_raw = early[:, 0:P]
        vec = early[:, P:P + NVEC]
        sout_raw = ssm_in[:, 4, :]
        outproj_w = late[:, 0:P]
        kvT = late[:, P:3 * P]
        q_w = late[:, 3 * P:4 * P]
        proj_w = late[:, 4 * P:5 * P]
        outproj_dup = late[:, 5 * P:5 * P + C]
        kv_bias = late[:, 5 * P + C:7 * P + C]
        vln_w = late[:, 7 * P + C:8 * P + C]
        vln_b = late[:, 8 * P + C:9 * P + C]
        v_end = 9 * P + C
        gate_w = late[:, v_end:v_end + E]
        gate_b = late[:, v_end + E:v_end + 2 * E]

        ident = sb("ident", [P, P])
        ident_bf = sb("ident_bf", [P, P], BF16)
        pick3 = sb("pick3", [3 * 2 * E, 2 * E], BF16)
        pick_q = sb("pick_q", [3 * 2 * E, E, 2, C], BF16)
        ones = sb("ones", [P, P])
        head_mask = sb("head_mask", [P, P])
        conv_diag = sb("conv_diag", [P, len(PE_TAPS), P])
        ln_kv = sb("ln_kv", [P, P])
        ln_v = sb("ln_v", [P, P])
        ln_vb = sb("ln_vb", [P, P])
        ln_kbv = sb("ln_kbv", [P, P])
        kln_bL = sb("kln_bL", [P, 1])
        out_b = sb("out_b", [P, 1])
        sout_b0 = sb("sout_b0", [P, 1])
        rev8 = sb("rev8", [P, E])
        in_w = sb("in_w", [P, P])
        in_b = sb("in_b", [P, 1])
        ssm_w = sb("ssm_w", [P, 2, 2, P])
        ssm_b = sb("ssm_b", [P, 2])
        half_g_b = sb("half_g_b", [P, 1])
        half_dw = sb("half_dw", [P, 3])
        sout_w = sb("sout_w", [P, 3, P])
        sout_b = sb("sout_b", [P, 1])
        outproj_q = sb("outproj_q", [P, C])
        kv_gsum = sb("kv_gsum", [P, 4 * HEADS])
        kv_bsum = sb("kv_bsum", [P, 4 * HEADS])
        kv_w = sb("kv_w", [P, 2 * P])
        kv_b = sb("kv_b", [P, 2 * P])
        w1_hl = sb("w1_hl", [P, E, FH], F32R)
        gate_hl = sb("gate_hl", [P, E], F32R)

        st = sb("st", [P, PAIRS, 4, 6])
        mv = sb("mv", [P, PAIRS, 4, 2])
        lnv = sb("lnv", [P, PAIRS, 4])
        rstd = sb("rstd", [P, PAIRS, 4])
        norm_t = sb("norm_t", [P, PAIRS, T, P])
        norm_d = sb("norm_d", [P, PAIRS, 2 * T, 2, C])
        norm_c = sb("norm_c", [P, PAIRS, L])
        zpad = sb("zpad", [P, PAIRS, H + 2, PADW])
        y_sb = sb("y_sb", [P, PAIRS, L])
        tanh_g = sb("tanh_g", [P, PAIRS, 2, L])
        a_sb = sb("a_sb", [P, PAIRS, 2, L])
        u_sb = sb("u_sb", [P, PAIRS, 2, PH])
        dirs = sb("dirs", [P, PAIRS, 2, 2 * L])
        dirs_sign = sb("dirs_sign", [P, PAIRS, 2, 2 * L])
        dirs_bad = sb("dirs_bad", [P, PAIRS, 2, 2 * L])
        o_sb = sb("o_sb", [P, PAIRS, L])
        o_sign = sb("o_sign", [P, PAIRS, L])
        o_bad = sb("o_bad", [P, PAIRS, L])
        x1 = sb("x1", [P, PAIRS, L])
        xa_c = sb("xa_c", [P, PAIRS, L])
        x1_xa = sb("x1_xa", [P, PAIRS, L])
        kv = sb("kv", [P, PAIRS, T, 2 * P])
        kv_sq = sb("kv_sq", [P, PAIRS, T, 2 * P])
        ss = sb("ss", [P, PAIRS, T * 4 * HEADS])
        ss_ln = sb("ss_ln", [P, PAIRS, T * 4 * HEADS])
        std = sb("std", [P, PAIRS, T * 4 * HEADS])
        std_ln = sb("std_ln", [P, PAIRS, T * 4 * HEADS])
        rinv = sb("rinv", [P, PAIRS, T * 4 * HEADS])
        kv_n = sb("kv_n", [P, PAIRS, T, 2 * P + 1])
        k_sum = sb("k_sum", [P, PAIRS, 1])
        heads1 = sb("heads1", [P, PAIRS, P])
        heads2 = sb("heads2", [P, PAIRS, P])
        heads3 = sb("heads3", [P, PAIRS, P])
        heads = sb("heads", [P, PAIRS, P])
        yq = sb("yq", [P, PAIRS, P + 1])
        zT = sb("zT", [P, PAIRS, P])
        zb = sb("zb", [P, PAIRS, 1])
        gelu_p = sb("gelu_p", [P, PAIRS, L])
        t2 = sb("t2", [P, PAIRS, L])
        xh = sb("xh", [P, PAIRS, 2 * L], F32R)
        xl = sb("xl", [P, PAIRS, 2 * L], F32R)
        lg = sb("lg", [P, PAIRS, 4, E])
        m1 = sb("m1", [P, PAIRS, 4])
        eq1 = sb("eq1", [P, PAIRS, 4, E])
        pr1 = sb("pr1", [P, PAIRS, 4, E])
        i1 = sb("i1", [P, PAIRS, 4])
        f1 = sb("f1", [P, PAIRS, 4, E])
        lg2 = sb("lg2", [P, PAIRS, 4, E])
        m2 = sb("m2", [P, PAIRS, 4])
        eq2 = sb("eq2", [P, PAIRS, 4, E])
        pr2 = sb("pr2", [P, PAIRS, 4, E])
        i2 = sb("i2", [P, PAIRS, 4])
        f2 = sb("f2", [P, PAIRS, 4, E])
        sel = sb("sel", [P, PAIRS, 4, E])
        m12 = sb("m12", [P, PAIRS, 4])
        ld = sb("ld", [P, PAIRS, 4, E])
        th = sb("th", [P, PAIRS, 4, E])
        wg2 = sb("wg2", [P, PAIRS, 4, E])
        wg = sb("wg", [P, PAIRS, 4, E])
        wr1 = sb("wr1", [P, PAIRS, 4, E])
        wr2 = sb("wr2", [P, PAIRS, 4, E])
        w3 = sb("w3", [P, PAIRS, T, 3, 2, E], BF16)
        w3T = sb("w3T", [3 * 2 * E, PAIRS, L], BF16)
        wbc = sb("wbc", [P, PAIRS, E, L])
        hs = sb("hs", [P, RING, 2 * L])
        prod = sb("prod", [P, 4, L])
        acc = sb("acc", [P, PAIRS, 2, L])
        part_sum = sb("part_sum", [P, 2, L])
        fin = sb("fin", [P, PAIRS, L])

        names = """xt_in early_in ssm_in late_in xp_in w1_in w2_in
            ident0 ident_ok bf_ok zeros_ok pick0 pick_ok pickq_ok mask0 mask1 mask_ok ones_ok rev_ok
            in_w_ok inb_ps in_b_ok diag_ok ssm_w_ok ssmb_ps ssm_b_ok half_g_ok half_dw_ok sout_w_ok sout_b0_ok sout_b_ok
            out_b_ok outq_ok kvg_ok kvw_ok kvbg_ok kvb_ok lnv_ok lnkv_ok w1h_ok w1l_ok gateh_ok gatel_ok
            tT_ps t_stats t_mv t_lnv t_rstd t_norm cT_ps c_norm
            z_ps z_ok taps conv_ps y_ok ag_ps tanh_ok a_ok u_ok u_left u_right dirs_ps dirs_ok dsign_ok dbad_ok dlim_ok
            dclean_ok out_ps o_ok osign_ok obad_ok olim_ok oclean_ok x1_ok x1xa_ok
            kv_ps kv_ok kvsq_ok ss_ok ssln_ok std_ok stdln_ok rinv_ok kvn_ok heads_ps ksum_ok h1_ok h2_ok h3_ok heads_ok
            yq_ps yq_ok zT_ps zT_ok zb_ok p_ps gelu_ok t2_ok xdup_ps xh_ok xl_ok
            lg_ps lg_ok gate_chain m12_ok ld_ok part_ok th_ok w3_ok w3T_ps w3T_ok wbc_ps wbc_ok
            h_ps h_ok e_ps prod_ok acc_ok psum_ok fin_ok out_done""".split()
        S = {n: sem(n) for n in names}

        def per_q(ap):
            return ap.rearrange("p (q l) -> p q l", q=2)

        def cols(i, n=1):
            return vec[:, i:i + n]

        def normed(n, h, t):
            return T * (PAIRS * n + h) + t + 1

        def to_tok(n, h):
            return PAIRS * (n - 1) + h + 1

        block = ctx.enter_context(nc.Block())
        out_pairs = out.rearrange("(h q) c y x -> h (q c) (y x)", q=2)

        @block.sync
        def _(sp):
            for h in range(PAIRS):
                sp.dma_start(x_tok[:, h, :, :], a["x_tok"][:, h]).then_inc(S["xt_in"], 16)
            sp.dma_start(ssm_in[:, :, :], a["ssm"]).then_inc(S["ssm_in"], 16)
            sp.dma_start(late[:, :], a["late"]).then_inc(S["late_in"], 16)
            sp.dma_start(w1_nat[:, :, :], a["w1"]).then_inc(S["w1_in"], 16)
            sp.dma_start(x_sb[:, :, :], a["x_chan"]).then_inc(S["xp_in"], 16)
            sp.dma_start(w2_sb[:, :, :], a["w2"]).then_inc(S["w2_in"], 16)
            for h in range(PAIRS):
                sp.wait_ge(S["fin_ok"], h + 1)
                sp.dma_start(out_pairs[h], fin[:, h, :]).then_inc(S["out_done"], 16)
            sp.wait_ge(S["out_done"], 16 * PAIRS)

        @block.gpsimd
        def _(pool):
            nc.gpsimd.memset(ident[:, :], 0.0).then_inc(S["ident0"], 1)
            pool.wait_ge(S["ident0"], 1)
            nc.gpsimd.affine_select(out=ident[:, :], in_=ident[:, :], compare_op=ALU.not_equal, fill=1.0, base=0,
                                    pattern=[[-1, P]], channel_multiplier=1).then_inc(S["ident_ok"], 1)
            nc.gpsimd.memset(zpad[:, :, :, :], 0.0).then_inc(S["zeros_ok"], 1)
            nc.gpsimd.memset(u_sb[:, :, :, 0:1], 0.0).then_inc(S["zeros_ok"], 1)
            nc.gpsimd.memset(u_sb[:, :, :, PH - 1:PH], 0.0).then_inc(S["zeros_ok"], 1)
            nc.gpsimd.memset(ones[:, :], 1.0).then_inc(S["ones_ok"], 1)
            nc.gpsimd.memset(kv_n[:, :, :, 2 * P:2 * P + 1], 1.0).then_inc(S["ones_ok"], 1)
            nc.gpsimd.iota(rev8[:, :], pattern=[[-1, E]], base=E, channel_multiplier=0,
                           allow_small_or_imprecise_dtypes=True).then_inc(S["rev_ok"], 1)
            hm = head_mask[:, :].rearrange("p (g d) -> p g d", d=HC)
            nc.gpsimd.memset(head_mask[:, :], 1.0 / L).then_inc(S["mask0"], 1)
            pool.wait_ge(S["mask0"], 1)
            nc.gpsimd.affine_select(out=hm, in_=hm, compare_op=ALU.is_ge, fill=0.0, base=0,
                                    pattern=[[-HC, P // HC], [0, HC]], channel_multiplier=1).then_inc(S["mask1"], 1)
            pool.wait_ge(S["mask1"], 1)
            nc.gpsimd.affine_select(out=hm, in_=hm, compare_op=ALU.is_ge, fill=0.0, base=HC - 1,
                                    pattern=[[HC, P // HC], [0, HC]], channel_multiplier=-1).then_inc(S["mask_ok"], 1)
            nc.gpsimd.memset(pick3[:, :], 0.0).then_inc(S["pick0"], 1)
            for j in range(3):
                pool.wait_ge(S["pick0"], j + 1)
                nc.gpsimd.affine_select(out=pick3[:, :], in_=pick3[:, :], compare_op=ALU.not_equal, fill=1.0,
                                        base=-2 * E * j, pattern=[[-1, 2 * E]],
                                        channel_multiplier=1).then_inc(S["pick0" if j < 2 else "pick_ok"], 1)
            pool.wait_ge(S["pick_ok"], 1)
            spread = pick3[:, :].rearrange("r (q e) -> r e q", q=2)
            for q in range(2):
                nc.gpsimd.tensor_copy(pick_q[:, :, q, :], spread[:, :, q:q + 1].to_broadcast([6 * E, E, C]))\
                    .then_inc(S["pickq_ok"], 1)
            pool.wait_ge(S["ident_ok"], 1)
            nc.gpsimd.tensor_copy(ident_bf[:, :], ident[:, :]).then_inc(S["bf_ok"], 1)

            for h in range(PAIRS):
                pool.wait_ge(S["u_ok"], h + 1)
                pool.wait_ge(S["zeros_ok"], 3)
                nc.gpsimd.tensor_copy(u_sb[:, h, :, 1:W], u_sb[:, h, :, L:L + W - 1]).then_inc(S["u_left"], 1)
                nc.gpsimd.tensor_copy(u_sb[:, h, :, L + W:L + 2 * W - 1],
                                      u_sb[:, h, :, W + 1:2 * W]).then_inc(S["u_right"], 1)
            for h in range(PAIRS):
                for k in range(2):
                    pool.wait_ge(S["dirs_ok"], 2 * h + k + 1)
                    nc.gpsimd.tensor_scalar(dirs_bad[:, h, k, :], dirs[:, h, k, :], 0.0, 0.0, ALU.mult, ALU.add)\
                        .then_inc(S["dbad_ok"], 1)
            for h in range(PAIRS):
                pool.wait_ge(S["o_ok"], h + 1)
                nc.gpsimd.tensor_scalar(o_bad[:, h, :], o_sb[:, h, :], 0.0, 0.0, ALU.mult, ALU.add)\
                    .then_inc(S["obad_ok"], 1)
            pool.wait_ge(S["w1h_ok"], 1)
            pool.wait_ge(S["obad_ok"], PAIRS)
            nc.gpsimd.tensor_tensor(w1_hl[C:P, :, :], w1_nat[C:P, :, :], w1_hl[C:P, :, :].bitcast(F32),
                                    ALU.subtract).then_inc(S["w1l_ok"], 1)
            pool.wait_ge(S["w1l_ok"], 1)
            for h in range(PAIRS):
                pool.wait_ge(S["x1_ok"], h + 1)
                pool.wait_ge(S["c_norm"], 2 * PAIRS + h + 1)
                nc.gpsimd.tensor_tensor(x1_xa[:, h, :], x1[:, h, :], xa_c[:, h, :], ALU.add).then_inc(S["x1xa_ok"], 1)
            for i in range(PAIRS * E // 2 - 1):
                h = i // (E // 2)
                pool.wait_ge(S["prod_ok"], 2 * i + 2)
                if i % (E // 2) == 0:
                    pool.wait_ge(S["t2_ok"], h + 1)
                    nc.gpsimd.tensor_tensor(acc[:, h, 0, :], t2[:, h, :], prod[:, 0, :], ALU.add).then_inc(S["acc_ok"], 1)
                    nc.gpsimd.tensor_copy(acc[:, h, 1, :], prod[:, 1, :]).then_inc(S["acc_ok"], 1)
                else:
                    pool.wait_ge(S["acc_ok"], 2 * i)
                    nc.gpsimd.tensor_tensor(acc[:, h, :, :], acc[:, h, :, :], prod[:, 2 * i % 4:2 * i % 4 + 2, :],
                                            ALU.add).then_inc(S["acc_ok"], 2)

        @block.scalar
        def _(act):
            act.dma_start(early[:, :], a["early"]).then_inc(S["early_in"], 16)
            nc.scalar.preload_act_table_set("natural_log_exp_and_others")

            def rsqrt(n, h, eps):
                act.wait_ge(S["t_mv"], PAIRS * n + h + 1)
                nc.scalar.activation(lnv[:, h, :], mv[:, h, :, 1], ACT.Ln, bias=eps).then_inc(S["t_lnv"], 1)
                act.wait_ge(S["t_lnv"], PAIRS * n + h + 1)
                nc.scalar.activation(rstd[:, h, :], lnv[:, h, :], ACT.Exp, scale=-0.5).then_inc(S["t_rstd"], 1)

            def norm_out(n, h, dst):
                act.wait_ge(S["cT_ps"], PAIRS * n + h + 1)
                nc.scalar.copy(dst[:, h, :], psM[:, h, L:2 * L]).then_inc(S["c_norm"], 1)

            def conv_diagonal(i):
                nc.scalar.activation(conv_diag[:, i, :], ident[:, :], ACT.Copy, scale=cols(V_CONV + PE_TAPS[i]))\
                    .then_inc(S["diag_ok"], 1)

            act.wait_ge(S["early_in"], 16)
            nc.scalar.activation(in_w[:, :], in_raw, ACT.Copy, scale=cols(V_LN0_W)).then_inc(S["in_w_ok"], 1)
            for h in range(PAIRS):
                rsqrt(0, h, LN_EPS_CONV)
            act.wait_ge(S["inb_ps"], 1)
            nc.scalar.activation(in_b[:, :], psB[:, 0, 0:1], ACT.Identity, bias=cols(V_IN_B)).then_inc(S["in_b_ok"], 1)
            act.wait_ge(S["ident_ok"], 1)
            for i in range(2):
                conv_diagonal(i)
            for h in range(PAIRS):
                norm_out(0, h, norm_c)
            for h in range(PAIRS):
                act.wait_ge(S["z_ps"], h + 1)
                act.wait_ge(S["zeros_ok"], 1)
                act.wait_ge(S["in_b_ok"], 1)
                nc.scalar.activation(zpad[:, h, 1:H + 1, 1:W + 1], psM[:, h, 0:L].rearrange("p (y x) -> p y x", x=W),
                                     ACT.Identity, bias=in_b[:, 0:1]).then_inc(S["z_ok"], 1)
            for i in range(2, len(PE_TAPS)):
                conv_diagonal(i)

            act.wait_ge(S["ssm_in"], 16)
            nc.scalar.activation(ssm_w[:, :, :, :].rearrange("p g q o -> p (g q) o"), ssm_in[:, 0:4, :], ACT.Copy,
                                 scale=cols(V_LN1_W)).then_inc(S["ssm_w_ok"], 1)
            nc.scalar.mul(half_dw[:, :], cols(V_SSM_DW, 3), 0.5).then_inc(S["half_dw_ok"], 1)
            act.wait_ge(S["ssmb_ps"], 2)
            nc.scalar.activation(ssm_b[:, 0:1], psB[:, 1, 0:1], ACT.Identity, bias=cols(V_SSM_A_B)).then_inc(S["ssm_b_ok"], 1)
            nc.scalar.activation(ssm_b[:, 1:2], psB[:, 1, 1:2], ACT.Identity, bias=cols(V_SSM_G_B)).then_inc(S["ssm_b_ok"], 1)
            nc.scalar.activation(sout_b0[:, :], psB[:, 1, 2:3], ACT.Identity, bias=cols(V_SSM_OUT_B)).then_inc(S["sout_b0_ok"], 1)
            act.wait_ge(S["ssm_b_ok"], 2)
            nc.scalar.mul(half_g_b[:, :], ssm_b[:, 1:2], 0.5).then_inc(S["half_g_ok"], 1)
            act.wait_ge(S["sout_b0_ok"], 1)
            nc.scalar.mul(sout_b[:, :], sout_b0[:, :], 1.0 / CLAMP).then_inc(S["sout_b_ok"], 1)
            nc.scalar.mul(out_b[:, :], cols(V_OUT_B), 1.0 / CLAMP).then_inc(S["out_b_ok"], 1)

            for h in range(PAIRS):
                rsqrt(1, h, LN_EPS_CONV)
            nc.scalar.preload_act_table_set("gelu_and_others")
            for h in range(PAIRS):
                norm_out(1, h, norm_c)
            for h in range(PAIRS):
                act.wait_ge(S["ag_ps"], 2 * h + 1)
                act.wait_ge(S["half_g_ok"], 1)
                nc.scalar.activation(tanh_g[:, h, :, :], per_q(psB[:, h, :]), ACT.Tanh, bias=half_g_b[:, 0:1],
                                     scale=0.5).then_inc(S["tanh_ok"], 1)
                if h == 0:
                    act.wait_ge(S["half_dw_ok"], 1)
                    for tap, (fwd, bwd) in ((1, (1, 1)), (0, (0, 2)), (2, (2, 0))):
                        for d, k in enumerate((fwd, bwd)):
                            nc.scalar.activation(sout_w[:, tap, d * C:(d + 1) * C], sout_raw[:, d * C:(d + 1) * C],
                                                 ACT.Copy, scale=half_dw[:, k:k + 1]).then_inc(S["sout_w_ok"], 1)
            nc.scalar.preload_act_table_set("natural_log_exp_and_others")
            act.wait_ge(S["w1_in"], 16)
            nc.scalar.copy(w1_hl[:, :, :], w1_nat[:, :, :]).then_inc(S["w1h_ok"], 1)
            act.wait_ge(S["late_in"], 16)
            nc.scalar.copy(gate_hl[:, :], gate_w).then_inc(S["gateh_ok"], 1)
            for h in range(PAIRS):
                for k, bank in enumerate((psA, psB)):
                    act.wait_ge(S["dirs_ps"], 2 * h + k + 1)
                    act.wait_ge(S["sout_b_ok"], 1)
                    nc.scalar.activation(dirs[:, h, k, :], bank[:, h, :], ACT.Identity, bias=sout_b[:, 0:1],
                                         scale=1.0 / CLAMP).then_inc(S["dirs_ok"], 1)
                    nc.scalar.activation(dirs_sign[:, h, k, :], bank[:, h, :], ACT.Sign, bias=sout_b[:, 0:1],
                                         scale=1.0 / CLAMP).then_inc(S["dsign_ok"], 1)
            for h in range(PAIRS):
                act.wait_ge(S["out_ps"], h + 1)
                act.wait_ge(S["out_b_ok"], 1)
                nc.scalar.activation(o_sb[:, h, :], psM[:, h, 0:L], ACT.Identity, bias=out_b[:, 0:1],
                                     scale=1.0 / CLAMP).then_inc(S["o_ok"], 1)
                nc.scalar.activation(o_sign[:, h, :], psM[:, h, 0:L], ACT.Sign, bias=out_b[:, 0:1],
                                     scale=1.0 / CLAMP).then_inc(S["osign_ok"], 1)
            for h in range(PAIRS):
                rsqrt(2, h, LN_EPS_TOKEN)
            for h in range(PAIRS):
                norm_out(2, h, xa_c)
            for h in range(PAIRS):
                act.wait_ge(S["kv_ok"], h + 1)
                nc.scalar.activation(kv_sq[:, h, :, :], kv[:, h, :, :], ACT.Square).then_inc(S["kvsq_ok"], 1)
            for h in range(PAIRS):
                act.wait_ge(S["ss_ok"], h + 1)
                nc.scalar.activation(ss_ln[:, h, :], ss[:, h, :], ACT.Ln, scale=1.0 / (HC - 1),
                                     bias=TINY_VARIANCE).then_inc(S["ssln_ok"], 1)
                act.wait_ge(S["ssln_ok"], h + 1)
                nc.scalar.activation(std[:, h, :], ss_ln[:, h, :], ACT.Exp, scale=0.5).then_inc(S["std_ok"], 1)
                act.wait_ge(S["std_ok"], h + 1)
                nc.scalar.activation(std_ln[:, h, :], std[:, h, :], ACT.Ln, bias=STD_EPS_HEAD).then_inc(S["stdln_ok"], 1)
                act.wait_ge(S["stdln_ok"], h + 1)
                nc.scalar.activation(rinv[:, h, :], std_ln[:, h, :], ACT.Exp, scale=-1.0).then_inc(S["rinv_ok"], 1)
            nc.scalar.preload_act_table_set("gelu_and_others")
            for h in range(PAIRS):
                act.wait_ge(S["zT_ps"], 2 * h + 2)
                nc.scalar.copy(zT[:, h, :], psT[:, h, 0:P]).then_inc(S["zT_ok"], 1)
                nc.scalar.activation(zb[:, h, :], psT[:, h, P:P + 1], ACT.Identity, bias=cols(V_PROJ_B)).then_inc(S["zb_ok"], 1)
            for h in range(PAIRS):
                act.wait_ge(S["p_ps"], h + 1)
                act.wait_ge(S["zb_ok"], h + 1)
                nc.scalar.activation(gelu_p[:, h, :], psM[:, h, 0:L], ACT.Gelu, bias=zb[:, h, :]).then_inc(S["gelu_ok"], 1)
            nc.scalar.preload_act_table_set("natural_log_exp_and_others")
            for h in range(PAIRS):
                rsqrt(3, h, LN_EPS_TOKEN)
            nc.scalar.preload_act_table_set("gelu_and_others")
            for h in range(PAIRS):
                act.wait_ge(S["xdup_ps"], h + 1)
                nc.scalar.copy(xh[:, h, :], psM[:, h, :]).then_inc(S["xh_ok"], 1)

            for n in range(PAIRS * E * CK):
                act.wait_ge(S["h_ps"], n + 1)
                if n >= RING:
                    act.wait_ge(S["e_ps"], (n - RING) // CK + 1)
                nc.scalar.activation(hs[:, n % RING, :], (psA, psB)[n % 2][:, n // 2 % 2, :], ACT.Gelu,
                                     bias=cols(V_B1 + n % (E * CK))).then_inc(S["h_ok"], 1)
                if n == TANH_AFTER:
                    act.wait_ge(S["ld_ok"], 1)
                    nc.scalar.activation(th[:, :, :, :], ld[:, :, :, :], ACT.Tanh, scale=0.5).then_inc(S["th_ok"], 1)

        @block.tensor
        def _(pe):
            def to_tokens(h, src):
                for t in range(T):
                    m = nc.tensor.transpose(psT[:, h, t * P:(t + 1) * P], src[:, h, t * P:(t + 1) * P], ident[:, :])
                m.then_inc(S["tT_ps"], 1)

            def to_channels(n, h):
                for t in range(T):
                    pe.wait_ge(S["t_norm"], normed(n, h, t))
                    m = nc.tensor.transpose(psM[:, h, L + t * P:L + (t + 1) * P], norm_t[:, h, t, :], ident[:, :])
                m.then_inc(S["cT_ps"], 1)

            def keep_clock(bank, n):
                for _ in range(n):
                    nc.tensor.matmul(bank[:, 0:P], ident[:, :], ident[:, :], start=True, stop=True)

            pe.wait_ge(S["ident_ok"], 1)
            keep_clock(psA[:, 1, :], 5)
            pe.wait_ge(S["early_in"], 16)
            nc.tensor.matmul(psB[:, 0, 0:1], in_raw, cols(V_LN0_B), start=True, stop=True).then_inc(S["inb_ps"], 1)
            keep_clock(psA[:, 1, :], 6)
            for h in range(PAIRS):
                to_channels(0, h)
            for h in range(PAIRS):
                pe.wait_ge(S["c_norm"], h + 1)
                pe.wait_ge(S["in_w_ok"], 1)
                nc.tensor.matmul(psM[:, h, 0:L], in_w[:, :], norm_c[:, h, :], start=True, stop=True).then_inc(S["z_ps"], 1)
            pe.wait_ge(S["ssm_in"], 16)
            for g in range(2):
                m = nc.tensor.matmul(psB[:, 1, g:g + 1], ssm_in[:, 2 * g, :], cols(V_LN1_B), start=True, stop=True)
            m.then_inc(S["ssmb_ps"], 1)
            nc.tensor.matmul(psB[:, 1, 2:3], sout_raw, cols(V_SSM_DW_B), start=True, stop=True).then_inc(S["ssmb_ps"], 1)
            keep_clock(psA[:, 0, :], 2)
            for h in range(PAIRS):
                pe.wait_ge(S["z_ok"], h + 1)
                for i, tap in enumerate(PE_TAPS):
                    dy, dx = divmod(tap, 3)
                    pe.wait_ge(S["diag_ok"], i + 1)
                    m = nc.tensor.matmul(psA[:, h, 0:L].rearrange("p (y x) -> p y x", x=W), conv_diag[:, i, :],
                                         zpad[:, h, dy:dy + H, dx:dx + W], start=(i == 0), stop=(i == len(PE_TAPS) - 1))
                m.then_inc(S["conv_ps"], 1)

            for h in range(PAIRS):
                pe.wait_ge(S["y_ok"], h + 1)
                to_tokens(h, y_sb)
            pe.wait_ge(S["in_b_ok"], 1)
            keep_clock(psB[:, 0, :], 10)
            for h in range(PAIRS):
                to_channels(1, h)
            for h in range(PAIRS):
                pe.wait_ge(S["c_norm"], PAIRS + h + 1)
                pe.wait_ge(S["ssm_w_ok"], 1)
                pe.wait_ge(S["ssm_b_ok"], 2)
                pe.wait_ge(S["sout_b0_ok"], 1)
                for g, bank in ((1, psB), (0, psA)):
                    for q in range(2):
                        m = nc.tensor.matmul(bank[:, h, q * L:(q + 1) * L], ssm_w[:, g, q, :], norm_c[:, h, :],
                                             start=True, stop=True)
                    m.then_inc(S["ag_ps"], 1)
            for h in range(PAIRS):
                pe.wait_ge(S["u_ok"], h + 1)
                mid = u_sb[:, h, :, W:W + L]
                bank = per_q(psA[:, h, :])
                pe.wait_ge(S["sout_w_ok"], 2)
                nc.tensor.matmul(bank, sout_w[:, 1, :], mid, start=True, stop=False)
                pe.wait_ge(S["sout_w_ok"], 4)
                nc.tensor.matmul(bank[:, :, 1:L], sout_w[:, 0, :], u_sb[:, h, :, W:W + L - 1], start=False, stop=False)
                pe.wait_ge(S["sout_w_ok"], 6)
                nc.tensor.matmul(bank[:, :, 0:L - 1], sout_w[:, 2, :], u_sb[:, h, :, W + 1:W + L], start=False,
                                 stop=True).then_inc(S["dirs_ps"], 1)
                bank = per_q(psB[:, h, :])
                nc.tensor.matmul(bank, sout_w[:, 1, :], mid, start=True, stop=False)
                pe.wait_ge(S["u_left"], h + 1)
                nc.tensor.matmul(bank, sout_w[:, 0, :], u_sb[:, h, :, 0:L], start=False, stop=False)
                pe.wait_ge(S["u_right"], h + 1)
                nc.tensor.matmul(bank, sout_w[:, 2, :], u_sb[:, h, :, 2 * W:2 * W + L], start=False,
                                 stop=True).then_inc(S["dirs_ps"], 1)
            for h in range(PAIRS):
                pe.wait_ge(S["late_in"], 16)
                pe.wait_ge(S["outq_ok"], 1)
                nc.tensor.matmul(psM[:, h, 0:L], outproj_w, y_sb[:, h, :], start=True, stop=False)
                for k in range(2):
                    pe.wait_ge(S["dclean_ok"], 2 * h + k + 1)
                    for q in range(2):
                        m = nc.tensor.matmul(psM[q * C:(q + 1) * C, h, 0:L], outproj_q[:, :],
                                             dirs[:, h, k, q * L:(q + 1) * L], start=False, stop=(k == 1))
                m.then_inc(S["out_ps"], 1)
            for h in range(PAIRS):
                pe.wait_ge(S["x1_ok"], h + 1)
                to_tokens(h, x1)
                keep_clock(psA[:, 0, :], (5, 9)[h])
            for h in range(PAIRS):
                to_channels(2, h)
            for h in range(PAIRS):
                pe.wait_ge(S["c_norm"], 2 * PAIRS + h + 1)
                pe.wait_ge(S["kvw_ok"], 1)
                pe.wait_ge(S["dsign_ok"], 2 * h + 1)
                for t in range(T):
                    m = nc.tensor.matmul(psA[:, h, t * 2 * P:(t + 1) * 2 * P], xa_c[:, h, t * P:(t + 1) * P], kv_w[:, :],
                                         start=True, stop=True)
                m.then_inc(S["kv_ps"], 1)
            pe.wait_ge(S["c_norm"], 3 * PAIRS)
            keep_clock(psM[:, 0, :], 14)
            for h in range(PAIRS):
                pe.wait_ge(S["kvn_ok"], h + 1)
                pe.wait_ge(S["ones_ok"], 2)
                pe.wait_ge(S["dsign_ok"], 2 * h + 2)
                for t in range(T):
                    nc.tensor.matmul(psB[:, h, 0:P + 1], kv_n[:, h, t, 0:P], kv_n[:, h, t, P:2 * P + 1],
                                     start=(t == 0), stop=(t == T - 1))
                for t in range(T):
                    m = nc.tensor.matmul(psT[:, h, 0:P], ones[:, :], kv_n[:, h, t, P:2 * P],
                                         start=(t == 0), stop=(t == T - 1))
                m.then_inc(S["heads_ps"], 1)
            for h in range(PAIRS):
                pe.wait_ge(S["heads_ok"], h + 1)
                nc.tensor.matmul(psB[:, h, P:2 * P], heads[:, h, :], q_w, start=True, stop=True)
                nc.tensor.matmul(psB[:, h, 2 * P:2 * P + 1], heads[:, h, :], cols(V_Q_B), start=True,
                                 stop=True).then_inc(S["yq_ps"], 1)
            for h in range(PAIRS):
                pe.wait_ge(S["yq_ok"], 2 * h + 2)
                nc.tensor.matmul(psT[:, h, 0:P], yq[:, h, 0:P], proj_w, start=True, stop=True).then_inc(S["zT_ps"], 1)
                nc.tensor.matmul(psT[:, h, P:P + 1], proj_w, yq[:, h, P:P + 1], start=True,
                                 stop=True).then_inc(S["zT_ps"], 1)
            for h in range(PAIRS):
                pe.wait_ge(S["zT_ok"], h + 1)
                nc.tensor.matmul(psM[:, h, 0:L], zT[:, h, :], xa_c[:, h, :], start=True, stop=True).then_inc(S["p_ps"], 1)
            for h in range(PAIRS):
                pe.wait_ge(S["t2_ok"], h + 1)
                pe.wait_ge(S["zb_ok"], h + 1)
                to_tokens(h, t2)
            keep_clock(psA[:, 0, :], 8)
            for h in range(PAIRS):
                for t in range(T):
                    pe.wait_ge(S["t_norm"], normed(3, h, t))
                    for q in range(2):
                        src = norm_d[:, h, q * T + t, :, :].rearrange("p a c -> p (a c)")
                        m = nc.tensor.transpose(psM[:, h, (q * T + t) * P:(q * T + t + 1) * P], src, ident[:, :])
                m.then_inc(S["xdup_ps"], 1)

            def logits(h):
                pe.wait_ge(S["xh_ok"], h + 1)
                pe.wait_ge(S["xl_ok"], h + 1)
                for g in range(4):
                    for x_part in (xh, xl):
                        m = nc.tensor.matmul(psT[:, h, E * g:E * (g + 1)], x_part[:, h, g * P:(g + 1) * P], gate_hl[:, :],
                                             start=(x_part is xh), stop=(x_part is xl))
                m.then_inc(S["lg_ps"], 1)

            def hidden(n):
                if n >= 4:
                    pe.wait_ge(S["h_ok"], n - 3)
                e, k = divmod(n % (E * CK), CK)
                h = n // (E * CK)
                w = w1_hl[:, e, k * P:(k + 1) * P]
                bank = (psA, psB)[n % 2][:, n // 2 % 2, :]
                nc.tensor.matmul(bank, w, xh[:, h, :], start=True, stop=False)
                nc.tensor.matmul(bank, w, xl[:, h, :], start=False, stop=True).then_inc(S["h_ps"], 1)

            def output(n):
                bank, c0 = output_slot(n)
                if n >= 4 and (n % 2 == 0 or n == 15):
                    pe.wait_ge(S["prod_ok"], 14 if n == 15 else n - 2)
                for k in range(CK):
                    s = CK * n + k
                    pe.wait_ge(S["h_ok"], s + 1)
                    for q in range(2):
                        m = nc.tensor.matmul(psM[q * C:(q + 1) * C, bank, c0:c0 + L], w2_sb[:, s % (E * CK), :],
                                             hs[:, s % RING, q * L:(q + 1) * L], start=(k == 0), stop=(k == CK - 1))
                m.then_inc(S["e_ps"], 1)

            def gate_rows():
                pe.wait_ge(S["w3_ok"], PAIRS)
                pe.wait_ge(S["bf_ok"], 1)
                for h in range(PAIRS):
                    pT = psT[:, h, 256:512].bitcast(BF16)
                    for t in range(T):
                        m = nc.tensor.transpose(pT[0:6 * E, t * P:(t + 1) * P],
                                                w3[:, h, t].rearrange("p i q e -> p (i q e)"), ident_bf[:, :])
                m.then_inc(S["w3T_ps"], 1)

            def spread_gates(i):
                h = i // (E // 2)
                pe.wait_ge(S["w3T_ok"], PAIRS)
                pe.wait_ge(S["pickq_ok"], 2)
                if i >= 2:
                    pe.wait_ge(S["wbc_ok"], i - 1)
                for g in range(2):
                    pick = pick_q[:, 2 * i % E + g, :, :].rearrange("r q c -> r (q c)")
                    m = nc.tensor.matmul(psT[:, i % 2, g * L:(g + 1) * L], pick, w3T[:, h, :], start=True, stop=True)
                m.then_inc(S["wbc_ps"], 1)

            pe.wait_ge(S["w1l_ok"], 1)
            pe.wait_ge(S["gatel_ok"], 1)
            pe.wait_ge(S["w2_in"], 16)
            pe.wait_ge(S["yq_ok"], 2 * PAIRS)
            keep_clock(psA[:, 0, :], 3)
            logits(0)
            for s in range(PAIRS * E):
                for k in range(CK):
                    hidden(CK * s + k)
                if s == 0:
                    logits(1)
                if s == ROWS_AFTER_HIDDEN:
                    gate_rows()
                for i in SPREADS_AFTER_HIDDEN.get(s, ()):
                    spread_gates(i)
                for n in OUTPUTS_AFTER.get(s, ()):
                    output(n)
                    for i in SPREADS_AFTER_OUTPUT.get(n, ()):
                        spread_gates(i)

        @block.vector
        def _(dve):
            def stats(n, h):
                if n:
                    dve.wait_ge(S["tT_ps"], to_tok(n, h))
                    dve.wait_ge(S["t_norm"], normed(n - 1, h, T - 1))
                else:
                    dve.wait_ge(S["xt_in"], 16 * PAIRS)
                for g in range(4):
                    src = psT[:, h, g * C:(g + 1) * C] if n else x_tok[:, h, g // 2, g % 2 * C:(g % 2 + 1) * C]
                    m = nc.vector.bn_stats(st[:, h, g, :], src)
                m.then_inc(S["t_stats"], 1)
                dve.wait_ge(S["t_stats"], PAIRS * n + h + 1)
                for g in range(4):
                    m = nc.vector.bn_aggr(mv[:, h, g, :], st[:, h, g, :])
                m.then_inc(S["t_mv"], 1)

            def normalise(n, h):
                dve.wait_ge(S["t_rstd"], PAIRS * n + h + 1)
                if n:
                    dve.wait_ge(S["cT_ps"], PAIRS * (n - 1) + h + 1)
                for g in range(4):
                    t, q = divmod(g, 2)
                    src = psT[:, h, g * C:(g + 1) * C] if n else x_tok[:, h, t, q * C:(q + 1) * C]
                    if n == 3:
                        dst = norm_d[:, h, q * T + t, :, :]
                        src = src.unsqueeze(1).to_broadcast([P, 2, C])
                    else:
                        dst = norm_t[:, h, t, q * C:(q + 1) * C]
                    m = nc.vector.tensor_scalar(dst, src, mv[:, h, g, 0:1], rstd[:, h, g:g + 1], ALU.subtract, ALU.mult)
                    if q == 1:
                        m.then_inc(S["t_norm"], 1)

            for h in range(PAIRS):
                stats(0, h)
            for h in range(PAIRS):
                normalise(0, h)
            dve.wait_ge(S["early_in"], 16)
            dve_taps = [tap for tap in range(9) if tap not in PE_TAPS]
            for i, tap in enumerate(dve_taps):
                dy, dx = divmod(tap, 3)
                for h in range(PAIRS):
                    z = zpad[:, h, dy:dy + H, dx:dx + W]
                    y = y_sb[:, h, :].rearrange("p (y x) -> p y x", x=W)
                    if i == 0:
                        dve.wait_ge(S["z_ok"], h + 1)
                        nc.vector.tensor_scalar(y, z, cols(V_CONV + tap), cols(V_CONV_B), ALU.mult, ALU.add)\
                            .then_inc(S["taps"], 1)
                    else:
                        dve.wait_ge(S["taps"], PAIRS * (i - 1) + h + 1)
                        nc.vector.scalar_tensor_tensor(out=y, in0=z, scalar=cols(V_CONV + tap), in1=y, op0=ALU.mult,
                                                       op1=ALU.add).then_inc(S["taps"], 1)
            for h in range(PAIRS):
                dve.wait_ge(S["taps"], PAIRS * (len(dve_taps) - 1) + h + 1)
                dve.wait_ge(S["conv_ps"], h + 1)
                nc.vector.tensor_tensor(y_sb[:, h, :], psA[:, h, 0:L], y_sb[:, h, :], ALU.add).then_inc(S["y_ok"], 1)
            for h in range(PAIRS):
                stats(1, h)
            for h in range(PAIRS):
                normalise(1, h)
            dve.wait_ge(S["late_in"], 16)
            nc.vector.tensor_scalar(outproj_q[:, :], outproj_dup, 0.25 * CLAMP, None, ALU.mult).then_inc(S["outq_ok"], 1)
            by_head = kvT.rearrange("p (h d) -> p h d", d=HC)
            nc.vector.tensor_reduce(kv_gsum[:, :], by_head, AX.X, ALU.add).then_inc(S["kvg_ok"], 1)
            by_head_b = kv_bias.rearrange("p (h d) -> p h d", d=HC)
            nc.vector.tensor_reduce(kv_bsum[:, :], by_head_b, AX.X, ALU.add).then_inc(S["kvbg_ok"], 1)
            dve.wait_ge(S["kvg_ok"], 1)
            nc.vector.scalar_tensor_tensor(out=kv_w[:, :].rearrange("p (h d) -> p h d", d=HC),
                                           in0=kv_gsum[:, :].unsqueeze(2).to_broadcast([P, 4 * HEADS, HC]),
                                           scalar=-1.0 / HC, in1=by_head, op0=ALU.mult, op1=ALU.add).then_inc(S["kvw_ok"], 1)
            dve.wait_ge(S["kvbg_ok"], 1)
            nc.vector.scalar_tensor_tensor(out=kv_b[:, :].rearrange("p (h d) -> p h d", d=HC),
                                           in0=kv_bsum[:, :].unsqueeze(2).to_broadcast([P, 4 * HEADS, HC]),
                                           scalar=-1.0 / HC, in1=by_head_b, op0=ALU.mult, op1=ALU.add).then_inc(S["kvb_ok"], 1)

            def ln_weights():
                dve.wait_ge(S["mask_ok"], 1)
                nc.vector.tensor_tensor(ln_v[:, :], head_mask[:, :], vln_w, ALU.mult).then_inc(S["lnv_ok"], 1)
                nc.vector.tensor_tensor(ln_vb[:, :], head_mask[:, :], vln_b, ALU.mult).then_inc(S["lnkv_ok"], 1)
                nc.vector.tensor_scalar(kln_bL[:, :], cols(V_KLN_B), float(L), None, ALU.mult).then_inc(S["lnkv_ok"], 1)
                dve.wait_ge(S["lnv_ok"], 1)
                nc.vector.tensor_scalar(ln_kv[:, :], ln_v[:, :], cols(V_KLN_W), None, ALU.mult).then_inc(S["lnkv_ok"], 1)
                nc.vector.tensor_scalar(ln_kbv[:, :], ln_v[:, :], cols(V_KLN_B), None, ALU.mult).then_inc(S["lnkv_ok"], 1)
                dve.wait_ge(S["gateh_ok"], 1)
                nc.vector.tensor_tensor(gate_hl[C:P, :], gate_w[C:P, :], gate_hl[C:P, :].bitcast(F32),
                                        ALU.subtract).then_inc(S["gatel_ok"], 1)

            for h in range(PAIRS):
                dve.wait_ge(S["ag_ps"], 2 * h + 2)
                dve.wait_ge(S["ssm_b_ok"], 2)
                nc.vector.tensor_scalar(a_sb[:, h, :, :], per_q(psA[:, h, :]), ssm_b[:, 0:1], None, ALU.add)\
                    .then_inc(S["a_ok"], 1)
                dve.wait_ge(S["tanh_ok"], h + 1)
                dve.wait_ge(S["a_ok"], h + 1)
                nc.vector.scalar_tensor_tensor(out=u_sb[:, h, :, W:W + L], in0=tanh_g[:, h, :, :], scalar=1.0,
                                               in1=a_sb[:, h, :, :], op0=ALU.add, op1=ALU.mult).then_inc(S["u_ok"], 1)
            ln_weights()
            for h in range(PAIRS):
                for k in range(2):
                    i = 2 * h + k + 1
                    dve.wait_ge(S["dirs_ok"], i)
                    dve.wait_ge(S["dsign_ok"], i)
                    nc.vector.scalar_tensor_tensor(out=dirs_sign[:, h, k, :], in0=dirs[:, h, k, :], scalar=0.0,
                                                   in1=dirs_sign[:, h, k, :], op0=ALU.min, op1=ALU.max)\
                        .then_inc(S["dlim_ok"], 1)
                    dve.wait_ge(S["dlim_ok"], i)
                    dve.wait_ge(S["dbad_ok"], i)
                    nc.vector.copy_predicated(dirs[:, h, k, :], dirs_bad[:, h, k, :].bitcast(I32),
                                              dirs_sign[:, h, k, :]).then_inc(S["dclean_ok"], 1)
            for h in range(PAIRS):
                dve.wait_ge(S["osign_ok"], h + 1)
                dve.wait_ge(S["o_ok"], h + 1)
                nc.vector.scalar_tensor_tensor(out=o_sign[:, h, :], in0=o_sb[:, h, :], scalar=0.0, in1=o_sign[:, h, :],
                                               op0=ALU.min, op1=ALU.max).then_inc(S["olim_ok"], 1)
                dve.wait_ge(S["olim_ok"], h + 1)
                dve.wait_ge(S["obad_ok"], h + 1)
                nc.vector.copy_predicated(o_sb[:, h, :], o_bad[:, h, :].bitcast(I32), o_sign[:, h, :])\
                    .then_inc(S["oclean_ok"], 1)
                dve.wait_ge(S["oclean_ok"], h + 1)
                dve.wait_ge(S["xp_in"], 16)
                nc.vector.scalar_tensor_tensor(out=x1[:, h, :], in0=o_sb[:, h, :], scalar=CLAMP, in1=x_sb[:, h, :],
                                               op0=ALU.mult, op1=ALU.add).then_inc(S["x1_ok"], 1)
            for h in range(PAIRS):
                stats(2, h)
            for h in range(PAIRS):
                normalise(2, h)
            for h in range(PAIRS):
                dve.wait_ge(S["kv_ps"], h + 1)
                dve.wait_ge(S["kvb_ok"], 1)
                nc.vector.tensor_tensor(kv[:, h, :, :], psA[:, h, :].rearrange("p (t n) -> p t n", t=T),
                                        kv_b[:, :].unsqueeze(1).to_broadcast([P, T, 2 * P]), ALU.add).then_inc(S["kv_ok"], 1)
            for h in range(PAIRS):
                dve.wait_ge(S["kvsq_ok"], h + 1)
                nc.vector.tensor_reduce(ss[:, h, :], kv_sq[:, h, :, :].rearrange("p t (h d) -> p (t h) d", d=HC),
                                        AX.X, ALU.add).then_inc(S["ss_ok"], 1)
            for h in range(PAIRS):
                dve.wait_ge(S["rinv_ok"], h + 1)
                nc.vector.tensor_tensor(kv_n[:, h, :, 0:2 * P].rearrange("p t (h d) -> p t h d", d=HC),
                                        kv[:, h, :, :].rearrange("p t (h d) -> p t h d", d=HC),
                                        rinv[:, h, :].rearrange("p (t h) -> p t h", t=T).unsqueeze(3)
                                        .to_broadcast([P, T, 4 * HEADS, HC]),
                                        ALU.mult).then_inc(S["kvn_ok"], 1)
            for h in range(PAIRS):
                dve.wait_ge(S["heads_ps"], h + 1)
                dve.wait_ge(S["lnkv_ok"], 4)
                nc.vector.tensor_scalar(k_sum[:, h, :], psB[:, h, P:P + 1], cols(V_KLN_W), kln_bL[:, :], ALU.mult, ALU.add)\
                    .then_inc(S["ksum_ok"], 1)
                nc.vector.tensor_tensor(heads1[:, h, :], psB[:, h, 0:P], ln_kv[:, :], ALU.mult).then_inc(S["h1_ok"], 1)
                nc.vector.tensor_tensor(heads3[:, h, :], psT[:, h, 0:P], ln_kbv[:, :], ALU.mult).then_inc(S["h3_ok"], 1)
                dve.wait_ge(S["ksum_ok"], h + 1)
                dve.wait_ge(S["h1_ok"], h + 1)
                nc.vector.scalar_tensor_tensor(out=heads2[:, h, :], in0=ln_vb[:, :], scalar=k_sum[:, h, :],
                                               in1=heads1[:, h, :], op0=ALU.mult, op1=ALU.add).then_inc(S["h2_ok"], 1)
                dve.wait_ge(S["h2_ok"], h + 1)
                dve.wait_ge(S["h3_ok"], h + 1)
                nc.vector.tensor_tensor(heads[:, h, :], heads2[:, h, :], heads3[:, h, :], ALU.add).then_inc(S["heads_ok"], 1)
            for h in range(PAIRS):
                dve.wait_ge(S["yq_ps"], h + 1)
                nc.vector.tensor_tensor(yq[:, h, 0:P], psB[:, h, P:2 * P], ident[:, :], ALU.add).then_inc(S["yq_ok"], 1)
                nc.vector.tensor_copy(yq[:, h, P:P + 1], psB[:, h, 2 * P:2 * P + 1]).then_inc(S["yq_ok"], 1)
            for h in range(PAIRS):
                dve.wait_ge(S["gelu_ok"], h + 1)
                dve.wait_ge(S["x1xa_ok"], h + 1)
                nc.vector.tensor_tensor(t2[:, h, :], gelu_p[:, h, :], x1_xa[:, h, :], ALU.add).then_inc(S["t2_ok"], 1)
            for h in range(PAIRS):
                stats(3, h)
            for h in range(PAIRS):
                normalise(3, h)
            for h in range(PAIRS):
                dve.wait_ge(S["xh_ok"], h + 1)
                nc.vector.tensor_tensor(xl[:, h, :], psM[:, h, :], xh[:, h, :].bitcast(F32), ALU.subtract)\
                    .then_inc(S["xl_ok"], 1)

            step = [0]

            def chain(ins):
                ins.then_inc(S["gate_chain"], 1)
                step[0] += 1
                dve.wait_ge(S["gate_chain"], step[0])

            G = 4 * PAIRS

            def over_e(ap):
                return ap.rearrange("p h g -> p (h g)").unsqueeze(2).to_broadcast([P, G, E])

            def flat(ap):
                return ap.rearrange("p h g e -> p (h g) e")

            def groups(ap):
                return ap.rearrange("p h g -> p (h g)")

            dve.wait_ge(S["rev_ok"], 1)
            rev = rev8[:, :].unsqueeze(1).to_broadcast([P, G, E])
            for h in range(PAIRS):
                dve.wait_ge(S["lg_ps"], h + 1)
                nc.vector.tensor_tensor(lg[:, h], psT[:, h, 0:4 * E].rearrange("p (g e) -> p g e", e=E),
                                        gate_b.unsqueeze(1).to_broadcast([P, 4, E]), ALU.add).then_inc(S["lg_ok"], 1)
            dve.wait_ge(S["lg_ok"], PAIRS)
            l_all = flat(lg[:, :, :, :])
            chain(nc.vector.tensor_reduce(groups(m1[:, :, :]), l_all, AX.X, ALU.max))
            chain(nc.vector.tensor_tensor(flat(eq1[:, :, :, :]), l_all, over_e(m1[:, :, :]), ALU.is_equal))
            chain(nc.vector.tensor_tensor(flat(pr1[:, :, :, :]), flat(eq1[:, :, :, :]), rev, ALU.mult))
            chain(nc.vector.tensor_reduce(groups(i1[:, :, :]), flat(pr1[:, :, :, :]), AX.X, ALU.max))
            chain(nc.vector.tensor_tensor(flat(f1[:, :, :, :]), rev, over_e(i1[:, :, :]), ALU.is_equal))
            chain(nc.vector.scalar_tensor_tensor(out=lg2[:, :, :, :], in0=f1[:, :, :, :], scalar=-3.0e38,
                                                 in1=lg[:, :, :, :], op0=ALU.mult, op1=ALU.add))
            chain(nc.vector.tensor_reduce(groups(m2[:, :, :]), flat(lg2[:, :, :, :]), AX.X, ALU.max))
            nc.vector.tensor_tensor(m12[:, :, :], m1[:, :, :], m2[:, :, :], ALU.add).then_inc(S["m12_ok"], 1)
            chain(nc.vector.tensor_tensor(flat(eq2[:, :, :, :]), flat(lg2[:, :, :, :]), over_e(m2[:, :, :]), ALU.is_equal))
            dve.wait_ge(S["m12_ok"], 1)
            nc.vector.scalar_tensor_tensor(out=flat(ld[:, :, :, :]), in0=l_all, scalar=2.0, in1=over_e(m12[:, :, :]),
                                           op0=ALU.mult, op1=ALU.subtract).then_inc(S["ld_ok"], 1)
            chain(nc.vector.tensor_tensor(flat(pr2[:, :, :, :]), flat(eq2[:, :, :, :]), rev, ALU.mult))
            chain(nc.vector.tensor_reduce(groups(i2[:, :, :]), flat(pr2[:, :, :, :]), AX.X, ALU.max))
            chain(nc.vector.tensor_tensor(flat(f2[:, :, :, :]), rev, over_e(i2[:, :, :]), ALU.is_equal))
            chain(nc.vector.tensor_tensor(sel[:, :, :, :], f1[:, :, :, :], f2[:, :, :, :], ALU.add))
            dve.wait_ge(S["th_ok"], 1)
            chain(nc.vector.scalar_tensor_tensor(out=wg2[:, :, :, :], in0=th[:, :, :, :], scalar=1.0, in1=sel[:, :, :, :],
                                                 op0=ALU.add, op1=ALU.mult))
            chain(nc.vector.tensor_scalar(wg[:, :, :, :], wg2[:, :, :, :], 0.5, None, ALU.mult))

            def part(h, i):
                return w3[:, h, :, i, :, :].rearrange("p t q e -> p q t e")

            def qt(ap):
                return ap.rearrange("p (q t) e -> p q t e", q=2)

            for i, (src, rest) in enumerate(((wg, wr1), (wr1, wr2), (wr2, None))):
                for h in range(PAIRS):
                    nc.vector.tensor_copy(part(h, i), qt(src[:, h])).then_inc(S["w3_ok" if rest is None else "part_ok"], 1)
                if rest is not None:
                    for h in range(PAIRS):
                        dve.wait_ge(S["part_ok"], 2 * PAIRS * i + h + 1)
                        nc.vector.tensor_tensor(qt(rest[:, h]), qt(src[:, h]), part(h, i), ALU.subtract)\
                            .then_inc(S["part_ok"], 1)
                    dve.wait_ge(S["part_ok"], 2 * PAIRS * (i + 1))
            for h in range(PAIRS):
                dve.wait_ge(S["w3T_ps"], 1)
                nc.vector.tensor_copy(w3T[:, h, :], psT[0:6 * E, h, 256:384].bitcast(BF16)).then_inc(S["w3T_ok"], 1)

            def gated(n):
                h, e = divmod(n, E)
                bank, c0 = output_slot(n)
                dve.wait_ge(S["e_ps"], n + 1 if n >= 14 else n // 2 * 2 + 2)
                if n >= 4:
                    dve.wait_ge(S["acc_ok"], 2 * (n // 2 - 1))
                nc.vector.scalar_tensor_tensor(out=prod[:, n % 4, :], in0=psM[:, bank, c0:c0 + L], scalar=cols(V_B2 + e),
                                               in1=wbc[:, h, e, :], op0=ALU.add, op1=ALU.mult).then_inc(S["prod_ok"], 1)

            for i in range(PAIRS * E // 2):
                h = i // (E // 2)
                dve.wait_ge(S["wbc_ps"], i + 1)
                nc.vector.tensor_copy(wbc[:, h, 2 * i % E:2 * i % E + 2, :], per_q(psT[:, i % 2, :])).then_inc(S["wbc_ok"], 1)
                dve.wait_ge(S["wbc_ok"], i + 1)
                if i < 7:
                    gated(2 * i)
                    gated(2 * i + 1)
                if i == 5:
                    dve.wait_ge(S["acc_ok"], E)
                    nc.vector.tensor_tensor(fin[:, 0, :], acc[:, 0, 0, :], acc[:, 0, 1, :], ALU.add).then_inc(S["fin_ok"], 1)
            gated(14)
            dve.wait_ge(S["acc_ok"], 2 * E - 2)
            nc.vector.tensor_tensor(part_sum[:, 0, :], acc[:, 1, 0, :], acc[:, 1, 1, :], ALU.add).then_inc(S["psum_ok"], 1)
            dve.wait_ge(S["psum_ok"], 1)
            dve.wait_ge(S["prod_ok"], 15)
            nc.vector.tensor_tensor(part_sum[:, 1, :], part_sum[:, 0, :], prod[:, 2, :], ALU.add).then_inc(S["psum_ok"], 1)
            gated(15)
            dve.wait_ge(S["psum_ok"], 2)
            dve.wait_ge(S["prod_ok"], 16)
            nc.vector.tensor_tensor(fin[:, 1, :], part_sum[:, 1, :], prod[:, 3, :], ALU.add).then_inc(S["fin_ok"], 1)


_INS = ['x', 'L0_conv_ln2d_w', 'L0_conv_ln2d_b', 'L0_conv_inproj_w', 'L0_conv_inproj_b', 'L0_conv_dw2d_w',
        'L0_conv_dw2d_b', 'L0_conv_ssm_ln_w', 'L0_conv_ssm_ln_b', 'L0_conv_ssm_in_w', 'L0_conv_ssm_in_b',
        'L0_conv_ssm_dw_w', 'L0_conv_ssm_dw_b', 'L0_conv_ssm_out_w', 'L0_conv_ssm_out_b', 'L0_conv_outproj_w',
        'L0_conv_outproj_b', 'L1_attn_W_qkv', 'L1_attn_b_qkv', 'L1_attn_kln_w', 'L1_attn_kln_b', 'L1_attn_vln_w',
        'L1_attn_vln_b', 'L1_attn_W_proj', 'L1_attn_b_proj', 'L1_ffn_Wg', 'L1_ffn_bg', 'L1_ffn_W1', 'L1_ffn_b1',
        'L1_ffn_W2', 'L1_ffn_b2']


def lay_out(inputs):
    import numpy as _np

    v = {name: _np.ascontiguousarray(inputs[name]) for name in _INS}
    shapes = {name: v[name].shape for name in _INS}
    x = v["x"]
    f = x.dtype
    b, c, hh, ww = x.shape
    p = 2 * c
    e, _, fh = v["L1_ffn_W1"].shape
    heads, _, hc = v["L1_attn_kln_w"].shape

    def diagonal(m):
        r = _np.zeros((2 * m.shape[0], 2 * m.shape[1]), f)
        r[:m.shape[0], :m.shape[1]] = m
        r[m.shape[0]:, m.shape[1]:] = m
        return r

    def column(m):
        m = m.reshape(-1, m.shape[-1])
        return _np.tile(m, (1, p // m.shape[1])).T

    def row(m):
        return _np.broadcast_to(_np.tile(m.reshape(-1), 2), (p, 2 * m.size))

    qkv_w = v["L1_attn_W_qkv"].reshape(heads, 3, hc, c).transpose(1, 0, 2, 3).reshape(3, c, c)
    qkv_b = v["L1_attn_b_qkv"].reshape(heads, 3, hc).transpose(1, 0, 2).reshape(3, c)
    vectors = [column(m) for m in (
        v["L0_conv_ln2d_w"], v["L0_conv_ln2d_b"], v["L0_conv_inproj_b"], v["L0_conv_dw2d_b"], v["L0_conv_ssm_ln_w"],
        v["L0_conv_ssm_ln_b"], v["L0_conv_ssm_in_b"].reshape(2, p), v["L0_conv_ssm_dw_b"], v["L0_conv_ssm_out_b"],
        v["L0_conv_outproj_b"], qkv_b[0], v["L1_attn_b_proj"], v["L1_attn_kln_w"].reshape(-1),
        v["L1_attn_kln_b"].reshape(-1), v["L0_conv_ssm_dw_w"].T, v["L0_conv_dw2d_w"].reshape(c, 9).T,
        v["L1_ffn_b1"].reshape(-1, p), v["L1_ffn_b2"])]
    ssm = _np.zeros((p, 5, p), f)
    for g in range(2):
        for q in range(2):
            ssm[q * c:(q + 1) * c, 2 * g + q, :] = v["L0_conv_ssm_in_w"][g * p:(g + 1) * p].T
    ssm[:, 4, :] = _np.tile(v["L0_conv_ssm_out_w"].T, (1, 2))
    outproj_t = v["L0_conv_outproj_w"].T
    return shapes, {
        "x_tok": x.reshape(2, 2, c, 2, p).transpose(4, 0, 3, 1, 2).reshape(p, 2, 2, p),
        "x_chan": x.reshape(2, p, hh * ww).transpose(1, 0, 2),
        "early": _np.concatenate([diagonal(v["L0_conv_inproj_w"].T)] + vectors, 1),
        "ssm": ssm,
        "late": _np.concatenate([
            diagonal(outproj_t), diagonal(qkv_w[1].T), diagonal(qkv_w[2].T), diagonal(qkv_w[0]),
            diagonal(v["L1_attn_W_proj"].T), _np.tile(outproj_t, (2, 1)), row(qkv_b[1]), row(qkv_b[2]),
            row(v["L1_attn_vln_w"]), row(v["L1_attn_vln_b"]), _np.tile(v["L1_ffn_Wg"], (2, 1)),
            _np.broadcast_to(v["L1_ffn_bg"], (p, e))], 1),
        "w1": _np.tile(v["L1_ffn_W1"].transpose(1, 0, 2), (2, 1, 1)),
        "w2": v["L1_ffn_W2"].reshape(e * fh // p, p, c).transpose(1, 0, 2),
    }


def kernel(**inputs):
    import numpy as _np
    import concourse.bacc as _bacc
    from concourse import mybir as _mybir
    from concourse.bass_utils import run_bass_kernel_spmd as _run

    shapes, laid = lay_out(inputs)
    nc = _bacc.Bacc("TRN2", target_bir_lowering=False, num_devices=1)
    arrays, aps = {}, {}
    for name, m in laid.items():
        arrays[f"in_{name}_dram"] = _np.ascontiguousarray(m)
        aps[name] = nc.dram_tensor(f"in_{name}_dram", m.shape, _mybir.dt.from_np(m.dtype), kind="ExternalInput").ap()
    out = nc.dram_tensor("out_0_dram", shapes["x"], _mybir.dt.float32, kind="ExternalOutput").ap()
    conv_attention_moe(nc, aps, shapes, out)
    r = _run(nc, [arrays], core_ids=[0])
    return r.results[0]["out_0_dram"]
```

```python
from contextlib import ExitStack

import concourse.bass as bass
from concourse import mybir

F32 = mybir.dt.float32
F32R = mybir.dt.float32r
BF16 = mybir.dt.bfloat16
I32 = mybir.dt.int32
ALU = mybir.AluOpType
ACT = mybir.ActivationFunctionType
AX = mybir.AxisListType

LN_EPS_CONV = 1e-6
LN_EPS_TOKEN = 1e-5
STD_EPS_HEAD = 1e-5
TINY_VARIANCE = 1e-19
CLAMP = 1e4

RING = 12


def output_slot(n):
    return (n // 2 % 2, n % 2 * 256) if n < 14 else (15 - n, 0)


(V_LN0_W, V_LN0_B, V_IN_B, V_CONV_B, V_LN1_W, V_LN1_B, V_SSM_A_B, V_SSM_G_B, V_SSM_DW_B, V_SSM_OUT_B,
 V_OUT_B, V_Q_B, V_PROJ_B, V_KLN_W, V_KLN_B, V_SSM_DW) = range(16)
V_CONV = V_SSM_DW + 3
V_B1 = V_CONV + 9
PE_TAPS = (0, 1, 2, 3, 4)


def conv_attention_moe(nc: bass.Bass, a: dict, shapes: dict, out: bass.AP):
    B, C, H, W = shapes["x"]
    L = H * W
    P = 128
    PAIRS = B // 2
    T = L // P
    HID = shapes["L0_conv_ssm_in_w"][0] // 2
    HEADS, _, HC = shapes["L1_attn_kln_w"]
    E, _, FH = shapes["L1_ffn_W1"]
    CK = FH // P
    V_B2 = V_B1 + E * CK
    NVEC = V_B2 + E
    PADW = W + 2
    PH = L + 2 * W
    assert 2 * C == P and HID == P and H == W and T == 2 and PAIRS == 2 and 2 * L == 512

    with ExitStack() as ctx:
        def sb(name, shape, dt=F32):
            return ctx.enter_context(nc.sbuf_tensor(name, shape, dt))

        def ps(name, shape, dt=F32):
            return ctx.enter_context(nc.psum_tensor(name, shape, dt))

        def sem(name):
            return ctx.enter_context(nc.semaphore(name))

        psT = ps("psT", [P, PAIRS, 512])
        psM = ps("psM", [P, PAIRS, 512])
        psA = ps("psA", [P, PAIRS, 512])
        psB = ps("psB", [P, PAIRS, 512])

        x_tok = sb("x_tok", [P, PAIRS, T, P])
        early = sb("early", [P, P + NVEC])
        ssm_in = sb("ssm_in", [P, 5, P])
        DW = 9 * P + C + 2 * E
        late = sb("late", [P, DW])
        x_sb = sb("x_sb", [P, PAIRS, L])
        w1_nat = sb("w1_nat", [P, E, FH])
        w2_sb = sb("w2_sb", [P, E * CK, C])
        in_raw = early[:, 0:P]
        vec = early[:, P:P + NVEC]
        sout_raw = ssm_in[:, 4, :]
        outproj_w = late[:, 0:P]
        kvT = late[:, P:3 * P]
        q_w = late[:, 3 * P:4 * P]
        proj_w = late[:, 4 * P:5 * P]
        outproj_dup = late[:, 5 * P:5 * P + C]
        kv_bias = late[:, 5 * P + C:7 * P + C]
        vln_w = late[:, 7 * P + C:8 * P + C]
        vln_b = late[:, 8 * P + C:9 * P + C]
        v_end = 9 * P + C
        gate_w = late[:, v_end:v_end + E]
        gate_b = late[:, v_end + E:v_end + 2 * E]

        ident = sb("ident", [P, P])
        ident_bf = sb("ident_bf", [P, P], BF16)
        pick3 = sb("pick3", [3 * 2 * E, 2 * E], BF16)
        pick_q = sb("pick_q", [3 * 2 * E, E, 2, C], BF16)
        ones = sb("ones", [P, P])
        first_row = sb("first_row", [P, P])
        head_mask = sb("head_mask", [P, P])
        conv_diag = sb("conv_diag", [P, len(PE_TAPS), P])
        ln_kv = sb("ln_kv", [P, P])
        ln_v = sb("ln_v", [P, P])
        ln_vb = sb("ln_vb", [P, P])
        ln_kbv = sb("ln_kbv", [P, P])
        kln_bL = sb("kln_bL", [P, 1])
        out_b = sb("out_b", [P, 1])
        sout_b0 = sb("sout_b0", [P, 1])
        minus_half = sb("minus_half", [P, 4])
        rev8 = sb("rev8", [P, E])
        in_w = sb("in_w", [P, P])
        in_b = sb("in_b", [P, 1])
        ssm_w = sb("ssm_w", [P, 2, 2, P])
        ssm_b = sb("ssm_b", [P, 2])
        sout_w = sb("sout_w", [P, 3, P])
        sout_b = sb("sout_b", [P, 1])
        outproj_q = sb("outproj_q", [P, C])
        kv_gsum = sb("kv_gsum", [P, 4 * HEADS])
        kv_bsum = sb("kv_bsum", [P, 4 * HEADS])
        kv_w = sb("kv_w", [P, 2 * P])
        kv_b = sb("kv_b", [P, 2 * P])
        w1_hl = sb("w1_hl", [P, E, FH], F32R)
        gate_hl = sb("gate_hl", [P, E], F32R)

        st = sb("st", [P, PAIRS, 4, 6])
        mv = sb("mv", [P, PAIRS, 4, 2])
        lnv = sb("lnv", [P, PAIRS, 4])
        rstd = sb("rstd", [P, PAIRS, 4])
        var_eps = sb("var_eps", [P, PAIRS, 4])
        norm_t = sb("norm_t", [P, PAIRS, T, P])
        norm_d = sb("norm_d", [P, PAIRS, 2 * T, 2, C])
        norm_c = sb("norm_c", [P, PAIRS, L])
        zpad = sb("zpad", [P, PAIRS, H + 2, PADW])
        y_sb = sb("y_sb", [P, PAIRS, L])
        gate_s = sb("gate_s", [P, PAIRS, 2, L])
        u_sb = sb("u_sb", [P, PAIRS, 2, PH])
        dirs = sb("dirs", [P, PAIRS, 2, 2 * L])
        dirs_sign = sb("dirs_sign", [P, PAIRS, 2, 2 * L])
        dirs_bad = sb("dirs_bad", [P, PAIRS, 2, 2 * L])
        o_sb = sb("o_sb", [P, PAIRS, L])
        o_sign = sb("o_sign", [P, PAIRS, L])
        o_bad = sb("o_bad", [P, PAIRS, L])
        x1 = sb("x1", [P, PAIRS, L])
        xa_c = sb("xa_c", [P, PAIRS, L])
        x1_xa = sb("x1_xa", [P, PAIRS, L])
        kv_sq = sb("kv_sq", [P, PAIRS, T, 2 * P])
        ss = sb("ss", [P, PAIRS, T * 4 * HEADS])
        ss_ln = sb("ss_ln", [P, PAIRS, T * 4 * HEADS])
        std = sb("std", [P, PAIRS, T * 4 * HEADS])
        std_ln = sb("std_ln", [P, PAIRS, T * 4 * HEADS])
        rinv = sb("rinv", [P, PAIRS, T * 4 * HEADS])
        kv_n = sb("kv_n", [P, PAIRS, T, 2 * P + 1])
        k_sum = sb("k_sum", [P, PAIRS, 1])
        heads1 = sb("heads1", [P, PAIRS, P])
        heads2 = sb("heads2", [P, PAIRS, P])
        heads3 = sb("heads3", [P, PAIRS, P])
        heads = sb("heads", [P, PAIRS, P])
        yq = sb("yq", [P, PAIRS, P + 1])
        zT = sb("zT", [P, PAIRS, P])
        zb = sb("zb", [P, PAIRS, 1])
        gelu_p = sb("gelu_p", [P, PAIRS, L])
        t2 = sb("t2", [P, PAIRS, L])
        xh = sb("xh", [P, PAIRS, 2 * L], F32R)
        xl = sb("xl", [P, PAIRS, 2 * L], F32R)
        lg = sb("lg", [P, PAIRS, 4, E])
        m1 = sb("m1", [P, PAIRS, 4])
        eq1 = sb("eq1", [P, PAIRS, 4, E])
        pr1 = sb("pr1", [P, PAIRS, 4, E])
        i1 = sb("i1", [P, PAIRS, 4])
        f1 = sb("f1", [P, PAIRS, 4, E])
        lg2 = sb("lg2", [P, PAIRS, 4, E])
        m2 = sb("m2", [P, PAIRS, 4])
        eq2 = sb("eq2", [P, PAIRS, 4, E])
        pr2 = sb("pr2", [P, PAIRS, 4, E])
        i2 = sb("i2", [P, PAIRS, 4])
        f2 = sb("f2", [P, PAIRS, 4, E])
        sel = sb("sel", [P, PAIRS, 4, E])
        m12 = sb("m12", [P, PAIRS, 4])
        ld = sb("ld", [P, PAIRS, 4, E])
        th = sb("th", [P, PAIRS, 4, E])
        wg2 = sb("wg2", [P, PAIRS, 4, E])
        wg = sb("wg", [P, PAIRS, 4, E])
        wr1 = sb("wr1", [P, PAIRS, 4, E])
        wr2 = sb("wr2", [P, PAIRS, 4, E])
        w3 = sb("w3", [P, PAIRS, T, 3, 2, E], BF16)
        w3T = sb("w3T", [3 * 2 * E, PAIRS, L], BF16)
        wbc = sb("wbc", [P, PAIRS, E, L])
        hs = sb("hs", [P, RING, 2 * L])
        prod = sb("prod", [P, 4, L])
        acc = sb("acc", [P, PAIRS, 2, L])
        part_sum = sb("part_sum", [P, 2, L])
        fin = sb("fin", [P, PAIRS, L])

        names = """early_in ssm_in late_in xp_in w1_in w2_in
            ident0 ident_ok bf_ok zeros_ok pick0 pick_ok pickq_ok mask0 mask1 mask_ok ones_ok row0 row_ok rev_ok
            in_w_ok inb_ps in_b_ok diag_ok ssm_w_ok ssmb_ps ssm_b_ok sout_w_ok sout_b0_ok sout_b_ok
            out_b_ok outq_ok kvg_ok kvw_ok kvbg_ok kvb_ok lnv_ok lnkv_ok w1h_ok w1l_ok gateh_ok gatel_ok
            wbc_ps wbc_ok h_ps h_ok e_ps prod_ok acc_ok psum_ok fin_ok out_done""".split()
        once_per_pair = """vare_ok z_ps z_ok conv_ps y_ok ag_ps sig_ok u_ok u_left u_right dirs_ps dirs_ok dsign_ok
            dbad_ok dlim_ok dclean_ok out_ps o_ok osign_ok obad_ok olim_ok oclean_ok x1_ok x1xa_ok kv_ps
            kvsq_ok ss_ok ssln_ok std_ok stdln_ok rinv_ok kvn_ok heads_ps ksum_ok h1_ok h2_ok h3_ok heads_ok yq_ps
            yq_ok zT_ps zT_ok zb_ok p_ps gelu_ok t2_ok xdup_ps xh_ok xl_ok lg_ps m12_ok ld_ok th_ok w3_ok w3T_ps
            w3T_ok""".split()
        pair_names = "xt_in tT_ps t_stats t_mv t_lnv t_rstd t_norm cT_ps c_norm taps gate_chain".split()
        S = {n: sem(n) for n in names + once_per_pair}
        Q = {n: [sem(f"{n}_{h}") for h in range(PAIRS)] for n in pair_names}

        def per_q(ap):
            return ap.rearrange("p (q l) -> p q l", q=2)

        def cols(i, n=1):
            return vec[:, i:i + n]

        def hidden_bank(c):
            return (psA, psB)[c % 2][:, c // 2 % 2, :]

        def copies_bank(h):
            return (psM, psT)[h][:, h, :]

        block = ctx.enter_context(nc.Block())
        out_pairs = out.rearrange("(h q) c y x -> h (q c) (y x)", q=2)

        @block.sync
        def _(sp):
            for h in range(PAIRS):
                sp.dma_start(x_tok[:, h, :, :], a["x_tok"][:, h]).then_inc(Q["xt_in"][h], 16)
            sp.dma_start(ssm_in[:, :, :], a["ssm"]).then_inc(S["ssm_in"], 16)
            sp.dma_start(late[:, :], a["late"]).then_inc(S["late_in"], 16)
            sp.dma_start(w1_nat[:, :, :], a["w1"]).then_inc(S["w1_in"], 16)
            sp.dma_start(x_sb[:, :, :], a["x_chan"]).then_inc(S["xp_in"], 16)
            sp.dma_start(w2_sb[:, :, :], a["w2"]).then_inc(S["w2_in"], 16)
            for h in range(PAIRS):
                sp.wait_ge(S["fin_ok"], h + 1)
                sp.dma_start(out_pairs[h], fin[:, h, :]).then_inc(S["out_done"], 16)
            sp.wait_ge(S["out_done"], 16 * PAIRS)

        @block.gpsimd
        def _(pool):
            nc.gpsimd.memset(ident[:, :], 0.0).then_inc(S["ident0"], 1)
            pool.wait_ge(S["ident0"], 1)
            nc.gpsimd.affine_select(out=ident[:, :], in_=ident[:, :], compare_op=ALU.not_equal, fill=1.0, base=0,
                                    pattern=[[-1, P]], channel_multiplier=1).then_inc(S["ident_ok"], 1)
            nc.gpsimd.memset(zpad[:, :, :, :], 0.0).then_inc(S["zeros_ok"], 1)
            nc.gpsimd.memset(u_sb[:, :, :, 0:1], 0.0).then_inc(S["zeros_ok"], 1)
            nc.gpsimd.memset(u_sb[:, :, :, PH - 1:PH], 0.0).then_inc(S["zeros_ok"], 1)
            nc.gpsimd.memset(ones[:, :], 1.0).then_inc(S["ones_ok"], 1)
            nc.gpsimd.memset(first_row[:, :], 0.0).then_inc(S["row0"], 1)
            pool.wait_ge(S["row0"], 1)
            nc.gpsimd.memset(first_row[0:1, :], 1.0).then_inc(S["row_ok"], 1)
            pool.wait_ge(S["row_ok"], 1)
            nc.gpsimd.memset(kv_n[:, :, :, 2 * P:2 * P + 1], 1.0).then_inc(S["ones_ok"], 1)
            nc.gpsimd.memset(minus_half[:, :], -0.5)
            nc.gpsimd.iota(rev8[:, :], pattern=[[-1, E]], base=E, channel_multiplier=0,
                           allow_small_or_imprecise_dtypes=True).then_inc(S["rev_ok"], 1)
            hm = head_mask[:, :].rearrange("p (g d) -> p g d", d=HC)
            nc.gpsimd.memset(head_mask[:, :], 1.0 / L).then_inc(S["mask0"], 1)
            pool.wait_ge(S["mask0"], 1)
            nc.gpsimd.affine_select(out=hm, in_=hm, compare_op=ALU.is_ge, fill=0.0, base=0,
                                    pattern=[[-HC, P // HC], [0, HC]], channel_multiplier=1).then_inc(S["mask1"], 1)
            pool.wait_ge(S["mask1"], 1)
            nc.gpsimd.affine_select(out=hm, in_=hm, compare_op=ALU.is_ge, fill=0.0, base=HC - 1,
                                    pattern=[[HC, P // HC], [0, HC]], channel_multiplier=-1).then_inc(S["mask_ok"], 1)
            nc.gpsimd.memset(pick3[:, :], 0.0).then_inc(S["pick0"], 1)
            for j in range(3):
                pool.wait_ge(S["pick0"], j + 1)
                nc.gpsimd.affine_select(out=pick3[:, :], in_=pick3[:, :], compare_op=ALU.not_equal, fill=1.0,
                                        base=-2 * E * j, pattern=[[-1, 2 * E]],
                                        channel_multiplier=1).then_inc(S["pick0" if j < 2 else "pick_ok"], 1)
            pool.wait_ge(S["pick_ok"], 1)
            spread = pick3[:, :].rearrange("r (q e) -> r e q", q=2)
            for q in range(2):
                nc.gpsimd.tensor_copy(pick_q[:, :, q, :], spread[:, :, q:q + 1].to_broadcast([6 * E, E, C]))\
                    .then_inc(S["pickq_ok"], 1)
            pool.wait_ge(S["ident_ok"], 1)
            nc.gpsimd.tensor_copy(ident_bf[:, :], ident[:, :]).then_inc(S["bf_ok"], 1)

            pool.wait_ge(S["early_in"], 16)
            pool.wait_ge(S["ssm_in"], 16)
            for tap, (fwd, bwd) in enumerate(((0, 2), (1, 1), (2, 0))):
                for d, k in enumerate((fwd, bwd)):
                    nc.gpsimd.tensor_scalar(sout_w[:, tap, d * C:(d + 1) * C], sout_raw[:, d * C:(d + 1) * C],
                                            cols(V_SSM_DW + k), None, ALU.mult).then_inc(S["sout_w_ok"], 1)
            pool.wait_ge(S["sout_w_ok"], 6)
            def wrap_columns(h):
                pool.wait_ge(S["u_ok"], h + 1)
                pool.wait_ge(S["zeros_ok"], 3)
                nc.gpsimd.tensor_copy(u_sb[:, h, :, 1:W], u_sb[:, h, :, L:L + W - 1]).then_inc(S["u_left"], 1)
                nc.gpsimd.tensor_copy(u_sb[:, h, :, L + W:L + 2 * W - 1],
                                      u_sb[:, h, :, W + 1:2 * W]).then_inc(S["u_right"], 1)
                pool.wait_ge(S["u_right"], h + 1)

            def bad_dirs(h, k):
                pool.wait_ge(S["dirs_ok"], 2 * h + k + 1)
                nc.gpsimd.tensor_scalar(dirs_bad[:, h, k, :], dirs[:, h, k, :], 0.0, 0.0, ALU.mult, ALU.add)\
                    .then_inc(S["dbad_ok"], 1)
                pool.wait_ge(S["dbad_ok"], 2 * h + k + 1)

            def bad_out(h):
                pool.wait_ge(S["o_ok"], h + 1)
                nc.gpsimd.tensor_scalar(o_bad[:, h, :], o_sb[:, h, :], 0.0, 0.0, ALU.mult, ALU.add)\
                    .then_inc(S["obad_ok"], 1)
                pool.wait_ge(S["obad_ok"], h + 1)

            def w1_low(i):
                pool.wait_ge(S["w1h_ok"], i + 1)
                rows, experts = slice(C, P), slice(2 * i, 2 * i + 2)
                nc.gpsimd.tensor_tensor(w1_hl[rows, experts, :], w1_nat[rows, experts, :],
                                        w1_hl[rows, experts, :].bitcast(F32), ALU.subtract).then_inc(S["w1l_ok"], 1)
                pool.wait_ge(S["w1l_ok"], i + 1)

            def attention_residual(h):
                pool.wait_ge(S["x1_ok"], h + 1)
                pool.wait_ge(Q["c_norm"][h], 3)
                nc.gpsimd.tensor_tensor(x1_xa[:, h, :], x1[:, h, :], xa_c[:, h, :], ALU.add).then_inc(S["x1xa_ok"], 1)
                pool.wait_ge(S["x1xa_ok"], h + 1)

            def token_rsqrt(h):
                pool.wait_ge(Q["t_mv"][h], 4)
                nc.gpsimd.tensor_scalar(var_eps[:, h, :], mv[:, h, :, 1], LN_EPS_TOKEN, None, ALU.add)\
                    .then_inc(S["vare_ok"], 1)
                pool.wait_ge(S["vare_ok"], h + 1)
                nc.gpsimd.tensor_tensor(rstd[:, h, :], var_eps[:, h, :], minus_half[:, :], ALU.pow)\
                    .then_inc(Q["t_rstd"][h], 1)

            def accumulate(i):
                h = i // (E // 2)
                pool.wait_ge(S["prod_ok"], 2 * i + 2)
                if i % (E // 2) == 0:
                    pool.wait_ge(S["t2_ok"], h + 1)
                    nc.gpsimd.tensor_tensor(acc[:, h, 0, :], t2[:, h, :], prod[:, 0, :], ALU.add).then_inc(S["acc_ok"], 1)
                    nc.gpsimd.tensor_copy(acc[:, h, 1, :], prod[:, 1, :]).then_inc(S["acc_ok"], 1)
                else:
                    pool.wait_ge(S["acc_ok"], 2 * i)
                    nc.gpsimd.tensor_tensor(acc[:, h, :, :], acc[:, h, :, :], prod[:, 2 * i % 4:2 * i % 4 + 2, :],
                                            ALU.add).then_inc(S["acc_ok"], 2)

            w1_low(0)
            w1_low(1)
            wrap_columns(0)
            bad_dirs(0, 0)
            bad_dirs(0, 1)
            bad_out(0)
            wrap_columns(1)
            bad_dirs(1, 0)
            bad_dirs(1, 1)
            bad_out(1)
            w1_low(2)
            attention_residual(0)
            w1_low(3)
            attention_residual(1)
            token_rsqrt(0)
            token_rsqrt(1)
            for i in range(0, 7):
                accumulate(i)

        @block.scalar
        def _(act):
            act.dma_start(early[:, :], a["early"]).then_inc(S["early_in"], 16)
            nc.scalar.preload_act_table_set("natural_log_exp_and_others")

            def rsqrt(n, h, eps):
                act.wait_ge(Q["t_mv"][h], n + 1)
                nc.scalar.activation(lnv[:, h, :], mv[:, h, :, 1], ACT.Ln, bias=eps).then_inc(Q["t_lnv"][h], 1)
                act.wait_ge(Q["t_lnv"][h], n + 1)
                nc.scalar.activation(rstd[:, h, :], lnv[:, h, :], ACT.Exp, scale=-0.5).then_inc(Q["t_rstd"][h], 1)

            def norm_out(n, h, dst):
                act.wait_ge(Q["cT_ps"][h], n + 1)
                nc.scalar.copy(dst[:, h, :], psM[:, h, L:2 * L]).then_inc(Q["c_norm"][h], 1)

            def conv_diagonal(i):
                act.wait_ge(S["early_in"], 16)
                act.wait_ge(S["ident_ok"], 1)
                nc.scalar.activation(conv_diag[:, i, :], ident[:, :], ACT.Copy, scale=cols(V_CONV + PE_TAPS[i]))\
                    .then_inc(S["diag_ok"], 1)

            def in_weights():
                act.wait_ge(S["early_in"], 16)
                nc.scalar.activation(in_w[:, :], in_raw, ACT.Copy, scale=cols(V_LN0_W)).then_inc(S["in_w_ok"], 1)

            def in_bias():
                act.wait_ge(S["inb_ps"], 1)
                nc.scalar.activation(in_b[:, :], psB[:, 1, 3:4], ACT.Identity, bias=cols(V_IN_B))\
                             .then_inc(S["in_b_ok"], 1)

            def in_out(h):
                act.wait_ge(S["z_ps"], h + 1)
                act.wait_ge(S["zeros_ok"], 1)
                act.wait_ge(S["in_b_ok"], 1)
                nc.scalar.activation(zpad[:, h, 1:H + 1, 1:W + 1], psM[:, h, 0:L].rearrange("p (y x) -> p y x", x=W),
                                     ACT.Identity, bias=in_b[:, 0:1]).then_inc(S["z_ok"], 1)

            def ssm_weights():
                act.wait_ge(S["ssm_in"], 16)
                act.wait_ge(S["early_in"], 16)
                nc.scalar.activation(ssm_w[:, :, :, :].rearrange("p g q o -> p (g q) o"), ssm_in[:, 0:4, :], ACT.Copy,
                                     scale=cols(V_LN1_W)).then_inc(S["ssm_w_ok"], 1)

            def ssm_biases():
                act.wait_ge(S["ssmb_ps"], 2)
                nc.scalar.activation(ssm_b[:, 0:1], psB[:, 1, 0:1], ACT.Identity, bias=cols(V_SSM_A_B))\
                             .then_inc(S["ssm_b_ok"], 1)
                nc.scalar.activation(ssm_b[:, 1:2], psB[:, 1, 1:2], ACT.Identity, bias=cols(V_SSM_G_B))\
                             .then_inc(S["ssm_b_ok"], 1)
                nc.scalar.activation(sout_b0[:, :], psB[:, 1, 2:3], ACT.Identity, bias=cols(V_SSM_OUT_B))\
                    .then_inc(S["sout_b0_ok"], 1)
                act.wait_ge(S["sout_b0_ok"], 1)
                nc.scalar.mul(sout_b[:, :], sout_b0[:, :], 1.0 / CLAMP).then_inc(S["sout_b_ok"], 1)
                nc.scalar.mul(out_b[:, :], cols(V_OUT_B), 1.0 / CLAMP).then_inc(S["out_b_ok"], 1)

            def ssm_gate(h):
                act.wait_ge(S["ag_ps"], 2 * h + 1)
                act.wait_ge(S["ssm_b_ok"], 2)
                nc.scalar.activation(gate_s[:, h, :, :], per_q(psB[:, h, :]), ACT.Sigmoid, bias=ssm_b[:, 1:2])\
                    .then_inc(S["sig_ok"], 1)

            def w1_high(i):
                act.wait_ge(S["w1_in"], 16)
                nc.scalar.copy(w1_hl[:, 2 * i:2 * i + 2, :], w1_nat[:, 2 * i:2 * i + 2, :]).then_inc(S["w1h_ok"], 1)

            def gate_high():
                act.wait_ge(S["late_in"], 16)
                nc.scalar.copy(gate_hl[:, :], gate_w).then_inc(S["gateh_ok"], 1)

            def ssm_out(h, k):
                bank = (psA, psB)[k][:, h, :]
                act.wait_ge(S["dirs_ps"], 2 * h + k + 1)
                act.wait_ge(S["sout_b_ok"], 1)
                nc.scalar.activation(dirs[:, h, k, :], bank, ACT.Identity, bias=sout_b[:, 0:1],
                                     scale=1.0 / CLAMP).then_inc(S["dirs_ok"], 1)
                nc.scalar.activation(dirs_sign[:, h, k, :], bank, ACT.Sign, bias=sout_b[:, 0:1],
                                     scale=1.0 / CLAMP).then_inc(S["dsign_ok"], 1)

            def conv_out(h):
                act.wait_ge(S["out_ps"], h + 1)
                act.wait_ge(S["out_b_ok"], 1)
                nc.scalar.activation(o_sb[:, h, :], psM[:, h, 0:L], ACT.Identity, bias=out_b[:, 0:1],
                                     scale=1.0 / CLAMP).then_inc(S["o_ok"], 1)
                nc.scalar.activation(o_sign[:, h, :], psM[:, h, 0:L], ACT.Sign, bias=out_b[:, 0:1],
                                     scale=1.0 / CLAMP).then_inc(S["osign_ok"], 1)

            def squares(h):
                act.wait_ge(S["kv_ps"], h + 1)
                nc.scalar.activation(kv_sq[:, h, :, :].rearrange("p t n -> p (t n)"), psA[:, h, :], ACT.Square)\
                             .then_inc(S["kvsq_ok"], 1)

            def head_rstd(h):
                act.wait_ge(S["ss_ok"], h + 1)
                nc.scalar.activation(ss_ln[:, h, :], ss[:, h, :], ACT.Ln, scale=1.0 / (HC - 1),
                                     bias=TINY_VARIANCE).then_inc(S["ssln_ok"], 1)
                act.wait_ge(S["ssln_ok"], h + 1)
                nc.scalar.activation(std[:, h, :], ss_ln[:, h, :], ACT.Exp, scale=0.5).then_inc(S["std_ok"], 1)
                act.wait_ge(S["std_ok"], h + 1)
                nc.scalar.activation(std_ln[:, h, :], std[:, h, :], ACT.Ln, bias=STD_EPS_HEAD).then_inc(S["stdln_ok"], 1)
                act.wait_ge(S["stdln_ok"], h + 1)
                nc.scalar.activation(rinv[:, h, :], std_ln[:, h, :], ACT.Exp, scale=-1.0).then_inc(S["rinv_ok"], 1)

            def attention_weight(h):
                act.wait_ge(S["zT_ps"], 2 * h + 2)
                nc.scalar.copy(zT[:, h, :], psT[:, h, 0:P]).then_inc(S["zT_ok"], 1)
                nc.scalar.activation(zb[:, h, :], psT[:, h, P:P + 1], ACT.Identity, bias=cols(V_PROJ_B))\
                             .then_inc(S["zb_ok"], 1)

            def proj_gelu(h):
                act.wait_ge(S["p_ps"], h + 1)
                act.wait_ge(S["zb_ok"], h + 1)
                nc.scalar.activation(gelu_p[:, h, :], psM[:, h, 0:L], ACT.Gelu, bias=zb[:, h, :])\
                             .then_inc(S["gelu_ok"], 1)

            def token_high(h):
                act.wait_ge(S["xdup_ps"], h + 1)
                nc.scalar.copy(xh[:, h, :], copies_bank(h)).then_inc(S["xh_ok"], 1)

            def hidden_gelu(n):
                act.wait_ge(S["h_ps"], n + 1)
                if n >= RING:
                    act.wait_ge(S["e_ps"], (n - RING) // CK + 1)
                nc.scalar.activation(hs[:, n % RING, :], hidden_bank(n), ACT.Gelu,
                                     bias=cols(V_B1 + n % (E * CK))).then_inc(S["h_ok"], 1)

            def gate_tanh(h):
                act.wait_ge(S["ld_ok"], h + 1)
                nc.scalar.activation(th[:, h, :, :], ld[:, h, :, :], ACT.Tanh, scale=0.5).then_inc(S["th_ok"], 1)

            conv_diagonal(0)
            rsqrt(0, 0, LN_EPS_CONV)
            conv_diagonal(1)
            conv_diagonal(2)
            conv_diagonal(3)
            in_bias()
            in_weights()
            norm_out(0, 0, norm_c)
            rsqrt(0, 1, LN_EPS_CONV)
            gate_high()
            in_out(0)
            conv_diagonal(4)
            norm_out(0, 1, norm_c)
            ssm_weights()
            in_out(1)
            ssm_biases()
            rsqrt(1, 0, LN_EPS_CONV)
            nc.scalar.preload_act_table_set("sigmoid_and_others")
            w1_high(0)
            norm_out(1, 0, norm_c)
            w1_high(1)
            w1_high(2)
            ssm_gate(0)
            w1_high(3)
            nc.scalar.preload_act_table_set("natural_log_exp_and_others")
            rsqrt(1, 1, LN_EPS_CONV)
            ssm_out(0, 0)
            nc.scalar.preload_act_table_set("sigmoid_and_others")
            norm_out(1, 1, norm_c)
            ssm_out(0, 1)
            ssm_gate(1)
            conv_out(0)
            nc.scalar.preload_act_table_set("natural_log_exp_and_others")
            rsqrt(2, 0, LN_EPS_TOKEN)
            ssm_out(1, 0)
            ssm_out(1, 1)
            norm_out(2, 0, xa_c)
            squares(0)
            head_rstd(0)
            conv_out(1)
            rsqrt(2, 1, LN_EPS_TOKEN)
            nc.scalar.preload_act_table_set("gelu_and_others")
            attention_weight(0)
            norm_out(2, 1, xa_c)
            proj_gelu(0)
            nc.scalar.preload_act_table_set("natural_log_exp_and_others")
            squares(1)
            head_rstd(1)
            token_high(0)
            nc.scalar.preload_act_table_set("gelu_and_others")
            for n in range(0, 2):
                hidden_gelu(n)
            attention_weight(1)
            hidden_gelu(2)
            proj_gelu(1)
            gate_tanh(0)
            for n in range(3, 10):
                hidden_gelu(n)
            token_high(1)
            for n in range(10, 20):
                hidden_gelu(n)
            gate_tanh(1)
            for n in range(20, 32):
                hidden_gelu(n)

        @block.tensor
        def _(pe):
            def keep_clock(n):
                for _ in range(n):
                    nc.tensor.matmul(psB[:, 0, 0:P], ident[:, :], ident[:, :], start=True, stop=True)

            def to_tokens(h, src, ready):
                pe.wait_ge(S[ready], h + 1)
                for t in range(T):
                    m = nc.tensor.transpose(psT[:, h, t * P:(t + 1) * P], src[:, h, t * P:(t + 1) * P], ident[:, :])
                m.then_inc(Q["tT_ps"][h], 1)

            def to_channels(n, h):
                for t in range(T):
                    pe.wait_ge(Q["t_norm"][h], T * n + t + 1)
                    m = nc.tensor.transpose(psM[:, h, L + t * P:L + (t + 1) * P], norm_t[:, h, t, :], ident[:, :])
                m.then_inc(Q["cT_ps"][h], 1)

            def in_bias_product():
                pe.wait_ge(S["early_in"], 16)
                nc.tensor.matmul(psB[:, 1, 3:4], in_raw, cols(V_LN0_B), start=True, stop=True).then_inc(S["inb_ps"], 1)

            def in_product(h):
                pe.wait_ge(Q["c_norm"][h], 1)
                pe.wait_ge(S["in_w_ok"], 1)
                nc.tensor.matmul(psM[:, h, 0:L], in_w[:, :], norm_c[:, h, :], start=True, stop=True)\
                             .then_inc(S["z_ps"], 1)

            def ssm_bias_products():
                pe.wait_ge(S["ssm_in"], 16)
                pe.wait_ge(S["early_in"], 16)
                pe.wait_ge(S["in_b_ok"], 1)
                for g in range(2):
                    m = nc.tensor.matmul(psB[:, 1, g:g + 1], ssm_in[:, 2 * g, :], cols(V_LN1_B), start=True, stop=True)
                m.then_inc(S["ssmb_ps"], 1)
                nc.tensor.matmul(psB[:, 1, 2:3], sout_raw, cols(V_SSM_DW_B), start=True, stop=True)\
                             .then_inc(S["ssmb_ps"], 1)

            def convolution(h):
                pe.wait_ge(S["z_ok"], h + 1)
                for i, tap in enumerate(PE_TAPS):
                    dy, dx = divmod(tap, 3)
                    pe.wait_ge(S["diag_ok"], i + 1)
                    m = nc.tensor.matmul(psA[:, h, 0:L].rearrange("p (y x) -> p y x", x=W), conv_diag[:, i, :],
                                         zpad[:, h, dy:dy + H, dx:dx + W], start=(i == 0), stop=(i == len(PE_TAPS) - 1))
                m.then_inc(S["conv_ps"], 1)

            def ssm_products(h):
                pe.wait_ge(Q["c_norm"][h], 2)
                pe.wait_ge(S["ssm_w_ok"], 1)
                pe.wait_ge(S["ssm_b_ok"], 2)
                pe.wait_ge(S["sout_b0_ok"], 1)
                for g, bank in ((1, psB), (0, psA)):
                    for q in range(2):
                        m = nc.tensor.matmul(bank[:, h, q * L:(q + 1) * L], ssm_w[:, g, q, :], norm_c[:, h, :],
                                             start=True, stop=True)
                    m.then_inc(S["ag_ps"], 1)

            def raster(h):
                bank = per_q(psA[:, h, :])
                pe.wait_ge(S["u_ok"], h + 1)
                pe.wait_ge(S["sout_w_ok"], 6)
                nc.tensor.matmul(bank, sout_w[:, 1, :], u_sb[:, h, :, W:W + L], start=True, stop=False)
                nc.tensor.matmul(bank[:, :, 1:L], sout_w[:, 0, :], u_sb[:, h, :, W:W + L - 1], start=False, stop=False)
                nc.tensor.matmul(bank[:, :, 0:L - 1], sout_w[:, 2, :], u_sb[:, h, :, W + 1:W + L], start=False,
                                 stop=True).then_inc(S["dirs_ps"], 1)

            def column(h):
                bank = per_q(psB[:, h, :])
                nc.tensor.matmul(bank, sout_w[:, 1, :], u_sb[:, h, :, W:W + L], start=True, stop=False)
                pe.wait_ge(S["u_left"], h + 1)
                nc.tensor.matmul(bank, sout_w[:, 0, :], u_sb[:, h, :, 0:L], start=False, stop=False)
                pe.wait_ge(S["u_right"], h + 1)
                nc.tensor.matmul(bank, sout_w[:, 2, :], u_sb[:, h, :, 2 * W:2 * W + L], start=False,
                                 stop=True).then_inc(S["dirs_ps"], 1)

            def outproj(h):
                pe.wait_ge(S["late_in"], 16)
                pe.wait_ge(S["outq_ok"], 1)
                nc.tensor.matmul(psM[:, h, 0:L], outproj_w, y_sb[:, h, :], start=True, stop=False)
                for k in range(2):
                    pe.wait_ge(S["dclean_ok"], 2 * h + k + 1)
                    for q in range(2):
                        m = nc.tensor.matmul(psM[q * C:(q + 1) * C, h, 0:L], outproj_q[:, :],
                                             dirs[:, h, k, q * L:(q + 1) * L], start=False, stop=(k == 1))
                m.then_inc(S["out_ps"], 1)

            def kv_bias_products(h):
                pe.wait_ge(S["kvb_ok"], 1)
                pe.wait_ge(S["row_ok"], 1)
                pe.wait_ge(S["dsign_ok"], 2 * h + 1)
                nc.tensor.matmul(psA[:, h, :].rearrange("p (t n) -> p t n", t=T), first_row[:, :],
                                 kv_b[:, :].unsqueeze(1).to_broadcast([P, T, 2 * P]), start=True, stop=False)

            def keys_values(h):
                pe.wait_ge(Q["c_norm"][h], 3)
                pe.wait_ge(S["kvw_ok"], 1)
                for t in range(T):
                    m = nc.tensor.matmul(psA[:, h, t * 2 * P:(t + 1) * 2 * P], xa_c[:, h, t * P:(t + 1) * P], kv_w[:, :],
                                         start=False, stop=(t == T - 1))
                m.then_inc(S["kv_ps"], 1)

            def head_products(h):
                pe.wait_ge(S["kvn_ok"], h + 1)
                pe.wait_ge(S["ones_ok"], 2)
                for t in range(T):
                    nc.tensor.matmul(psA[:, h, 0:P + 1], kv_n[:, h, t, 0:P], kv_n[:, h, t, P:2 * P + 1],
                                     start=(t == 0), stop=(t == T - 1))
                for t in range(T):
                    m = nc.tensor.matmul(psT[:, h, 0:P], ones[:, :], kv_n[:, h, t, P:2 * P],
                                         start=(t == 0), stop=(t == T - 1))
                m.then_inc(S["heads_ps"], 1)

            def query_product(h):
                pe.wait_ge(S["heads_ok"], h + 1)
                nc.tensor.matmul(psA[:, h, P:2 * P], heads[:, h, :], q_w, start=True, stop=True)
                nc.tensor.matmul(psA[:, h, 2 * P:2 * P + 1], heads[:, h, :], cols(V_Q_B), start=True,
                                 stop=True).then_inc(S["yq_ps"], 1)

            def proj_product(h):
                pe.wait_ge(S["yq_ok"], 2 * h + 2)
                nc.tensor.matmul(psT[:, h, 0:P], yq[:, h, 0:P], proj_w, start=True, stop=True).then_inc(S["zT_ps"], 1)
                nc.tensor.matmul(psT[:, h, P:P + 1], proj_w, yq[:, h, P:P + 1], start=True,
                                 stop=True).then_inc(S["zT_ps"], 1)

            def attention(h):
                pe.wait_ge(S["zT_ok"], h + 1)
                nc.tensor.matmul(psM[:, h, 0:L], zT[:, h, :], xa_c[:, h, :], start=True, stop=True).then_inc(S["p_ps"], 1)

            def token_copies(h):
                for t in range(T):
                    pe.wait_ge(Q["t_norm"][h], T * 3 + (t + 1 if h == 0 else T))
                    for q in range(2):
                        src = norm_d[:, h, q * T + t, :, :].rearrange("p a c -> p (a c)")
                        m = nc.tensor.transpose(copies_bank(h)[:, (q * T + t) * P:(q * T + t + 1) * P], src, ident[:, :])
                m.then_inc(S["xdup_ps"], 1)

            def logits(h):
                pe.wait_ge(S["xh_ok"], h + 1)
                pe.wait_ge(S["xl_ok"], h + 1)
                pe.wait_ge(S["gatel_ok"], 1)
                for g in range(4):
                    for x_part in (xh, xl):
                        m = nc.tensor.matmul(psT[:, h, E * g:E * (g + 1)], x_part[:, h, g * P:(g + 1) * P], gate_hl[:, :],
                                             start=(x_part is xh), stop=(x_part is xl))
                m.then_inc(S["lg_ps"], 1)

            def hidden(n):
                h, e = divmod(n, E)
                if h == 0 and e % 2 == 0:
                    pe.wait_ge(S["w1l_ok"], e // 2 + 1)
                if n <= 1:
                    pe.wait_ge(S["yq_ok"], 2 * n + 2)
                    pe.wait_ge(S["dsign_ok"], 2 * n + 2)
                pe.wait_ge(S["xl_ok"], h + 1)
                for k in range(CK):
                    c = CK * n + k
                    if c >= 4:
                        pe.wait_ge(S["h_ok"], c - 3)
                    w = w1_hl[:, e, k * P:(k + 1) * P]
                    nc.tensor.matmul(hidden_bank(c), w, xh[:, h, :], start=True, stop=False)
                    nc.tensor.matmul(hidden_bank(c), w, xl[:, h, :], start=False, stop=True).then_inc(S["h_ps"], 1)

            def output(n):
                bank, c0 = output_slot(n)
                if n == 0:
                    pe.wait_ge(S["w2_in"], 16)
                if n in (0, 2):
                    pe.wait_ge(S["gelu_ok"], n // 2 + 1)
                if n >= 4 and (n % 2 == 0 or n == 15):
                    pe.wait_ge(S["prod_ok"], 14 if n == 15 else n - 2)
                for k in range(CK):
                    s = CK * n + k
                    pe.wait_ge(S["h_ok"], s + 1)
                    for q in range(2):
                        m = nc.tensor.matmul(psM[q * C:(q + 1) * C, bank, c0:c0 + L], w2_sb[:, s % (E * CK), :],
                                             hs[:, s % RING, q * L:(q + 1) * L], start=(k == 0), stop=(k == CK - 1))
                m.then_inc(S["e_ps"], 1)

            def gate_rows(h):
                pe.wait_ge(S["w3_ok"], h + 1)
                pe.wait_ge(S["bf_ok"], 1)
                pT = psT[:, h, 256:512].bitcast(BF16)
                for t in range(T):
                    m = nc.tensor.transpose(pT[0:6 * E, t * P:(t + 1) * P], w3[:, h, t].rearrange("p i q e -> p (i q e)"),
                                            ident_bf[:, :])
                m.then_inc(S["w3T_ps"], 1)

            def spread_gates(i):
                h = i // (E // 2)
                pe.wait_ge(S["w3T_ok"], h + 1)
                pe.wait_ge(S["pickq_ok"], 2)
                if i:
                    pe.wait_ge(S["wbc_ok"], i)
                for g in range(2):
                    pick = pick_q[:, 2 * i % E + g, :, :].rearrange("r q c -> r (q c)")
                    m = nc.tensor.matmul(psT[:, h, g * L:(g + 1) * L], pick, w3T[:, h, :], start=True, stop=True)
                m.then_inc(S["wbc_ps"], 1)

            pe.wait_ge(S["ident_ok"], 1)

            keep_clock(5)
            in_bias_product()
            keep_clock(4)
            to_channels(0, 0)
            ssm_bias_products()
            in_product(0)
            keep_clock(2)
            to_channels(0, 1)
            convolution(0)
            keep_clock(1)
            in_product(1)
            to_tokens(0, y_sb, "y_ok")
            keep_clock(1)
            convolution(1)
            to_channels(1, 0)
            keep_clock(2)
            ssm_products(0)
            to_tokens(1, y_sb, "y_ok")
            raster(0)
            to_channels(1, 1)
            column(0)
            ssm_products(1)
            outproj(0)
            kv_bias_products(0)
            raster(1)
            to_tokens(0, x1, "x1_ok")
            column(1)
            keep_clock(3)
            to_channels(2, 0)
            keep_clock(4)
            keys_values(0)
            keep_clock(1)
            outproj(1)
            kv_bias_products(1)
            head_products(0)
            keep_clock(3)
            to_tokens(1, x1, "x1_ok")
            keep_clock(4)
            query_product(0)
            proj_product(0)
            keep_clock(3)
            to_channels(2, 1)
            keep_clock(1)
            attention(0)
            keys_values(1)
            to_tokens(0, t2, "t2_ok")
            keep_clock(9)
            token_copies(0)
            keep_clock(2)
            head_products(1)
            logits(0)
            query_product(1)
            hidden(0)
            proj_product(1)
            hidden(1)
            attention(1)
            hidden(2)
            output(0)
            to_tokens(1, t2, "t2_ok")
            hidden(3)
            gate_rows(0)
            hidden(4)
            spread_gates(0)
            output(1)
            hidden(5)
            output(2)
            token_copies(1)
            hidden(6)
            spread_gates(1)
            output(3)
            hidden(7)
            logits(1)
            output(4)
            spread_gates(2)
            hidden(8)
            output(5)
            hidden(9)
            output(6)
            spread_gates(3)
            output(7)
            hidden(10)
            output(8)
            gate_rows(1)
            hidden(11)
            output(9)
            spread_gates(4)
            hidden(12)
            output(10)
            hidden(13)
            output(11)
            spread_gates(5)
            output(12)
            output(13)
            hidden(14)
            spread_gates(6)
            hidden(15)
            output(14)
            spread_gates(7)
            output(15)

        @block.vector
        def _(dve):
            def stats(n, h):
                if n:
                    dve.wait_ge(Q["tT_ps"][h], n)
                    dve.wait_ge(Q["t_norm"][h], T * n)
                else:
                    dve.wait_ge(Q["xt_in"][h], 16)
                for g in range(4):
                    src = psT[:, h, g * C:(g + 1) * C] if n else x_tok[:, h, g // 2, g % 2 * C:(g % 2 + 1) * C]
                    m = nc.vector.bn_stats(st[:, h, g, :], src)
                m.then_inc(Q["t_stats"][h], 1)
                dve.wait_ge(Q["t_stats"][h], n + 1)
                for g in range(4):
                    m = nc.vector.bn_aggr(mv[:, h, g, :], st[:, h, g, :])
                m.then_inc(Q["t_mv"][h], 1)

            def normalise(n, h):
                dve.wait_ge(Q["t_rstd"][h], n + 1)
                if n:
                    dve.wait_ge(Q["cT_ps"][h], n)
                for g in range(4):
                    t, q = divmod(g, 2)
                    src = psT[:, h, g * C:(g + 1) * C] if n else x_tok[:, h, t, q * C:(q + 1) * C]
                    if n == 3:
                        dst = norm_d[:, h, q * T + t, :, :]
                        src = src.unsqueeze(1).to_broadcast([P, 2, C])
                    else:
                        dst = norm_t[:, h, t, q * C:(q + 1) * C]
                    m = nc.vector.tensor_scalar(dst, src, mv[:, h, g, 0:1], rstd[:, h, g:g + 1], ALU.subtract, ALU.mult)
                    if q == 1:
                        m.then_inc(Q["t_norm"][h], 1)

            dve_taps = [tap for tap in range(9) if tap not in PE_TAPS]

            def conv_tap(i, h):
                dy, dx = divmod(dve_taps[i], 3)
                z = zpad[:, h, dy:dy + H, dx:dx + W]
                y = y_sb[:, h, :].rearrange("p (y x) -> p y x", x=W)
                w = cols(V_CONV + dve_taps[i])
                if i == 0:
                    dve.wait_ge(S["early_in"], 16)
                    dve.wait_ge(S["z_ok"], h + 1)
                    nc.vector.tensor_scalar(y, z, w, cols(V_CONV_B), ALU.mult, ALU.add).then_inc(Q["taps"][h], 1)
                else:
                    dve.wait_ge(Q["taps"][h], i)
                    nc.vector.scalar_tensor_tensor(out=y, in0=z, scalar=w, in1=y, op0=ALU.mult, op1=ALU.add)\
                        .then_inc(Q["taps"][h], 1)

            def conv_sum(h):
                dve.wait_ge(Q["taps"][h], len(dve_taps))
                dve.wait_ge(S["conv_ps"], h + 1)
                nc.vector.tensor_tensor(y_sb[:, h, :], psA[:, h, 0:L], y_sb[:, h, :], ALU.add).then_inc(S["y_ok"], 1)

            by_head = kvT.rearrange("p (h d) -> p h d", d=HC)
            by_head_b = kv_bias.rearrange("p (h d) -> p h d", d=HC)

            def weight_sums():
                dve.wait_ge(S["late_in"], 16)
                nc.vector.tensor_scalar(outproj_q[:, :], outproj_dup, 0.25 * CLAMP, None, ALU.mult)\
                             .then_inc(S["outq_ok"], 1)
                nc.vector.tensor_reduce(kv_gsum[:, :], by_head, AX.X, ALU.add).then_inc(S["kvg_ok"], 1)
                nc.vector.tensor_reduce(kv_bsum[:, :], by_head_b, AX.X, ALU.add).then_inc(S["kvbg_ok"], 1)

            def gated_u(h):
                dve.wait_ge(S["ag_ps"], 2 * h + 2)
                dve.wait_ge(S["ssm_b_ok"], 2)
                dve.wait_ge(S["sig_ok"], h + 1)
                nc.vector.scalar_tensor_tensor(out=u_sb[:, h, :, W:W + L], in0=per_q(psA[:, h, :]), scalar=ssm_b[:, 0:1],
                                               in1=gate_s[:, h, :, :], op0=ALU.add, op1=ALU.mult).then_inc(S["u_ok"], 1)

            def kv_weights():
                dve.wait_ge(S["kvg_ok"], 1)
                nc.vector.scalar_tensor_tensor(out=kv_w[:, :].rearrange("p (h d) -> p h d", d=HC),
                                               in0=kv_gsum[:, :].unsqueeze(2).to_broadcast([P, 4 * HEADS, HC]),
                                               scalar=-1.0 / HC, in1=by_head, op0=ALU.mult, op1=ALU.add)\
                                                            .then_inc(S["kvw_ok"], 1)
                dve.wait_ge(S["kvbg_ok"], 1)
                nc.vector.scalar_tensor_tensor(out=kv_b[:, :].rearrange("p (h d) -> p h d", d=HC),
                                               in0=kv_bsum[:, :].unsqueeze(2).to_broadcast([P, 4 * HEADS, HC]),
                                               scalar=-1.0 / HC, in1=by_head_b, op0=ALU.mult, op1=ALU.add)\
                                                            .then_inc(S["kvb_ok"], 1)

            def ln_weights():
                dve.wait_ge(S["mask_ok"], 1)
                dve.wait_ge(S["late_in"], 16)
                dve.wait_ge(S["early_in"], 16)
                nc.vector.tensor_tensor(ln_v[:, :], head_mask[:, :], vln_w, ALU.mult).then_inc(S["lnv_ok"], 1)
                nc.vector.tensor_tensor(ln_vb[:, :], head_mask[:, :], vln_b, ALU.mult).then_inc(S["lnkv_ok"], 1)
                nc.vector.tensor_scalar(kln_bL[:, :], cols(V_KLN_B), float(L), None, ALU.mult).then_inc(S["lnkv_ok"], 1)
                dve.wait_ge(S["lnv_ok"], 1)
                nc.vector.tensor_scalar(ln_kv[:, :], ln_v[:, :], cols(V_KLN_W), None, ALU.mult).then_inc(S["lnkv_ok"], 1)
                nc.vector.tensor_scalar(ln_kbv[:, :], ln_v[:, :], cols(V_KLN_B), None, ALU.mult).then_inc(S["lnkv_ok"], 1)

            def gate_low():
                dve.wait_ge(S["gateh_ok"], 1)
                nc.vector.tensor_tensor(gate_hl[C:P, :], gate_w[C:P, :], gate_hl[C:P, :].bitcast(F32),
                                        ALU.subtract).then_inc(S["gatel_ok"], 1)

            def clean_dirs(h, k):
                dve.wait_ge(S["dirs_ok"], 2 * h + k + 1)
                dve.wait_ge(S["dsign_ok"], 2 * h + k + 1)
                nc.vector.scalar_tensor_tensor(out=dirs_sign[:, h, k, :], in0=dirs[:, h, k, :], scalar=0.0,
                                               in1=dirs_sign[:, h, k, :], op0=ALU.min, op1=ALU.max)\
                    .then_inc(S["dlim_ok"], 1)
                dve.wait_ge(S["dlim_ok"], 2 * h + k + 1)
                dve.wait_ge(S["dbad_ok"], 2 * h + k + 1)
                nc.vector.copy_predicated(dirs[:, h, k, :], dirs_bad[:, h, k, :].bitcast(I32),
                                          dirs_sign[:, h, k, :]).then_inc(S["dclean_ok"], 1)

            def residual(h):
                dve.wait_ge(S["osign_ok"], h + 1)
                dve.wait_ge(S["o_ok"], h + 1)
                nc.vector.scalar_tensor_tensor(out=o_sign[:, h, :], in0=o_sb[:, h, :], scalar=0.0, in1=o_sign[:, h, :],
                                               op0=ALU.min, op1=ALU.max).then_inc(S["olim_ok"], 1)
                dve.wait_ge(S["olim_ok"], h + 1)
                dve.wait_ge(S["obad_ok"], h + 1)
                nc.vector.copy_predicated(o_sb[:, h, :], o_bad[:, h, :].bitcast(I32), o_sign[:, h, :])\
                    .then_inc(S["oclean_ok"], 1)
                dve.wait_ge(S["oclean_ok"], h + 1)
                dve.wait_ge(S["xp_in"], 16)
                nc.vector.scalar_tensor_tensor(out=x1[:, h, :], in0=o_sb[:, h, :], scalar=CLAMP, in1=x_sb[:, h, :],
                                               op0=ALU.mult, op1=ALU.add).then_inc(S["x1_ok"], 1)

            def square_sums(h):
                dve.wait_ge(S["kvsq_ok"], h + 1)
                nc.vector.tensor_reduce(ss[:, h, :], kv_sq[:, h, :, :].rearrange("p t (h d) -> p (t h) d", d=HC),
                                        AX.X, ALU.add).then_inc(S["ss_ok"], 1)

            def kv_scaled(h):
                dve.wait_ge(S["rinv_ok"], h + 1)
                nc.vector.tensor_tensor(kv_n[:, h, :, 0:2 * P].rearrange("p t (h d) -> p t h d", d=HC),
                                        psA[:, h, :].rearrange("p (t h d) -> p t h d", t=T, d=HC),
                                        rinv[:, h, :].rearrange("p (t h) -> p t h", t=T).unsqueeze(3)
                                        .to_broadcast([P, T, 4 * HEADS, HC]), ALU.mult).then_inc(S["kvn_ok"], 1)

            def head_matrix(h):
                dve.wait_ge(S["heads_ps"], h + 1)
                dve.wait_ge(S["lnkv_ok"], 4)
                nc.vector.tensor_scalar(k_sum[:, h, :], psA[:, h, P:P + 1], cols(V_KLN_W), kln_bL[:, :], ALU.mult, ALU.add)\
                    .then_inc(S["ksum_ok"], 1)
                nc.vector.tensor_tensor(heads1[:, h, :], psA[:, h, 0:P], ln_kv[:, :], ALU.mult).then_inc(S["h1_ok"], 1)
                nc.vector.tensor_tensor(heads3[:, h, :], psT[:, h, 0:P], ln_kbv[:, :], ALU.mult).then_inc(S["h3_ok"], 1)
                dve.wait_ge(S["ksum_ok"], h + 1)
                dve.wait_ge(S["h1_ok"], h + 1)
                nc.vector.scalar_tensor_tensor(out=heads2[:, h, :], in0=ln_vb[:, :], scalar=k_sum[:, h, :],
                                               in1=heads1[:, h, :], op0=ALU.mult, op1=ALU.add).then_inc(S["h2_ok"], 1)
                dve.wait_ge(S["h2_ok"], h + 1)
                dve.wait_ge(S["h3_ok"], h + 1)
                nc.vector.tensor_tensor(heads[:, h, :], heads2[:, h, :], heads3[:, h, :], ALU.add)\
                             .then_inc(S["heads_ok"], 1)

            def query_and_bias(h):
                dve.wait_ge(S["yq_ps"], h + 1)
                nc.vector.tensor_tensor(yq[:, h, 0:P], psA[:, h, P:2 * P], ident[:, :], ALU.add).then_inc(S["yq_ok"], 1)
                nc.vector.tensor_copy(yq[:, h, P:P + 1], psA[:, h, 2 * P:2 * P + 1]).then_inc(S["yq_ok"], 1)

            def tokens_after_attention(h):
                dve.wait_ge(S["gelu_ok"], h + 1)
                dve.wait_ge(S["x1xa_ok"], h + 1)
                nc.vector.tensor_tensor(t2[:, h, :], gelu_p[:, h, :], x1_xa[:, h, :], ALU.add).then_inc(S["t2_ok"], 1)

            def token_low(h):
                dve.wait_ge(S["xh_ok"], h + 1)
                nc.vector.tensor_tensor(xl[:, h, :], copies_bank(h), xh[:, h, :].bitcast(F32), ALU.subtract)\
                    .then_inc(S["xl_ok"], 1)

            steps = [0, 0]

            def chain(h, ins):
                ins.then_inc(Q["gate_chain"][h], 1)
                steps[h] += 1
                dve.wait_ge(Q["gate_chain"][h], steps[h])

            def over_e(ap):
                return ap.unsqueeze(2).to_broadcast([P, 4, E])

            rev = rev8[:, :].unsqueeze(1).to_broadcast([P, 4, E])

            def largest(h):
                dve.wait_ge(S["lg_ps"], h + 1)
                dve.wait_ge(S["rev_ok"], 1)
                chain(h, nc.vector.tensor_tensor(lg[:, h], psT[:, h, 0:4 * E].rearrange("p (g e) -> p g e", e=E),
                                                 gate_b.unsqueeze(1).to_broadcast([P, 4, E]), ALU.add))
                chain(h, nc.vector.tensor_reduce(m1[:, h], lg[:, h], AX.X, ALU.max))
                chain(h, nc.vector.tensor_tensor(eq1[:, h], lg[:, h], over_e(m1[:, h]), ALU.is_equal))
                chain(h, nc.vector.tensor_tensor(pr1[:, h], eq1[:, h], rev, ALU.mult))
                chain(h, nc.vector.tensor_reduce(i1[:, h], pr1[:, h], AX.X, ALU.max))
                chain(h, nc.vector.tensor_tensor(f1[:, h], rev, over_e(i1[:, h]), ALU.is_equal))

            def second(h):
                chain(h, nc.vector.scalar_tensor_tensor(out=lg2[:, h], in0=f1[:, h], scalar=-3.0e38, in1=lg[:, h],
                                                        op0=ALU.mult, op1=ALU.add))
                chain(h, nc.vector.tensor_reduce(m2[:, h], lg2[:, h], AX.X, ALU.max))
                nc.vector.tensor_tensor(m12[:, h], m1[:, h], m2[:, h], ALU.add).then_inc(S["m12_ok"], 1)
                chain(h, nc.vector.tensor_tensor(eq2[:, h], lg2[:, h], over_e(m2[:, h]), ALU.is_equal))
                dve.wait_ge(S["m12_ok"], h + 1)
                nc.vector.scalar_tensor_tensor(out=ld[:, h], in0=lg[:, h], scalar=2.0, in1=over_e(m12[:, h]),
                                               op0=ALU.mult, op1=ALU.subtract).then_inc(S["ld_ok"], 1)
                chain(h, nc.vector.tensor_tensor(pr2[:, h], eq2[:, h], rev, ALU.mult))
                chain(h, nc.vector.tensor_reduce(i2[:, h], pr2[:, h], AX.X, ALU.max))
                chain(h, nc.vector.tensor_tensor(f2[:, h], rev, over_e(i2[:, h]), ALU.is_equal))
                chain(h, nc.vector.tensor_tensor(sel[:, h], f1[:, h], f2[:, h], ALU.add))

            def gate_parts(h):
                dve.wait_ge(S["th_ok"], h + 1)
                chain(h, nc.vector.scalar_tensor_tensor(out=wg2[:, h], in0=th[:, h], scalar=1.0, in1=sel[:, h],
                                                        op0=ALU.add, op1=ALU.mult))
                chain(h, nc.vector.tensor_scalar(wg[:, h], wg2[:, h], 0.5, None, ALU.mult))

                def part(i):
                    return w3[:, h, :, i, :, :].rearrange("p t q e -> p q t e")

                def qt(ap):
                    return ap.rearrange("p (q t) e -> p q t e", q=2)
                chain(h, nc.vector.tensor_copy(part(0), qt(wg[:, h])))
                chain(h, nc.vector.tensor_tensor(qt(wr1[:, h]), qt(wg[:, h]), part(0), ALU.subtract))
                chain(h, nc.vector.tensor_copy(part(1), qt(wr1[:, h])))
                chain(h, nc.vector.tensor_tensor(qt(wr2[:, h]), qt(wr1[:, h]), part(1), ALU.subtract))
                nc.vector.tensor_copy(part(2), qt(wr2[:, h])).then_inc(S["w3_ok"], 1)

            def rows_out(h):
                dve.wait_ge(S["w3T_ps"], h + 1)
                nc.vector.tensor_copy(w3T[:, h, :], psT[0:6 * E, h, 256:384].bitcast(BF16)).then_inc(S["w3T_ok"], 1)

            def spread_out(i):
                h = i // (E // 2)
                dve.wait_ge(S["wbc_ps"], i + 1)
                nc.vector.tensor_copy(wbc[:, h, 2 * i % E:2 * i % E + 2, :], per_q(psT[:, h, :])).then_inc(S["wbc_ok"], 1)

            def gated(n):
                h, e = divmod(n, E)
                bank, c0 = output_slot(n)
                dve.wait_ge(S["e_ps"], n + 1 if n >= 14 else n // 2 * 2 + 2)
                dve.wait_ge(S["wbc_ok"], n // 2 + 1)
                if n >= 4:
                    dve.wait_ge(S["acc_ok"], 2 * (n // 2 - 1))
                nc.vector.scalar_tensor_tensor(out=prod[:, n % 4, :], in0=psM[:, bank, c0:c0 + L], scalar=cols(V_B2 + e),
                                               in1=wbc[:, h, e, :], op0=ALU.add, op1=ALU.mult).then_inc(S["prod_ok"], 1)

            def gated_pair(i):
                spread_out(i)
                gated(2 * i)
                gated(2 * i + 1)

            def first_pair_sum():
                dve.wait_ge(S["acc_ok"], E)
                nc.vector.tensor_tensor(fin[:, 0, :], acc[:, 0, 0, :], acc[:, 0, 1, :], ALU.add).then_inc(S["fin_ok"], 1)

            def last_experts():
                spread_out(7)
                gated(14)
                dve.wait_ge(S["acc_ok"], 2 * E - 2)
                nc.vector.tensor_tensor(part_sum[:, 0, :], acc[:, 1, 0, :], acc[:, 1, 1, :], ALU.add)\
                             .then_inc(S["psum_ok"], 1)
                dve.wait_ge(S["psum_ok"], 1)
                dve.wait_ge(S["prod_ok"], 15)
                nc.vector.tensor_tensor(part_sum[:, 1, :], part_sum[:, 0, :], prod[:, 2, :], ALU.add)\
                             .then_inc(S["psum_ok"], 1)
                gated(15)
                dve.wait_ge(S["psum_ok"], 2)
                dve.wait_ge(S["prod_ok"], 16)
                nc.vector.tensor_tensor(fin[:, 1, :], part_sum[:, 1, :], prod[:, 3, :], ALU.add).then_inc(S["fin_ok"], 1)

            stats(0, 0)
            normalise(0, 0)
            stats(0, 1)
            normalise(0, 1)
            weight_sums()
            conv_tap(0, 0)
            conv_tap(1, 0)
            conv_tap(2, 0)
            conv_tap(3, 0)
            conv_sum(0)
            stats(1, 0)
            conv_tap(0, 1)
            normalise(1, 0)
            ln_weights()
            conv_tap(1, 1)
            conv_tap(2, 1)
            gate_low()
            conv_tap(3, 1)
            conv_sum(1)
            gated_u(0)
            stats(1, 1)
            normalise(1, 1)
            clean_dirs(0, 0)
            kv_weights()
            clean_dirs(0, 1)
            gated_u(1)
            residual(0)
            stats(2, 0)
            normalise(2, 0)
            clean_dirs(1, 0)
            clean_dirs(1, 1)
            square_sums(0)
            kv_scaled(0)
            residual(1)
            head_matrix(0)
            stats(2, 1)
            query_and_bias(0)
            normalise(2, 1)
            tokens_after_attention(0)
            stats(3, 0)
            square_sums(1)
            normalise(3, 0)
            kv_scaled(1)
            token_low(0)
            head_matrix(1)
            query_and_bias(1)
            largest(0)
            second(0)
            tokens_after_attention(1)
            gate_parts(0)
            stats(3, 1)
            rows_out(0)
            normalise(3, 1)
            gated_pair(0)
            token_low(1)
            gated_pair(1)
            largest(1)
            second(1)
            gated_pair(2)
            gate_parts(1)
            gated_pair(3)
            rows_out(1)
            gated_pair(4)
            first_pair_sum()
            gated_pair(5)
            gated_pair(6)
            last_experts()


_INS = ['x', 'L0_conv_ln2d_w', 'L0_conv_ln2d_b', 'L0_conv_inproj_w', 'L0_conv_inproj_b', 'L0_conv_dw2d_w',
        'L0_conv_dw2d_b', 'L0_conv_ssm_ln_w', 'L0_conv_ssm_ln_b', 'L0_conv_ssm_in_w', 'L0_conv_ssm_in_b',
        'L0_conv_ssm_dw_w', 'L0_conv_ssm_dw_b', 'L0_conv_ssm_out_w', 'L0_conv_ssm_out_b', 'L0_conv_outproj_w',
        'L0_conv_outproj_b', 'L1_attn_W_qkv', 'L1_attn_b_qkv', 'L1_attn_kln_w', 'L1_attn_kln_b', 'L1_attn_vln_w',
        'L1_attn_vln_b', 'L1_attn_W_proj', 'L1_attn_b_proj', 'L1_ffn_Wg', 'L1_ffn_bg', 'L1_ffn_W1', 'L1_ffn_b1',
        'L1_ffn_W2', 'L1_ffn_b2']


def lay_out(inputs):
    import numpy as _np

    v = {name: _np.ascontiguousarray(inputs[name]) for name in _INS}
    shapes = {name: v[name].shape for name in _INS}
    x = v["x"]
    f = x.dtype
    b, c, hh, ww = x.shape
    p = 2 * c
    e, _, fh = v["L1_ffn_W1"].shape
    heads, _, hc = v["L1_attn_kln_w"].shape

    def diagonal(m):
        r = _np.zeros((2 * m.shape[0], 2 * m.shape[1]), f)
        r[:m.shape[0], :m.shape[1]] = m
        r[m.shape[0]:, m.shape[1]:] = m
        return r

    def column(m):
        m = m.reshape(-1, m.shape[-1])
        return _np.tile(m, (1, p // m.shape[1])).T

    def row(m):
        return _np.broadcast_to(_np.tile(m.reshape(-1), 2), (p, 2 * m.size))

    qkv_w = v["L1_attn_W_qkv"].reshape(heads, 3, hc, c).transpose(1, 0, 2, 3).reshape(3, c, c)
    qkv_b = v["L1_attn_b_qkv"].reshape(heads, 3, hc).transpose(1, 0, 2).reshape(3, c)
    vectors = [column(m) for m in (
        v["L0_conv_ln2d_w"], v["L0_conv_ln2d_b"], v["L0_conv_inproj_b"], v["L0_conv_dw2d_b"], v["L0_conv_ssm_ln_w"],
        v["L0_conv_ssm_ln_b"], v["L0_conv_ssm_in_b"].reshape(2, p), v["L0_conv_ssm_dw_b"], v["L0_conv_ssm_out_b"],
        v["L0_conv_outproj_b"], qkv_b[0], v["L1_attn_b_proj"], v["L1_attn_kln_w"].reshape(-1),
        v["L1_attn_kln_b"].reshape(-1), v["L0_conv_ssm_dw_w"].T, v["L0_conv_dw2d_w"].reshape(c, 9).T,
        v["L1_ffn_b1"].reshape(-1, p), v["L1_ffn_b2"])]
    ssm = _np.zeros((p, 5, p), f)
    for g in range(2):
        for q in range(2):
            ssm[q * c:(q + 1) * c, 2 * g + q, :] = v["L0_conv_ssm_in_w"][g * p:(g + 1) * p].T
    ssm[:, 4, :] = _np.tile(v["L0_conv_ssm_out_w"].T, (1, 2))
    outproj_t = v["L0_conv_outproj_w"].T
    return shapes, {
        "x_tok": x.reshape(2, 2, c, 2, p).transpose(4, 0, 3, 1, 2).reshape(p, 2, 2, p),
        "x_chan": x.reshape(2, p, hh * ww).transpose(1, 0, 2),
        "early": _np.concatenate([diagonal(v["L0_conv_inproj_w"].T)] + vectors, 1),
        "ssm": ssm,
        "late": _np.concatenate([
            diagonal(outproj_t), diagonal(qkv_w[1].T), diagonal(qkv_w[2].T), diagonal(qkv_w[0]),
            diagonal(v["L1_attn_W_proj"].T), _np.tile(outproj_t, (2, 1)), row(qkv_b[1]), row(qkv_b[2]),
            row(v["L1_attn_vln_w"]), row(v["L1_attn_vln_b"]), _np.tile(v["L1_ffn_Wg"], (2, 1)),
            _np.broadcast_to(v["L1_ffn_bg"], (p, e))], 1),
        "w1": _np.tile(v["L1_ffn_W1"].transpose(1, 0, 2), (2, 1, 1)),
        "w2": v["L1_ffn_W2"].reshape(e * fh // p, p, c).transpose(1, 0, 2),
    }


def kernel(**inputs):
    import numpy as _np
    import concourse.bacc as _bacc
    from concourse import mybir as _mybir
    from concourse.bass_utils import run_bass_kernel_spmd as _run

    shapes, laid = lay_out(inputs)
    nc = _bacc.Bacc("TRN2", target_bir_lowering=False, num_devices=1)
    arrays, aps = {}, {}
    for name, m in laid.items():
        arrays[f"in_{name}_dram"] = _np.ascontiguousarray(m)
        aps[name] = nc.dram_tensor(f"in_{name}_dram", m.shape, _mybir.dt.from_np(m.dtype), kind="ExternalInput").ap()
    out = nc.dram_tensor("out_0_dram", shapes["x"], _mybir.dt.float32, kind="ExternalOutput").ap()
    conv_attention_moe(nc, aps, shapes, out)
    r = _run(nc, [arrays], core_ids=[0])
    return r.results[0]["out_0_dram"]
```
